# Optimizing a Trainium2 kernel written in Bass

```python
import numpy as np
import jax
import jax.numpy as jnp

def _softmax(x, axis=-1):
    return jax.nn.softmax(x, axis=axis)

def _gelu(x):
    return jax.nn.gelu(x, approximate=True)

def _silu(x):
    return jax.nn.silu(x)

def _sigmoid(x):
    return jax.nn.sigmoid(x)

def _layernorm(x, axis=-1, eps=1e-05):
    m = jnp.mean(x, axis=axis, keepdims=True)
    v = jnp.var(x, axis=axis, keepdims=True)
    return (x - m) / jnp.sqrt(v + eps)

def _scatter_add(tgt, idx, src, axis=0):
    return tgt.at[idx].add(src)

def _segment_sum(src, seg, n):
    return jax.ops.segment_sum(src, seg, n)
kernel_name = 'mk_xattn_ffn_d2_seqx_r8_9f44b2'

def setup_inputs(seed: int=0):
    np.random.seed(seed)
    _w = jnp.asarray

    def _rec_inputs():
        import jax
        import jax.numpy as jnp
        _rk = jax.random.key(seed)
        x = 7.22e-05 + 1 * jax.random.normal(jax.random.fold_in(_rk, 1), (4, 512, 128), jnp.float32)
        _lenS = 512 - jax.random.randint(jax.random.fold_in(_rk, 7), (4,), 0, max(1, 512 // 4) + 1, jnp.int32)
        _lenS2 = 77 - jax.random.randint(jax.random.fold_in(_rk, 8), (4,), 0, max(1, 77 // 4) + 1, jnp.int32)
        _ctx_1024P = jax.random.normal(jax.random.fold_in(_rk, 11), (4, 16, 128), jnp.float32)
        _ctx_1024c = jax.random.dirichlet(jax.random.fold_in(_rk, 511), 0.3 * jnp.ones((16,), jnp.float32), (4, 77))
        _ctx_1024t = jnp.einsum('bsk,bkd->bsd', _ctx_1024c, _ctx_1024P)
        _ctx_1024t = _ctx_1024t * jax.lax.rsqrt(jnp.mean(jnp.square(_ctx_1024t)) + 1e-12) * 0.953939
        ctx_1024 = 4.13588e-05 + 0.999923 * (_ctx_1024t + 0.3 * jax.random.normal(jax.random.fold_in(_rk, 611), (4, 77, 128), jnp.float32))
        _validS = jnp.arange(512)[None, :] < _lenS[:, None]
        _validS2 = jnp.arange(77)[None, :] < _lenS2[:, None]
        _causal = jnp.tril(jnp.ones((512, 512), dtype=bool))
        mask_SxS2_ik0 = jnp.where(jnp.broadcast_to(_validS2[0:1, :], (512, 77)), 0, 1).astype(jnp.int32)
        mask_BxS2_if1 = jnp.where(jnp.ones((4, 77), dtype=bool), 1, 0).astype(jnp.int32)
        return (x, ctx_1024, mask_SxS2_ik0, mask_BxS2_if1)
    x, ctx_1024, mask_SxS2_ik0, mask_BxS2_if1 = _rec_inputs()

    def _L0_xattn_setup():
        import jax, jax.numpy as jnp
        import numpy as np
        B, S, D, H = (4, 256, 128, 16)
        DK = D // H
        key = jax.random.key(seed)
        ks = jax.random.split(key, 12)
        scale = 1.0 / np.sqrt(D)
        inp = {'q': jax.random.normal(ks[0], (B, S, D), jnp.float32), 'k': jax.random.normal(ks[1], (B, S, D), jnp.float32), 'v': jax.random.normal(ks[2], (B, S, D), jnp.float32), 'Wq': jax.random.normal(ks[3], (D, D), jnp.float32) * scale, 'bq': jax.random.normal(ks[4], (D,), jnp.float32) * scale, 'Wk': jax.random.normal(ks[5], (D, D), jnp.float32) * scale, 'bk': jax.random.normal(ks[6], (D,), jnp.float32) * scale, 'Wv': jax.random.normal(ks[7], (D, D), jnp.float32) * scale, 'bv': jax.random.normal(ks[8], (D,), jnp.float32) * scale, 'Wo': jax.random.normal(ks[9], (D, D), jnp.float32) * scale, 'bo': jax.random.normal(ks[10], (D,), jnp.float32) * scale, 'attn_mask': jnp.tril(jnp.ones((S, S), jnp.int32)), 'padding_mask': jnp.ones((B, S), jnp.int32)}
        return inp
    _L0_xattn_all = _L0_xattn_setup()
    _L0_xattn_in = {k: v for k, v in _L0_xattn_all.items() if k in ('Wq', 'bq', 'Wk', 'bk', 'Wv', 'bv', 'Wo', 'bo')}
    del _L0_xattn_all

    def _L0_ffn_setup():
        import jax, jax.numpy as jnp
        import numpy as np
        D_MODEL = 128
        D_FF = 512
        N_EXPERTS = 8
        TOP_K = 2
        B, T = (4, 256)
        key = jax.random.key(seed)
        ks = jax.random.split(key, 5)
        x = jax.random.normal(ks[0], (B, T, D_MODEL), dtype=jnp.float32)

        def lin(k, shape, fan_in):
            return jax.random.normal(k, shape, dtype=jnp.float32) / np.float32(np.sqrt(fan_in))
        return {'x': x, 'router_w': lin(ks[1], (N_EXPERTS, D_MODEL), D_MODEL), 'w_gate': lin(ks[2], (N_EXPERTS, D_MODEL, D_FF), D_MODEL), 'w_up': lin(ks[3], (N_EXPERTS, D_MODEL, D_FF), D_MODEL), 'w_down': lin(ks[4], (N_EXPERTS, D_FF, D_MODEL), D_FF)}
    _L0_ffn_all = _L0_ffn_setup()
    _L0_ffn_in = {k: v for k, v in _L0_ffn_all.items() if k in ('router_w', 'w_gate', 'w_up', 'w_down')}
    del _L0_ffn_all

    def _L1_xattn_setup():
        import jax, jax.numpy as jnp
        import numpy as np
        B, N, C = (4, 256, 128)
        key = jax.random.key(seed)
        ks = jax.random.split(key, 5)
        s = 1.0 / np.sqrt(C)
        return {'event_f': jax.random.normal(ks[0], (B, N, C), dtype=jnp.float32), 'img_f': jax.random.normal(ks[1], (B, N, C), dtype=jnp.float32), 'Wq': jax.random.normal(ks[2], (C, C), dtype=jnp.float32) * s, 'bq': jnp.zeros((C,), dtype=jnp.float32), 'Wk': jax.random.normal(ks[3], (C, C), dtype=jnp.float32) * s, 'bk': jnp.zeros((C,), dtype=jnp.float32), 'Wv': jax.random.normal(ks[4], (C, C), dtype=jnp.float32) * s, 'bv': jnp.zeros((C,), dtype=jnp.float32)}
    _L1_xattn_all = _L1_xattn_setup()
    _L1_xattn_in = {k: v for k, v in _L1_xattn_all.items() if k in ('Wq', 'bq', 'Wk', 'bk', 'Wv', 'bv')}
    del _L1_xattn_all

    def _L1_ffn_setup():
        import jax, jax.numpy as jnp
        import numpy as np
        B, S, IN, OUT, E, R = (8, 512, 128, 128, 8, 8)
        LORA_ALPHA = 16
        SCALING = LORA_ALPHA / R
        key = jax.random.key(seed)
        k = jax.random.split(key, 6)
        x = jax.random.normal(k[0], (B, S, IN), dtype=jnp.float32)
        base_w = jax.random.normal(k[1], (OUT, IN), dtype=jnp.float32) * 0.02
        base_b = jnp.zeros((OUT,), dtype=jnp.float32)
        lora_A = jax.random.normal(k[2], (IN, R), dtype=jnp.float32) * 0.02
        lora_B = jax.random.normal(k[3], (E, R, OUT), dtype=jnp.float32) * 0.02
        router_w = jax.random.normal(k[4], (E, IN), dtype=jnp.float32) * 0.02
        router_b = jnp.zeros((E,), dtype=jnp.float32)
        return {'x': x, 'base_w': base_w, 'base_b': base_b, 'lora_A': lora_A, 'lora_B': lora_B, 'router_w': router_w, 'router_b': router_b}
    _L1_ffn_all = _L1_ffn_setup()
    _L1_ffn_in = {k: v for k, v in _L1_ffn_all.items() if k in ('base_w', 'base_b', 'lora_A', 'lora_B', 'router_w', 'router_b')}
    del _L1_ffn_all
    return {'x': x, 'ctx_1024': ctx_1024, 'mask_SxS2_ik0': mask_SxS2_ik0, 'mask_BxS2_if1': mask_BxS2_if1, 'L0_xattn_Wq': _L0_xattn_in['Wq'], 'L0_xattn_bq': _L0_xattn_in['bq'], 'L0_xattn_Wk': _L0_xattn_in['Wk'], 'L0_xattn_bk': _L0_xattn_in['bk'], 'L0_xattn_Wv': _L0_xattn_in['Wv'], 'L0_xattn_bv': _L0_xattn_in['bv'], 'L0_xattn_Wo': _L0_xattn_in['Wo'], 'L0_xattn_bo': _L0_xattn_in['bo'], 'L0_ffn_router_w': _L0_ffn_in['router_w'], 'L0_ffn_w_gate': _L0_ffn_in['w_gate'], 'L0_ffn_w_up': _L0_ffn_in['w_up'], 'L0_ffn_w_down': _L0_ffn_in['w_down'], 'L1_xattn_Wq': _L1_xattn_in['Wq'], 'L1_xattn_bq': _L1_xattn_in['bq'], 'L1_xattn_Wk': _L1_xattn_in['Wk'], 'L1_xattn_bk': _L1_xattn_in['bk'], 'L1_xattn_Wv': _L1_xattn_in['Wv'], 'L1_xattn_bv': _L1_xattn_in['bv'], 'L1_ffn_base_w': _L1_ffn_in['base_w'], 'L1_ffn_base_b': _L1_ffn_in['base_b'], 'L1_ffn_lora_A': _L1_ffn_in['lora_A'], 'L1_ffn_lora_B': _L1_ffn_in['lora_B'], 'L1_ffn_router_w': _L1_ffn_in['router_w'], 'L1_ffn_router_b': _L1_ffn_in['router_b']}

def reference(x, ctx_1024, mask_SxS2_ik0, mask_BxS2_if1, L0_xattn_Wq, L0_xattn_bq, L0_xattn_Wk, L0_xattn_bk, L0_xattn_Wv, L0_xattn_bv, L0_xattn_Wo, L0_xattn_bo, L0_ffn_router_w, L0_ffn_w_gate, L0_ffn_w_up, L0_ffn_w_down, L1_xattn_Wq, L1_xattn_bq, L1_xattn_Wk, L1_xattn_bk, L1_xattn_Wv, L1_xattn_bv, L1_ffn_base_w, L1_ffn_base_b, L1_ffn_lora_A, L1_ffn_lora_B, L1_ffn_router_w, L1_ffn_router_b):
    import jax
    import jax.numpy as jnp

    def _L0_xattn_ref(q, k, v, Wq, bq, Wk, bk, Wv, bv, Wo, bo, attn_mask, padding_mask):
        import jax, jax.numpy as jnp
        import numpy as np
        B, S, D, H = (4, 256, 128, 16)
        DK = D // H
        bs = q.shape[0]

        def split_heads(x):
            return x.reshape(bs, -1, H, DK).transpose(0, 2, 1, 3)
        qh = split_heads(q @ Wq.T + bq)
        kh = split_heads(k @ Wk.T + bk)
        vh = split_heads(v @ Wv.T + bv)
        scores = jnp.einsum('bhqd,bhkd->bhqk', qh, kh) / np.sqrt(DK).astype(np.float32)
        keep = (padding_mask[:, None, None, :] != 0) & (attn_mask[None, None, :, :] != 0)
        scores = jnp.where(keep, scores, -jnp.inf)
        probs = jax.nn.softmax(scores, axis=-1)
        ctx = jnp.einsum('bhqk,bhkd->bhqd', probs, vh)
        concat = ctx.transpose(0, 2, 1, 3).reshape(bs, -1, D)
        return concat @ Wo.T + bo

    def _L0_ffn_ref(x, router_w, w_gate, w_up, w_down):
        import jax, jax.numpy as jnp
        import numpy as np
        D_MODEL = 128
        D_FF = 512
        N_EXPERTS = 8
        TOP_K = 2
        B, T = (4, 256)
        Bx, Tx, D = x.shape
        xf = x.reshape(-1, D)
        logits = xf @ router_w.T
        scores = jax.nn.softmax(logits, axis=-1)
        topk_scores, topk_ids = jax.lax.top_k(scores, TOP_K)
        topk_scores = topk_scores / topk_scores.sum(-1, keepdims=True)
        cw = (jax.nn.one_hot(topk_ids, N_EXPERTS, dtype=xf.dtype) * topk_scores[..., None]).sum(1)

        def body(acc, inputs):
            wg, wu, wd, w = inputs
            h = jax.nn.silu(xf @ wg) * (xf @ wu)
            acc = acc + w[:, None] * (h @ wd)
            return (acc, None)
        out, _ = jax.lax.scan(body, jnp.zeros_like(xf), (w_gate, w_up, w_down, cw.T))
        return out.reshape(Bx, Tx, D)

    def _L1_xattn_ref(event_f, img_f, Wq, bq, Wk, bk, Wv, bv):
        import jax, jax.numpy as jnp
        import numpy as np
        B, N, C = (4, 256, 128)
        q = jnp.einsum('bnc,cd->bnd', event_f, Wq) + bq
        k = jnp.einsum('bnc,cd->bnd', img_f, Wk) + bk
        v = jnp.einsum('bnc,cd->bnd', img_f, Wv) + bv
        scale = 1.0 / jnp.sqrt(jnp.asarray(q.shape[-1], dtype=q.dtype))
        scores = jnp.einsum('bqc,bkc->bqk', q, k) * scale
        p_attn = jax.nn.softmax(scores, axis=-1)
        return jnp.einsum('bqk,bkc->bqc', p_attn, v)

    def _L1_ffn_ref(x, base_w, base_b, lora_A, lora_B, router_w, router_b):
        import jax, jax.numpy as jnp
        import numpy as np
        B, S, IN, OUT, E, R = (8, 512, 128, 128, 8, 8)
        LORA_ALPHA = 16
        SCALING = LORA_ALPHA / R
        result = jnp.einsum('bsd,od->bso', x, base_w) + base_b
        logits = jnp.einsum('bsd,ed->bse', x, router_w) + router_b
        gating = jax.nn.softmax(logits, axis=-1).astype(jnp.bfloat16)
        mid = jnp.einsum('bsd,dr->bsr', x, lora_A)
        lora_out = jnp.einsum('bsr,erd,bse->bsd', mid, lora_B, gating.astype(jnp.float32))
        return result + lora_out * SCALING
    x = x + _L0_xattn_ref(_layernorm(x, axis=-1), ctx_1024, ctx_1024, L0_xattn_Wq, L0_xattn_bq, L0_xattn_Wk, L0_xattn_bk, L0_xattn_Wv, L0_xattn_bv, L0_xattn_Wo, L0_xattn_bo, mask_SxS2_ik0, mask_BxS2_if1)
    x = x + _L0_ffn_ref(_layernorm(x, axis=-1), L0_ffn_router_w, L0_ffn_w_gate, L0_ffn_w_up, L0_ffn_w_down)
    x = x + _L1_xattn_ref(_layernorm(x, axis=-1), ctx_1024, L1_xattn_Wq, L1_xattn_bq, L1_xattn_Wk, L1_xattn_bk, L1_xattn_Wv, L1_xattn_bv)
    x = x + _L1_ffn_ref(_layernorm(x, axis=-1), L1_ffn_base_w, L1_ffn_base_b, L1_ffn_lora_A, L1_ffn_lora_B, L1_ffn_router_w, L1_ffn_router_b)
    return x

_drawn_inputs = setup_inputs


def setup_inputs(seed=0):
    import zlib

    import numpy as np

    out = dict(_drawn_inputs(seed))
    spreads = {'L1_xattn_bq': (0.0, 0.418),
     'L1_xattn_bk': (0.0, 0.8),
     'L1_xattn_bv': (0.0, 0.1),
     'L1_ffn_base_b': (0.0, 0.1),
     'L1_ffn_router_b': (0.0, 0.8)}
    factors = {'L0_xattn_bk': 8.0, 'L1_ffn_lora_A': 8.0, 'L1_ffn_lora_B': 8.0, 'L1_ffn_router_w': 8.0}
    for name, (base, spread) in spreads.items():
        noise = np.random.default_rng([zlib.crc32(name.encode()), seed]).standard_normal(out[name].shape)
        drawn = base * np.exp(spread * noise) if base else spread * noise
        out[name] = jnp.asarray(drawn.astype(out[name].dtype))
    for name, factor in factors.items():
        out[name] = (out[name] * factor).astype(out[name].dtype)
    return out
```

```python
from contextlib import ExitStack

import concourse.bass as bass
from concourse import mybir

F32 = mybir.dt.float32
F32R = mybir.dt.float32r
BF16 = mybir.dt.bfloat16
I32 = mybir.dt.int32
ALU = mybir.AluOpType
ACT = mybir.ActivationFunctionType
AX_X = mybir.AxisListType.X

P = 128
B, S, D = 4, 512, 128
TB = S // P
NT = B * TB
TOK = B * S
SK, SKP = 77, 78
H = 16
DK = D // H
OC = DK + 1
HK = H * SK
CH = 124
NC = -(-HK // CH)
GROUPS = [(0, 6), (6, 6), (12, 4)]
E, FF = 8, 512
FC = FF // P
TOPK = 2
ST = (TOK * TOPK + E * (P - 1)) // P
ROWS = TOPK * TOK
R = 8
HARD = -1.0e30
EPS = 1e-5
WP = 1024
NW = 3 * E * FF // WP
SLOTS = 4

WK0, WV0, CTX, WO0, RT0, WQ1, WK1, WV1, FB1, NSPLIT = 0, 128, 256, 568, 696, 704, 832, 960, 1088, 1232
EARLY = WO0
IDN, WQ0, HM, COL, LB, BLK, LT8, TIDX, PCOL, WDS, M128, SPARE, NPLAIN = (
    0, 128, 256, 272, 276, 404, 434, 498, 530, 532, 540, 556, 556 + ST)
BO, BV0, BV1, BB1, RB1, NROWS = 0, 128, 368, 496, 624, 632
UT, ON, IOP, IOT, IDB, NTAB = 0, 128, 256, 384, 384 + ST, 512 + ST
FBW = D + E + R


def first_head(c):
    return min(CH * c // SK, H - 3)


def rows_of(c):
    return min(CH, HK - CH * c)


T0_USES = [("x", 0), ("x", 1), ("x", 2), ("o", 0), ("y", 0), ("x", 3)] + [(k, b) for b in (1, 2, 3) for k in ("o", "y")]
T1_USES = ([("kt", 0), ("bias", 0), ("flags", 0), ("shift", 0), ("shift", 1)]
           + [("wo", 0), ("logits", 0), ("shift", 2), ("wo", 1), ("logits", 1), ("shift", 3)]
           + [(k, b) for b in (2, 3) for k in ("wo", "logits")])


def t0(kind, b):
    return T0_USES.index((kind, b))


def t1(kind, b):
    return T1_USES.index((kind, b))


def a_job(kind, b, n):
    return 15 * b + (n if kind == "keys" else 3 + n)


def unit(n):
    return n // len(GROUPS), GROUPS[n % len(GROUPS)]


T_JOBS = [("x", 0), ("x", 1), ("x", 2), ("x", 3), ("p", 0), ("p", 1), ("p", 2), ("p", 3),
          ("y", 0), ("y", 1), ("y", 2), ("z", 0), ("z", 1), ("y", 3), ("z", 2), ("z", 3)]
PE_END = [0, 1, "s0", 2, "s1", 3, "s2", 4, "s3", 5, "v0", 6, "v1", 7, "v2", 8, "v3", 9, "b0", 10, "b1",
          11, "l0", 12, "l1", "b2", 13, "b3", 14, "l2", 15, "l3"]
ACT_END = [0, 1, 2, "e0", 3, "e1", 4, "e2", 5, "e3", 6, 7, 8, 9, 10, "g0", "g1", 11, 12, 13, "g2", "g3", 14, 15]
DVE_END = ["c0", "c1", "n0", "c2", "n1", 0, "c3", "n2", 1, "s0", "n3", 2, "s1", 3, "s2", 4, "s3", 5, "a0", 6,
           "a1", 7, "m0", "a2", "m1", 8, "a3", "m2", 9, "m3", "g0", "o0", 10, "g1", "o1", 11, 12, "f0", 13, "f1",
           "g2", "o2", "g3", "o3", 14, 15, "f2", "f3"]
HEAD = 6
LOOPS = (ST - 1 - HEAD) // SLOTS

UNITS_AT = [[], [0], [1, 2], [3], [4, 5], [6, 7], [8], [9, 10], [11], []]


def spread(ap, axis, n):
    v = ap.unsqueeze(axis)
    return v.broadcast_to([*v.shape[:axis], n, *v.shape[axis + 1:]])


def xattn_moe_xattn_lora_kernel(nc, x, split, plain, rows, tables, select, mask_t, pad_t, w_gate, w_up, w_down, out):
    with ExitStack() as stack:
        def sb(name, shape, dt=F32):
            return stack.enter_context(nc.sbuf_tensor("sb_" + name, shape, dt))

        def bank(name):
            return stack.enter_context(nc.psum_tensor("ps_" + name, [P, 512], F32))

        def sem(name):
            return stack.enter_context(nc.semaphore(name))

        normed_d = nc.dram_tensor("normed_rows", [TOK, D], F32).ap()
        expert_d = nc.dram_tensor("expert_rows", [ROWS + ST * P, D], F32).ap()

        w_hi = [sb(n + "_hi", [P, E * FF], F32R) for n in ("gate", "up", "down")]
        w_lo = [sb(n + "_lo", [P, E * FF], F32R) for n in ("gate", "up", "down")]
        work = sb("work", [P, SLOTS * WP])
        X = sb("X", [P, NT, D])
        XN = sb("XN", [P, 2, TB, D])
        T_hi = sb("T_hi", [P, 3, S], F32R)
        T_lo = sb("T_lo", [P, 3, S], F32R)
        kq_hi = sb("kq_hi", [P, 2 * HK], F32R)
        kq_lo = sb("kq_lo", [P, 2 * HK], F32R)
        sel = sb("sel", [P, B, HK], BF16)
        Z = sb("Z", [P, B, S], BF16)
        probs = sb("probs", [P, 3, S])
        vblk = sb("vblk", [P, B, NC, 3 * OC])
        sp_hi = sb("sp_hi", [P, NSPLIT], F32R)
        sp_lo = sb("sp_lo", [P, NSPLIT], F32R)
        pl = sb("pl", [P, NPLAIN])
        rw = sb("rw", [P, NROWS])
        tab = sb("tab", [P, NTAB], BF16)
        kt = sb("bias1", [P, B * SKP])
        kt_hi = sb("kt_hi", [P, B * SKP], F32R)
        kt_lo = sb("kt_lo", [P, B * SKP], F32R)
        bq_hi = sb("bq_hi", [P, H], F32R)
        bq_lo = sb("bq_lo", [P, H], F32R)
        bqm = sb("bqm", [P, H])
        stats = sb("stats", [P, TB, 6])
        mv = sb("mv", [P, 4 * B, TB, 2])
        rstd = sb("rstd", [P, 4 * B, TB])
        power = sb("power", [P, TB])
        negmax = sb("negmax", [P, TB, H])
        shift = sb("shift", [P, TB, 2 * H], BF16)
        O = sb("O", [P, TB, D])
        rsum = sb("rsum", [P, TB, H])
        flags = sb("flags", [P, NT])
        flag2 = sb("flag2", [P, NT])
        padf = sb("padf", [SK, 2, B])
        padk = sb("padk", [SK, B], BF16)
        padi = sb("padi", [SK, B], I32)
        L = sb("L", [P, NT, E])
        L2 = sb("L2", [P, TB, E])
        oh = sb("oh", [P, TOPK, NT, E])
        m12 = sb("m12", [P, TOPK, NT])
        mx = sb("mx", [P, TOPK, NT])
        cnt = sb("cnt", [P, NT, E], BF16)
        wts = sb("wts", [P, TOPK, NT])
        et = sb("et", [P, NT])
        etab = sb("etab", [1, ST], I32)
        gidx = sb("gidx", [P, ST], I32)
        didx = sb("didx", [P, ST], I32)
        L3 = sb("L3", [P, TB, E])
        tiles = sb("tiles", [P, 2, E])
        nm1 = sb("nm1", [P, NT])
        sum1 = sb("sum1", [P, NT])
        gl = sb("gl", [P, 2, TB, E])
        gm = sb("gm", [P, TB])
        gates = sb("gates", [P, TB, E], BF16)

        ident = pl[:, IDN:IDN + P]
        sp = work[:, 0:NSPLIT]
        qm_hi = w_hi[2][:, 0:H * D].rearrange("p (h d) -> p h d", h=H)
        qm_lo = w_hi[2][:, H * D:2 * H * D].rearrange("p (h d) -> p h d", h=H)
        ctx3_hi = w_lo[2][:, 0:B * 3 * SK].rearrange("p (b k) -> p b k", b=B)
        ctx3_lo = w_lo[2][:, 1024:1024 + B * 3 * SK].rearrange("p (b k) -> p b k", b=B)
        maskt = probs[0:SK, 0, :].bitcast(I32)
        keept = probs[0:SK, 1, 0:S // 2].bitcast(BF16)
        maskz = probs[0:SK, 2, :]
        onehot = work[:, 0:2048].bitcast(BF16).rearrange("p (q i) -> p q i", i=P)
        where = work[:, 2048:2048 + 48 * ST].bitcast(BF16).rearrange("p (v q i) -> p v q i", v=3, i=ST)
        G = work[:, 0:512].rearrange("p (s d) -> p s d", s=SLOTS)
        SG = work[:, 512:1536].rearrange("p (s f) -> p s f", s=2)
        HH = work[:, 1536:2560].rearrange("p (s f) -> p s f", s=2)
        Y = work[:, 2560:3072].rearrange("p (s d) -> p s d", s=SLOTS)
        XT_hi, XT_lo = T_hi[:, 0, :], T_lo[:, 0, :]
        yk = work[:, 0:TOPK * NT * D].rearrange("p (k t d) -> p k t d", k=TOPK, t=NT)
        P1 = probs[:, :, :].rearrange("p a s -> p (a s)")[:, 0:NT * SKP].rearrange("p (t k) -> p t k", k=SKP)
        scratch = probs[:, :, :].rearrange("p a s -> p (a s)")
        pos = scratch[:, 0:256].rearrange("p (k t e) -> p k t e", k=TOPK, e=E)
        cmp16 = scratch[:, 256:384].rearrange("p (e m) -> p e m", e=E)
        cmp8 = scratch[:, 384:448].rearrange("p (e f) -> p e f", e=E)
        cmpt = scratch[:, 448:448 + ST * E].rearrange("p (i e) -> p i e", e=E)
        inv = scratch[:, 1024:1024 + 4 * ST]
        etf = scratch[:, 1180:1180 + ST]
        sloti = scratch[:, 1220:1316].bitcast(I32).rearrange("p (v k t) -> p v k t", v=3, k=TOPK)
        tile_row = scratch[:, 1316:1380].rearrange("p (v k t) -> p v k t", v=2, k=TOPK)
        slot = scratch[:, 1380:1412].rearrange("p (k t) -> p k t", k=TOPK)
        bias3 = XN[0:H, 1, :, :].rearrange("p t d -> p (t d)").bitcast(BF16)[:, 0:3 * B * SKP].rearrange(
            "p (v k) -> p v k", v=3)
        pairs = vblk[:, 0:2, :, :].rearrange("p b c j -> p (b c j)")[:, 0:2 * TB * E * R].rearrange(
            "p (u t j) -> p u t j", u=2, t=TB)
        K1, A1, V1, LBM, BQ1 = 0, 312, 624, 1136, 1264
        ident_bf = tab[:, IDB:IDB + P]
        bq1_hi, bq1_lo = kq_hi[:, BQ1:BQ1 + P], kq_lo[:, BQ1:BQ1 + P]

        ringA = [bank(f"A{i}") for i in range(2)]
        ringB = [bank(f"B{i}") for i in range(2)]
        accs = [bank(f"acc{i}") for i in range(2)]
        T0, T1 = bank("T0"), bank("T1")

        plain_in, split_in, late_in, rows_in, tab_in = (sem(n) for n in ("plain_in", "split_in", "late_in", "rows_in", "tab_in"))
        mask_in, sel_in, bias_rows_in = (sem(n) for n in ("mask_in", "sel_in", "bias_rows_in"))
        x_in = [sem(f"x_in{b}") for b in range(B)]
        w_in = [sem(f"w_in{i}") for i in range(SLOTS)]
        gathered = [sem(f"gathered{i}") for i in range(SLOTS)]
        scattered = [sem(f"scattered{i}") for i in range(SLOTS)]
        expert_in = [sem(f"expert_in{b}") for b in range(B)]
        normed_out, result_out = sem("normed_out"), sem("result_out")
        split_hi, split_done = sem("split_hi"), sem("split_done")
        heads_done, ctx3_done, ctx3_hi_done = sem("heads_done"), sem("ctx3_done"), sem("ctx3_hi_done")
        kt_hi_done, biasrows_done, experts_done = sem("kt_hi_done"), sem("biasrows_done"), sem("experts_done")
        t0_filled, t0_hi, t0_freed = sem("t0_filled"), sem("t0_hi"), sem("t0_freed")
        t1_filled, t1_freed = sem("t1_filled"), sem("t1_freed")
        a_filled, a_hi, a_freed = sem("a_filled"), sem("a_hi"), sem("a_freed")
        b_filled, exp_done, pv_done = sem("b_filled"), sem("exp_done"), sem("pv_done")
        v_filled, v_done, o_done = sem("v_filled"), sem("v_done"), sem("o_done")
        keep_done, z_done, shift_done = sem("keep_done"), sem("z_done"), sem("shift_done")
        ln_stats, ln_rstd, ln_done = sem("ln_stats"), sem("ln_rstd"), sem("ln_done")
        w_hi_done, w_lo_done = sem("w_hi_done"), sem("w_lo_done")
        dve_step, act_step, pool_step = sem("dve_step"), sem("act_step"), sem("pool_step")
        picked, rank_filled, onehot_done, inverse_filled, index_done = (
            sem(n) for n in ("picked", "rank_filled", "onehot_done", "inverse_filled", "index_done"))
        wexp_done, weights_done = sem("wexp_done"), sem("weights_done")
        gate_filled, up_filled, silu_done, h_done = (sem(n) for n in ("gate_filled", "up_filled", "silu_done", "h_done"))
        ht_filled, ht_hi, ht_ready = sem("ht_filled"), sem("ht_hi"), sem("ht_ready")
        xt_filled, xt_hi, xt_ready = sem("xt_filled"), sem("xt_hi"), sem("xt_ready")
        y_filled, y_copied = sem("y_filled"), sem("y_copied")
        k1_filled, k1_hi, k1_done = sem("k1_filled"), sem("k1_hi"), sem("k1_done")
        f_filled, f_hi, f_freed = sem("f_filled"), sem("f_hi"), sem("f_freed")
        sc_filled, sc_copied, negmax1_done, p1_done = (sem(n) for n in ("sc_filled", "sc_copied", "negmax1_done", "p1_done"))
        pv1_filled, pv1_freed, fb_filled, fb_freed = (sem(n) for n in ("pv1_filled", "pv1_freed", "fb_filled", "fb_freed"))
        gate_in, gate_exp, outer_done, lora_filled, result_done = (
            sem(n) for n in ("gate_in", "gate_exp", "outer_done", "lora_filled", "result_done"))
        pool_x = sem("pool_x")

        block = stack.enter_context(nc.Block())

        @block.sync
        def _(sp_eng):
            sp_eng.dma_start(sp[:, 0:EARLY], split[:, 0:EARLY]).then_inc(split_in, 16)
            sp_eng.dma_start(pl[:, :], plain).then_inc(plain_in, 16)
            xt = x.rearrange("(b t p) d -> b p t d", p=P, t=TB)
            sp_eng.dma_start(X[:, 0:TB, :], xt[0]).then_inc(x_in[0], 16)
            sp_eng.dma_start(maskt, mask_t).then_inc(mask_in, 16)
            sp_eng.dma_start(padi[:, :], pad_t).then_inc(mask_in, 16)
            sp_eng.dma_start(sel[:, :, :], spread(select, 1, B)).then_inc(sel_in, 16)
            sp_eng.dma_start(rw[:, :], rows.broadcast_to([P, NROWS])).then_inc(rows_in, 16)
            for b in range(1, B):
                sp_eng.dma_start(X[:, b * TB:(b + 1) * TB, :], xt[b]).then_inc(x_in[b], 16)
            sp_eng.dma_start(sp[:, EARLY:], split[:, EARLY:]).then_inc(late_in, 16)
            sp_eng.dma_start(tab[:, :], tables).then_inc(tab_in, 16)

            sp_eng.wait_ge(sel_in, 16)
            sp_eng.wait_ge(biasrows_done, 1)
            for b in range(B):
                for part in range(3):
                    dst = sel[SK + part:SK + part + 1, b, :].rearrange("o (h k) -> o h k", k=SK)
                    sp_eng.dma_start(dst, bias3[:, part, b * SKP:b * SKP + SK]).then_inc(bias_rows_in, 16)

            def piece(i):
                slot, which, e = (i + 2) % SLOTS, i // 4, 2 * (i % 4)
                if i in (2, 3):
                    sp_eng.wait_ge(split_done, 2)
                if i >= SLOTS:
                    sp_eng.wait_ge(w_lo_done, i - SLOTS + 1)
                for n in range(2):
                    at = work[:, slot * WP + n * FF:slot * WP + (n + 1) * FF]
                    if which < 2:
                        src = (w_gate, w_up)[which][e + n]
                    else:
                        src = w_down[e + n].rearrange("(c p) d -> p c d", p=P)
                        at = at.rearrange("p (c d) -> p c d", c=FC)
                    sp_eng.dma_start(at, src).then_inc(w_in[slot], 16)

            nd = normed_d.rearrange("(b t p) d -> b p t d", p=P, t=TB)
            for i in range(SLOTS):
                piece(i)
            for b in range(B):
                for i in range(SLOTS + 3 * b, min(SLOTS + 3 * b + 3, NW)):
                    piece(i)
                if b >= 1:
                    sp_eng.wait_ge(ln_done, B + b)
                    sp_eng.dma_start(nd[b - 1], XN[:, 1, :, :]).then_inc(normed_out, 16)
            sp_eng.wait_ge(ln_done, 2 * B)
            sp_eng.dma_start(nd[B - 1], XN[:, 1, :, :]).then_inc(normed_out, 16)

            for i in range(SLOTS):
                sp_eng.wait_ge(scattered[i], 16 * len(range(i, ST, SLOTS)))
            ed = expert_d[0:ROWS, :].rearrange("(k b t p) d -> k b p t d", k=TOPK, b=B, p=P)
            for b in range(B):
                for k in range(TOPK):
                    sp_eng.dma_start(yk[:, k, b * TB:(b + 1) * TB, :], ed[k, b]).then_inc(expert_in[b], 16)
            ot = out.rearrange("(b t p) d -> b p t d", p=P, t=TB)
            for b in range(B):
                sp_eng.wait_ge(result_done, b + 1)
                sp_eng.dma_start(ot[b], X[:, b * TB:(b + 1) * TB, :]).then_inc(result_out, 16)
            sp_eng.wait_ge(result_out, 16 * B)
            sp_eng.wait_ge(normed_out, 16 * B)

        @block.gpsimd
        def _(pool):
            steps = [0]

            def then(ins):
                steps[0] += 1
                ins.then_inc(pool_step, 1)
                pool.wait_ge(pool_step, steps[0])

            def rstd_of(n):
                pool.wait_ge(ln_stats, n + 1)
                then(pool.tensor_scalar(rstd[:, n, :], mv[:, n, :, 1], EPS, None, ALU.add))
                pool.tensor_tensor(rstd[:, n, :], rstd[:, n, :], power[:, :], ALU.pow).then_inc(ln_rstd, 1)

            then(pool.memset(power[:, :], -0.5))
            rstd_of(0)
            pool.wait_ge(split_done, 1)
            low = sp_lo[:, CTX:CTX + B * SKP].bitcast(F32).rearrange("p (b k) -> p b k", k=SKP)[:, :, 0:SK]
            pool.tensor_copy(ctx3_lo.rearrange("p b (r k) -> p b r k", r=3), spread(low, 2, 3)).then_inc(ctx3_done, 1)
            for n in range(1, B):
                rstd_of(n)

            def residual(b):
                here = X[:, b * TB:(b + 1) * TB, :]
                pool.wait_ge(ln_done, b + 1)
                if b == 0:
                    pool.wait_ge(rows_in, 16)
                    pool.wait_ge(t1_freed, t1("flags", 0) + 1)
                then(pool.tensor_tensor(here, here, spread(rw[:, BO:BO + D], 1, TB), ALU.add))
                for t in range(b * TB, (b + 1) * TB):
                    ins = pool.tensor_scalar(X[:, t, :], X[:, t, :], flags[:, t:t + 1], None, ALU.add)
                ins.then_inc(pool_x, 1)

            def low_part(i):
                at = slice((i % 4) * WP, (i % 4 + 1) * WP)
                slot = (i + 2) % SLOTS
                pool.wait_ge(w_hi_done, i + 1)
                pool.tensor_tensor(w_lo[i // 4][:, at], work[:, slot * WP:(slot + 1) * WP],
                                   w_hi[i // 4][:, at].bitcast(F32), ALU.subtract).then_inc(w_lo_done, 1)

            for b in range(B):
                residual(b)
                low_part(3 * b)
                low_part(3 * b + 1)
                if b >= 1:
                    rstd_of(B + b - 1)
                low_part(3 * b + 2)
            rstd_of(2 * B - 1)

            pool.wait_ge(index_done, 1)
            pool.wait_ge(normed_out, 16 * B)
            def gather(s):
                n = s % SLOTS
                if s >= SLOTS:
                    pool.wait_ge(xt_filled, s - SLOTS + 1)
                pool.indirect_dma_start(
                    out=G[:, n, :], out_offset=None, in_=normed_d,
                    in_offset=bass.IndirectOffsetOnAxis(ap=gidx[:, s:s + 1], axis=0)).then_inc(gathered[n], 16)

            def scatter(s):
                n = s % SLOTS
                pool.wait_ge(y_copied, s + 1)
                pool.indirect_dma_start(
                    out=expert_d, out_offset=bass.IndirectOffsetOnAxis(ap=didx[:, s:s + 1], axis=0),
                    in_=Y[:, n, :], in_offset=None).then_inc(scattered[n], 16)

            for s in range(ST + SLOTS + 2):
                if s < ST:
                    gather(s)
                if s >= SLOTS + 2:
                    scatter(s - SLOTS - 2)

            for n in range(2 * B, 3 * B):
                rstd_of(n)
            def add_bias(b):
                here = X[:, b * TB:(b + 1) * TB, :]
                pool.wait_ge(ln_done, 3 * B + b + 1)
                pool.tensor_tensor(here, here, spread(rw[:, BB1:BB1 + D], 1, TB), ALU.add).then_inc(pool_x, 1)

            for n in range(3 * B, 4 * B):
                rstd_of(n)
                if n >= 3 * B + 2:
                    add_bias(n - 3 * B - 2)
            add_bias(B - 2)
            add_bias(B - 1)

        @block.scalar
        def _(act):
            act.wait_ge(split_in, 16)
            act.activation(sp_hi[:, 0:EARLY], sp[:, 0:EARLY], ACT.Copy).then_inc(split_hi, 1)
            keys_in = sp[:, CTX:CTX + B * SKP].rearrange("p (b k) -> p b k", k=SKP)[:, :, 0:SK]
            act.activation(ctx3_hi.rearrange("p b (r k) -> p b r k", r=3), spread(keys_in, 2, 3), ACT.Copy)\
               .then_inc(ctx3_hi_done, 1)
            act.wait_ge(late_in, 16)
            act.activation(sp_hi[:, EARLY:], sp[:, EARLY:], ACT.Copy).then_inc(split_hi, 1)
            act.wait_ge(t1_filled, t1("kt", 0) + 1)
            act.wait_ge(plain_in, 16)
            act.activation(kt_hi[:, :], T1[:, 0:B * SKP], ACT.Identity, bias=pl[:, COL + 1:COL + 2]).then_inc(kt_hi_done, 1)

            def turned_hi(kind, b):
                n = t0(kind, b)
                act.wait_ge(t0_filled, n + 1)
                act.activation(T_hi[:, b % 2 if kind == "x" else 2, :], T0[:, :], ACT.Copy).then_inc(t0_hi, 1)

            def keys_hi(b, n):
                h0, nh = GROUPS[n]
                job = a_job("keys", b, n)
                act.wait_ge(a_filled, job + 1)
                at = slice((b % 2) * HK + h0 * SK, (b % 2) * HK + (h0 + nh) * SK)
                act.activation(kq_hi[:, at].rearrange("p (h k) -> p h k", k=SK),
                               ringA[job % 2][:, 0:nh * SKP].rearrange("p (h k) -> p h k", k=SKP)[:, :, 0:SK],
                               ACT.Copy).then_inc(a_hi, 1)

            def shift_in(b):
                act.wait_ge(t1_filled, t1("shift", b) + 1)
                act.activation(Z[96:96 + 2 * H, b, :], T1[0:2 * H, 0:S // 2].bitcast(BF16), ACT.Copy).then_inc(t1_freed, 1)

            def exps(b, c):
                n = NC * b + c
                act.wait_ge(b_filled, n + 1)
                if n >= 3:
                    act.wait_ge(pv_done, n - 2)
                act.activation(probs[0:rows_of(c), n % 3, :], ringB[n % 2][0:rows_of(c), :], ACT.Exp,
                               scale=DK ** -0.5).then_inc(exp_done, 1)

            def high_part(i):
                slot = (i + 2) % SLOTS
                act.wait_ge(w_in[slot], 32 * (i // SLOTS + 1))
                if i == 8:
                    act.wait_ge(a_filled, a_job("keys", B - 1, 2) + 1)
                act.activation(w_hi[i // 4][:, (i % 4) * WP:(i % 4 + 1) * WP], work[:, slot * WP:(slot + 1) * WP],
                               ACT.Copy).then_inc(w_hi_done, 1)

            for n in range(3):
                keys_hi(0, n)
            turned_hi("x", 0)
            shift_in(0)
            for b in range(B):
                for c in range(NC):
                    exps(b, c)
                    if c == 0 and b + 1 < B:
                        turned_hi("x", b + 1)
                        for n in range(3):
                            keys_hi(b + 1, n)
                    if c == 2 and b >= 1:
                        turned_hi("o", b - 1)
                    if c == 8 and b >= 1:
                        turned_hi("y", b - 1)
                    if c in (1, 4, 7):
                        high_part(3 * b + c // 3)
                if b + 1 < B:
                    shift_in(b + 1)
            turned_hi("o", B - 1)
            turned_hi("y", B - 1)

            act.wait_ge(picked, B)
            act.activation(et[:, :], et[:, :], ACT.Exp).then_inc(wexp_done, 1)

            act.wait_ge(k1_filled, 1)
            act.activation(kq_hi[:, K1:K1 + B * SKP], T0[:, 0:B * SKP], ACT.Identity,
                           bias=pl[:, COL + 2:COL + 3]).then_inc(k1_hi, 1)
            act.wait_ge(k1_filled, 2)
            act.activation(kq_hi[:, A1:A1 + B * SKP], T0[:, 0:B * SKP], ACT.Copy).then_inc(k1_hi, 1)
            act.wait_ge(k1_done, 3)
            act.activation(kq_hi[0:SK, V1:V1 + B * D], O[0:SK, :, :].rearrange("p t d -> p (t d)"), ACT.Copy)\
               .then_inc(k1_hi, 1)
            act.wait_ge(k1_filled, 4)
            act.activation(kt[:, :], T0[:, 0:B * SKP], ACT.Copy).then_inc(k1_hi, 1)

            def xt_high(i, k):
                s, u = 4 * i + k, k % 2
                act.wait_ge(xt_filled, s + 1)
                if k >= 2:
                    act.wait_ge(up_filled, s - 1)
                act.activation(XT_hi[:, u * P:(u + 1) * P], T0[:, 0:P], ACT.Copy).then_inc(xt_hi, 1)

            def silu(i, k):
                s, u = 4 * i + k, k % 2
                act.wait_ge(gate_filled, s + 1)
                if k >= 2:
                    act.wait_ge(h_done, s - 1)
                act.activation(SG[:, u, :], ringA[u][:, :], ACT.Silu).then_inc(silu_done, 1)

            def ht_high(i, k):
                s, u = 4 * i + k, k % 2
                act.wait_ge(ht_filled, s + 1)
                if k >= 2:
                    act.wait_ge(y_filled, s - 1)
                act.activation(T_hi[:, 1 + u, :], accs[u][:, :], ACT.Copy).then_inc(ht_hi, 1)

            def step(i, k):
                if k < ST:
                    silu(i, k)
                if k + 1 < ST:
                    xt_high(i, k + 1)
                if 1 <= k <= ST:
                    ht_high(i, k - 1)

            xt_high(0, 0)
            for k in range(HEAD):
                step(0, k)
            with act.Fori(0, LOOPS) as i:
                for u in range(SLOTS):
                    step(i, HEAD + u)
            for k in range(HEAD + SLOTS * LOOPS, ST + 2):
                step(0, k)

            def part(n):
                kind, b = T_JOBS[n]
                rows_ = {"x": P, "p": SK, "y": P, "z": E * R}[kind]
                act.wait_ge(f_filled, n + 1)
                act.activation(T_hi[0:rows_, n % 3, :], (T0, T1)[n % 2][0:rows_, :], ACT.Copy).then_inc(f_hi, 1)

            def exp1(b):
                act.wait_ge(negmax1_done, b + 1)
                for t in range(b * TB, (b + 1) * TB):
                    ins = act.activation(P1[:, t, 0:SK], P1[:, t, 0:SK], ACT.Exp, bias=nm1[:, t:t + 1],
                                         scale=D ** -0.5, accum_out=sum1[:, t:t + 1])
                ins.then_inc(p1_done, 1)

            def gate_exps(b):
                act.wait_ge(gate_in, b + 1)
                act.activation(gl[:, b % 2, :, :], gl[:, b % 2, :, :], ACT.Exp).then_inc(gate_exp, 1)

            for what in ACT_END:
                if isinstance(what, int):
                    part(what)
                elif what[0] == "e":
                    exp1(int(what[1]))
                else:
                    gate_exps(int(what[1]))

        @block.vector
        def _(dve):
            steps = [0]

            def then(ins):
                steps[0] += 1
                ins.then_inc(dve_step, 1)
                dve.wait_ge(dve_step, steps[0])

            def norm_stats(n):
                b = n % B
                if n:
                    dve.wait_ge(ln_stats, n)
                for t in range(TB):
                    ins = dve.bn_stats(stats[:, t, :], X[:, b * TB + t, :])
                then(ins)
                for t in range(TB):
                    ins = dve.bn_aggr(mv[:, n, t, :], stats[:, t, :])
                ins.then_inc(ln_stats, 1)

            def norm(n, slot):
                b = n % B
                dve.wait_ge(ln_rstd, n + 1)
                for t in range(TB):
                    ins = dve.tensor_scalar(XN[:, slot, t, :], X[:, b * TB + t, :], mv[:, n, t, 0:1],
                                            rstd[:, n, t:t + 1], ALU.subtract, ALU.mult)
                ins.then_inc(ln_done, 1)

            dve.wait_ge(x_in[0], 16)
            norm_stats(0)
            dve.wait_ge(split_hi, 1)
            dve.tensor_tensor(sp_lo[:, 0:EARLY], sp[:, 0:EARLY], sp_hi[:, 0:EARLY].bitcast(F32), ALU.subtract)\
               .then_inc(split_done, 1)
            dve.wait_ge(plain_in, 16)
            wq = pl[:, WQ0:WQ0 + D]
            for h in range(H):
                ins = dve.tensor_scalar(qm_hi[:, h, :], wq, pl[:, HM + h:HM + h + 1], None, ALU.mult)
            then(ins)
            for h in range(H):
                ins = dve.scalar_tensor_tensor(out=qm_lo[:, h, :], in0=wq, scalar=pl[:, HM + h:HM + h + 1],
                                               in1=qm_hi[:, h, :].bitcast(F32), op0=ALU.mult, op1=ALU.subtract)
            ins.then_inc(heads_done, 1)
            then(dve.tensor_scalar(bqm[:, :], pl[:, HM:HM + H], pl[:, COL:COL + 1], None, ALU.mult))
            then(dve.tensor_copy(bq_hi[:, :], bqm[:, :]))
            dve.tensor_tensor(bq_lo[:, :], bqm[:, :], bq_hi[:, :].bitcast(F32), ALU.subtract).then_inc(heads_done, 1)
            dve.wait_ge(kt_hi_done, 1)
            dve.scalar_tensor_tensor(out=kt_lo[:, :], in0=T1[:, 0:B * SKP], scalar=pl[:, COL + 1:COL + 2],
                                     in1=kt_hi[:, :].bitcast(F32), op0=ALU.add, op1=ALU.subtract).then_inc(t1_freed, 1)
            norm(0, 0)

            dve.wait_ge(mask_in, 32)
            dve.tensor_scalar(keept, maskt, 0, None, ALU.not_equal).then_inc(keep_done, 1)
            dve.tensor_scalar(padk[:, :], padi[:, :], 0, None, ALU.not_equal).then_inc(keep_done, 1)
            dve.tensor_scalar(maskz, maskt, 0, HARD, ALU.is_equal, ALU.mult)
            dve.memset(Z[64:96, :, :], 1.0)
            then(dve.tensor_scalar(padf[:, 0, :], padi[:, :], 0, HARD, ALU.is_equal, ALU.mult))
            for b in range(B):
                ins = dve.tensor_scalar(Z[0:SK, b, :], maskz, padf[:, 0, b:b + 1], None, ALU.add)
            ins.then_inc(z_done, 1)

            dve.wait_ge(t1_filled, t1("bias", 0) + 1)
            rest = O[0:H, :, :].rearrange("p t d -> p (t d)")[:, 0:B * SKP]
            then(dve.tensor_copy(bias3[:, 0, :], T1[0:H, 0:B * SKP]))
            dve.tensor_tensor(rest, T1[0:H, 0:B * SKP], bias3[:, 0, :], ALU.subtract).then_inc(t1_freed, 1)
            dve.wait_ge(t1_freed, t1("bias", 0) + 1)
            then(dve.tensor_copy(bias3[:, 1, :], rest))
            then(dve.tensor_tensor(rest, rest, bias3[:, 1, :], ALU.subtract))
            dve.tensor_copy(bias3[:, 2, :], rest).then_inc(biasrows_done, 1)

            def keys_lo(b, n):
                h0, nh = GROUPS[n]
                job = a_job("keys", b, n)
                dve.wait_ge(a_hi, 3 * b + n + 1)
                at = slice((b % 2) * HK + h0 * SK, (b % 2) * HK + (h0 + nh) * SK)
                dve.tensor_tensor(kq_lo[:, at].rearrange("p (h k) -> p h k", k=SK),
                                  ringA[job % 2][:, 0:nh * SKP].rearrange("p (h k) -> p h k", k=SKP)[:, :, 0:SK],
                                  kq_hi[:, at].bitcast(F32).rearrange("p (h k) -> p h k", k=SK),
                                  ALU.subtract).then_inc(a_freed, 1)

            def turned_lo(kind, b):
                n = t0(kind, b)
                u = b % 2 if kind == "x" else 2
                dve.wait_ge(t0_hi, n + 1)
                dve.tensor_tensor(T_lo[:, u, :], T0[:, :], T_hi[:, u, :].bitcast(F32), ALU.subtract).then_inc(t0_freed, 1)

            def row_max(b, n):
                t, (h0, nh) = unit(n)
                job = a_job("max", b, n)
                dve.wait_ge(a_filled, job + 1)
                dve.tensor_reduce(negmax[:, t, h0:h0 + nh],
                                  ringA[job % 2][:, 0:nh * SK].rearrange("p (h k) -> p h k", k=SK),
                                  AX_X, ALU.max, negate=True).then_inc(a_freed, 1)

            def shift_out(b):
                dve.wait_ge(a_freed, a_job("max", b, 11) + 1)
                if b >= 1:
                    dve.wait_ge(t1_filled, t1("shift", b - 1) + 1)
                then(dve.tensor_copy(shift[:, :, 0:H], negmax[:, :, :]))
                dve.tensor_tensor(shift[:, :, H:2 * H], negmax[:, :, :], shift[:, :, 0:H], ALU.subtract).then_inc(shift_done, 1)

            for n in range(3):
                keys_lo(0, n)
            turned_lo("x", 0)
            for b in range(B):
                dve.wait_ge(v_filled, b + 1)
                if b == 0:
                    dve.wait_ge(rows_in, 16)
                block_mask = pl[0:CH, BLK:BLK + 3 * NC].rearrange("p (c h) -> p c h", h=3)
                v3 = vblk[0:CH, b, :, :].rearrange("p c (h j) -> p (c h) j", j=OC)
                m3 = pl[0:CH, BLK:BLK + 3 * NC]
                then(dve.tensor_tensor(v3[:, :, 0:DK], accs[b % 2][0:CH, 0:3 * DK * NC].rearrange("p (g j) -> p g j", j=DK),
                                       rw[0:CH, BV0:BV0 + 3 * DK * NC].rearrange("p (g j) -> p g j", j=DK), ALU.add))
                dve.tensor_tensor(v3[:, :, 0:DK], v3[:, :, 0:DK], spread(m3, 2, DK), ALU.mult)
                dve.tensor_copy(v3[:, :, DK], m3).then_inc(v_done, 1)
            dve.wait_ge(t1_filled, t1("flags", 0) + 1)
            then(dve.tensor_scalar(flags[:, :].rearrange("p (b t) -> p t b", t=TB),
                                   T1[:, 0:NT].rearrange("p (t b) -> p t b", b=B), 0.0, 3e38, ALU.is_equal, ALU.mult))
            then(dve.tensor_scalar(flag2[:, :], flags[:, :], 1e10, None, ALU.mult))
            dve.tensor_tensor(flags[:, :], flag2[:, :], flag2[:, :], ALU.subtract).then_inc(t1_freed, 1)
            for n in range(12):
                row_max(0, n)
            shift_out(0)
            for b in range(1, B):
                dve.wait_ge(x_in[b], 16)
                norm_stats(b)
            dve.wait_ge(t0_filled, t0("x", 0) + 1)
            norm(1, 0)
            dve.wait_ge(split_hi, 2)
            dve.tensor_tensor(sp_lo[:, EARLY:], sp[:, EARLY:], sp_hi[:, EARLY:].bitcast(F32), ALU.subtract)\
               .then_inc(split_done, 1)

            def context(b):
                dve.wait_ge(pv_done, NC * (b + 1))
                halves = [accs[u][:, 0:2 * H * OC].rearrange("p (t h j) -> p t h j", t=2, j=OC) for u in range(2)]
                dve.reciprocal(rsum[:, 0:2, :], halves[0][:, :, :, DK])
                then(dve.reciprocal(rsum[:, 2:4, :], halves[1][:, :, :, DK]))
                if b >= 1:
                    dve.wait_ge(t0_filled, t0("o", b - 1) + 1)
                for t in range(TB):
                    ins = dve.tensor_tensor(O[:, t, :].rearrange("p (h j) -> p h j", j=DK), halves[t // 2][:, t % 2, :, 0:DK],
                                            spread(rsum[:, t, :], 2, DK), ALU.mult)
                ins.then_inc(o_done, 1)

            def add_attention(b):
                here = X[:, b * TB:(b + 1) * TB, :]
                dve.wait_ge(t1_filled, t1("wo", b) + 1)
                dve.wait_ge(pool_x, b + 1)
                dve.tensor_tensor(here, here, T1[:, :].rearrange("p (t d) -> p t d", t=TB), ALU.add).then_inc(t1_freed, 1)
                dve.wait_ge(t1_freed, t1("wo", b) + 1)
                norm_stats(B + b)

            def norm_for_experts(b):
                if b >= 1:
                    dve.wait_ge(normed_out, 16 * b)
                norm(B + b, 1)

            def pick(b):
                here = slice(b * TB, (b + 1) * TB)
                l, l2 = L[:, here, :], L2[:, :, :]
                falling = spread(pl[:, WDS:WDS + E], 1, TB)
                dve.wait_ge(t1_filled, t1("logits", b) + 1)
                dve.tensor_copy(l, T1[:, 0:TB * E].rearrange("p (t e) -> p t e", e=E)).then_inc(t1_freed, 1)
                dve.wait_ge(t1_freed, t1("logits", b) + 1)
                for k in range(TOPK):
                    src = (l, l2)[k]
                    then(dve.tensor_reduce(m12[:, k, here], src, AX_X, ALU.max))
                    then(dve.tensor_tensor(L3[:, :, :], src, spread(m12[:, k, here], 2, E), ALU.is_equal))
                    then(dve.tensor_tensor(L3[:, :, :], L3[:, :, :], falling, ALU.mult))
                    then(dve.tensor_reduce(mx[:, k, here], L3[:, :, :], AX_X, ALU.max))
                    then(dve.tensor_tensor(oh[:, k, here, :], falling, spread(mx[:, k, here], 2, E), ALU.is_equal))
                    if k == 0:
                        then(dve.scalar_tensor_tensor(out=l2, in0=oh[:, 0, here, :], scalar=HARD, in1=l,
                                                      op0=ALU.mult, op1=ALU.add))
                dve.tensor_tensor(et[:, here], m12[:, 1, here], m12[:, 0, here], ALU.subtract)
                dve.tensor_tensor(cnt[:, here, :], oh[:, 0, here, :], oh[:, 1, here, :], ALU.add).then_inc(picked, 1)

            for b in range(B):
                for c in range(NC):
                    if c == 0:
                        if b >= 1:
                            context(b - 1)
                        if b + 1 < B:
                            for n in range(3):
                                keys_lo(b + 1, n)
                            turned_lo("x", b + 1)
                    if b + 1 < B:
                        for n in UNITS_AT[c]:
                            row_max(b + 1, n)
                    if c == 3:
                        if b + 2 < B:
                            norm(b + 2, 0)
                        if b >= 1:
                            turned_lo("o", b - 1)
                    if b >= 1 and c == 5:
                        add_attention(b - 1)
                    if b >= 1 and c == 7:
                        norm_for_experts(b - 1)
                    if b >= 1 and c == 9:
                        turned_lo("y", b - 1)
                        pick(b - 1)
                if b + 1 < B:
                    shift_out(b + 1)
            context(B - 1)
            turned_lo("o", B - 1)
            add_attention(B - 1)
            norm_for_experts(B - 1)
            turned_lo("y", B - 1)
            pick(B - 1)

            dve.wait_ge(tab_in, 16)
            dve.wait_ge(rank_filled, 1)
            rank = T1[:, 0:NT * E].rearrange("p (t e) -> p t e", e=E)
            total = T1[:, NT * E:NT * E + E]
            then(dve.tensor_tensor(cmp16[:, :, :], spread(total, 2, 16), spread(pl[:, M128:M128 + 16], 1, E), ALU.is_gt))
            then(dve.tensor_reduce(tiles[:, 0, :], cmp16[:, :, :], AX_X, ALU.add))
            then(dve.tensor_tensor(cmp8[:, :, :], spread(tiles[:, 0, :], 1, E),
                                   pl[:, LT8:LT8 + E * E].rearrange("p (e f) -> p e f", f=E), ALU.mult))
            then(dve.tensor_reduce(tiles[:, 1, :], cmp8[:, :, :], AX_X, ALU.add))
            then(dve.scalar_tensor_tensor(out=pos[:, 0, :, :], in0=spread(tiles[:, 1, :], 1, NT), scalar=float(P),
                                          in1=rank, op0=ALU.mult, op1=ALU.add))
            then(dve.tensor_tensor(pos[:, 1, :, :], pos[:, 0, :, :], oh[:, 1, :, :], ALU.mult))
            then(dve.tensor_tensor(pos[:, 0, :, :], pos[:, 0, :, :], oh[:, 0, :, :], ALU.mult))
            then(dve.tensor_reduce(slot[:, :, :], pos[:, :, :, :], AX_X, ALU.add))
            then(dve.tensor_scalar(mx[:, :, :], mx[:, :, :], 0.0, float(P * P), ALU.is_equal, ALU.mult))
            then(dve.tensor_tensor(sloti[:, 0, :, :], slot[:, :, :], mx[:, :, :], ALU.add))
            dve.tensor_scalar(sloti[:, 1, :, :], sloti[:, 0, :, :], 7, None, ALU.logical_shift_right)
            then(dve.tensor_scalar(sloti[:, 2, :, :], sloti[:, 0, :, :], P - 1, None, ALU.bitwise_and))
            then(dve.tensor_copy(tile_row[:, :, :, :], sloti[:, 1:3, :, :]))
            row_of = tile_row[:, 1, :, :].rearrange("p k t -> p (k t)")
            tile_of = tile_row[:, 0, :, :].rearrange("p k t -> p (k t)")
            then(dve.tensor_tensor(where[:, 2, :, :], spread(tab[:, IOT:IOT + ST], 1, TOPK * NT),
                                   spread(tile_of, 2, ST), ALU.is_equal))
            dve.tensor_tensor(where[:, 0, :, :], where[:, 2, :, :], spread(pl[:, TIDX:TIDX + TOPK * NT], 2, ST), ALU.mult)
            dve.tensor_scalar(where[:, 1, :, :], where[:, 2, :, :], pl[:, PCOL:PCOL + 1], None, ALU.mult)\
               .then_inc(onehot_done, 1)
            for q in range(TOPK * NT):
                dve.tensor_scalar(onehot[:, q, :], tab[:, IOP:IOP + P], row_of[:, q:q + 1], None, ALU.is_equal)\
                   .then_inc(onehot_done, 1)
            then(dve.tensor_tensor(tiles[:, 0, :], tiles[:, 0, :], tiles[:, 1, :], ALU.add))
            then(dve.tensor_tensor(cmpt[0:1, :, :], spread(tiles[0:1, 0, :], 1, ST), spread(tab[0:1, IOT:IOT + ST], 2, E),
                                   ALU.is_le))
            then(dve.tensor_reduce(etf[0:1, :], cmpt[0:1, :, :], AX_X, ALU.add))
            dve.tensor_scalar(etab[0:1, :], etf[0:1, :], float(E - 1), None, ALU.min).then_inc(experts_done, 1)
            dve.wait_ge(inverse_filled, 1)
            then(dve.tensor_copy(inv[:, 0:3 * ST], T1[:, 0:3 * ST]))
            spare = pl[:, SPARE:SPARE + ST]
            dve.tensor_tensor(inv[:, 3 * ST:4 * ST], inv[:, 2 * ST:3 * ST], spare, ALU.mult)
            then(dve.scalar_tensor_tensor(out=inv[:, 0:ST], in0=inv[:, 0:ST], scalar=float(P), in1=inv[:, ST:2 * ST],
                                          op0=ALU.mult, op1=ALU.add))
            then(dve.tensor_copy(gidx[:, :], inv[:, 0:ST]))
            then(dve.tensor_tensor(inv[:, ST:2 * ST], spare, inv[:, 3 * ST:4 * ST], ALU.subtract))
            dve.tensor_tensor(didx[:, :], inv[:, 0:ST], inv[:, ST:2 * ST], ALU.add)
            dve.tensor_scalar(gidx[:, :], gidx[:, :], TOK - 1, None, ALU.bitwise_and).then_inc(index_done, 1)

            dve.wait_ge(wexp_done, 1)
            then(dve.tensor_scalar(wts[:, 0, :], et[:, :], 1.0, None, ALU.add))
            then(dve.reciprocal(wts[:, 0, :], wts[:, 0, :]))
            then(dve.tensor_tensor(wts[:, 1, :], et[:, :], wts[:, 0, :], ALU.mult))

            dve.wait_ge(k1_hi, 1)
            dve.scalar_tensor_tensor(out=kq_lo[:, K1:K1 + B * SKP], in0=T0[:, 0:B * SKP], scalar=pl[:, COL + 2:COL + 3],
                                     in1=kq_hi[:, K1:K1 + B * SKP].bitcast(F32), op0=ALU.add, op1=ALU.subtract)\
               .then_inc(k1_done, 1)
            dve.wait_ge(k1_hi, 2)
            dve.tensor_tensor(kq_lo[:, A1:A1 + B * SKP], T0[:, 0:B * SKP], kq_hi[:, A1:A1 + B * SKP].bitcast(F32),
                              ALU.subtract).then_inc(k1_done, 1)
            dve.wait_ge(k1_filled, 3)
            v1 = O[0:SK, :, :]
            dve.tensor_tensor(v1, T0[0:SK, :].rearrange("p (b d) -> p b d", d=D), spread(rw[0:SK, BV1:BV1 + D], 1, B),
                              ALU.add).then_inc(k1_done, 1)
            dve.wait_ge(k1_hi, 3)
            dve.tensor_tensor(kq_lo[0:SK, V1:V1 + B * D], v1.rearrange("p t d -> p (t d)"),
                              kq_hi[0:SK, V1:V1 + B * D].bitcast(F32), ALU.subtract).then_inc(k1_done, 1)
            then(dve.tensor_scalar(bq1_hi, ident, 0.0, pl[:, COL + 3:COL + 4], ALU.mult, ALU.add))
            dve.tensor_scalar(bq1_lo, bq1_hi.bitcast(F32), -1.0, pl[:, COL + 3:COL + 4], ALU.mult, ALU.add).then_inc(k1_done, 1)
            then(dve.tensor_scalar(kq_hi[0:E * R, LBM:LBM + D], pl[0:E * R, LB:LB + D], 2.0, None, ALU.mult))
            dve.scalar_tensor_tensor(out=kq_lo[0:E * R, LBM:LBM + D], in0=pl[0:E * R, LB:LB + D], scalar=2.0,
                                     in1=kq_hi[0:E * R, LBM:LBM + D].bitcast(F32), op0=ALU.mult, op1=ALU.subtract)\
               .then_inc(k1_done, 1)

            def xt_low(i, k):
                s, u = 4 * i + k, k % 2
                dve.wait_ge(xt_hi, s + 1)
                dve.tensor_tensor(XT_lo[:, u * P:(u + 1) * P], T0[:, 0:P], XT_hi[:, u * P:(u + 1) * P].bitcast(F32),
                                  ALU.subtract).then_inc(xt_ready, 1)

            def hidden(i, k):
                s, u = 4 * i + k, k % 2
                dve.wait_ge(silu_done, s + 1)
                dve.wait_ge(up_filled, s + 1)
                if k >= 2:
                    dve.wait_ge(ht_filled, s - 1)
                dve.tensor_tensor(HH[:, u, :], SG[:, u, :], ringB[u][:, :], ALU.mult).then_inc(h_done, 1)

            def ht_low(i, k):
                s, u = 4 * i + k, k % 2
                dve.wait_ge(ht_hi, s + 1)
                dve.tensor_tensor(T_lo[:, 1 + u, :], accs[u][:, :], T_hi[:, 1 + u, :].bitcast(F32), ALU.subtract)\
                   .then_inc(ht_ready, 1)

            def results(i, k):
                s, n = 4 * i + k, k % SLOTS
                dve.wait_ge(y_filled, s + 1)
                if k >= SLOTS or not isinstance(i, int):
                    dve.wait_ge(scattered[n], 16 * (i + k // SLOTS))
                dve.tensor_copy(Y[:, n, :], T1[:, 0:D]).then_inc(y_copied, 1)

            def step(i, k):
                if k < ST:
                    hidden(i, k)
                if k >= 2:
                    results(i, k - 2)
                if k + 1 < ST:
                    xt_low(i, k + 1)
                if 1 <= k <= ST:
                    ht_low(i, k - 1)

            xt_low(0, 0)
            for k in range(HEAD):
                step(0, k)
            with dve.Fori(0, LOOPS) as i:
                for u in range(SLOTS):
                    step(i, HEAD + u)
            for k in range(HEAD + SLOTS * LOOPS, ST + 2):
                step(0, k)

            def combine(b):
                dve.wait_ge(expert_in[b], 32)
                for k in range(TOPK):
                    for t in range(b * TB, (b + 1) * TB):
                        ins = dve.scalar_tensor_tensor(out=X[:, t, :], in0=yk[:, k, t, :], scalar=wts[:, k, t:t + 1],
                                                       in1=X[:, t, :], op0=ALU.mult, op1=ALU.add)
                    then(ins)
                norm_stats(2 * B + b)

            def norm3(b):
                if b >= 2:
                    dve.wait_ge(f_filled, T_JOBS.index(("x", b - 2)) + 1)
                norm(2 * B + b, b % 2)

            def low(n):
                kind, b = T_JOBS[n]
                rows_ = {"x": P, "p": SK, "y": P, "z": E * R}[kind]
                dve.wait_ge(f_hi, n + 1)
                dve.tensor_tensor(T_lo[0:rows_, n % 3, :], (T0, T1)[n % 2][0:rows_, :],
                                  T_hi[0:rows_, n % 3, :].bitcast(F32), ALU.subtract).then_inc(f_freed, 1)

            def scores1(b):
                here = slice(b * TB, (b + 1) * TB)
                dve.wait_ge(sc_filled, b + 1)
                then(dve.tensor_tensor(P1[:, here, 0:SK], ringA[b % 2][:, 0:TB * SKP].rearrange("p (t k) -> p t k", k=SKP)[:, :, 0:SK],
                                       spread(kt[:, b * SKP:b * SKP + SK], 1, TB), ALU.add))
                then(dve.tensor_reduce(nm1[:, here], P1[:, here, 0:SK], AX_X, ALU.max, negate=True))
                dve.tensor_scalar(nm1[:, here], nm1[:, here], D ** -0.5, None, ALU.mult).then_inc(negmax1_done, 1)

            def attend1(b):
                here = slice(b * TB, (b + 1) * TB)
                dve.wait_ge(pv1_filled, b + 1)
                then(dve.reciprocal(sum1[:, here], sum1[:, here]))
                for t in range(TB):
                    ins = dve.scalar_tensor_tensor(out=X[:, b * TB + t, :], in0=ringB[b % 2][:, t * D:(t + 1) * D],
                                                   scalar=sum1[:, b * TB + t:b * TB + t + 1], in1=X[:, b * TB + t, :],
                                                   op0=ALU.mult, op1=ALU.add)
                then(ins)
                norm_stats(3 * B + b)

            def norm4(b):
                if b >= 2:
                    dve.wait_ge(f_filled, T_JOBS.index(("y", b - 2)) + 1)
                norm(3 * B + b, b % 2)

            def fused(b, u):
                return (accs, ringA)[b % 2][u][:, 0:2 * FBW].rearrange("p (t j) -> p t j", t=2)

            def softmax(b):
                u = b % 2
                dve.wait_ge(fb_filled, b + 1)
                for n in range(2):
                    ins = dve.tensor_tensor(gl[:, u, 2 * n:2 * n + 2, :], fused(b, n)[:, :, D:D + E],
                                            spread(rw[:, RB1:RB1 + E], 1, 2), ALU.add)
                then(ins)
                then(dve.tensor_reduce(gm[:, :], gl[:, u, :, :], AX_X, ALU.max, negate=True))
                dve.tensor_tensor(gl[:, u, :, :], gl[:, u, :, :], spread(gm[:, :], 2, E), ALU.add).then_inc(gate_in, 1)

            def outer(b):
                u = b % 2
                dve.wait_ge(gate_exp, b + 1)
                then(dve.tensor_reduce(gm[:, :], gl[:, u, :, :], AX_X, ALU.add))
                then(dve.reciprocal(gm[:, :], gm[:, :]))
                then(dve.tensor_tensor(gates[:, :, :], gl[:, u, :, :], spread(gm[:, :], 2, E), ALU.mult))
                for t in range(TB):
                    mid = fused(b, t // 2)[:, t % 2, D + E:D + E + R]
                    ins = dve.tensor_tensor(pairs[:, u, t, :].rearrange("p (e r) -> p e r", r=R), spread(mid, 1, E),
                                            spread(gates[:, t, :], 2, R), ALU.mult)
                ins.then_inc(outer_done, 1)

            def finish(b):
                dve.wait_ge(lora_filled, b + 1)
                dve.wait_ge(pool_x, B + b + 1)
                for n in range(2):
                    here = X[:, b * TB + 2 * n:b * TB + 2 * n + 2, :]
                    ins = dve.tensor_tensor(here, here, fused(b, n)[:, :, 0:D], ALU.add)
                ins.then_inc(result_done, 1)

            todo = {"c": combine, "n": norm3, "s": scores1, "a": attend1, "m": norm4, "g": softmax, "o": outer, "f": finish}
            for what in DVE_END:
                if isinstance(what, int):
                    low(what)
                else:
                    todo[what[0]](int(what[1]))

        @block.tensor
        def _(pe):
            def three(where_, left, right, start=True, stop=True):
                (lh, ll), (rh, rl) = left, right
                pe.matmul(where_, lh, rh, start=start, stop=False, skip_group_check=True)
                pe.matmul(where_, lh, rl, start=False, stop=False, skip_group_check=True)
                return pe.matmul(where_, ll, rh, start=False, stop=stop, skip_group_check=True)

            def packed(a, n):
                return sp_hi[:, a:a + n], sp_lo[:, a:a + n]

            def kept(a, n, rows_=P):
                return kq_hi[0:rows_, a:a + n], kq_lo[0:rows_, a:a + n]

            def t1_free(kind, b):
                if t1(kind, b):
                    pe.wait_ge(t1_freed, t1(kind, b))

            pe.wait_ge(split_done, 1)
            three(T1[:, 0:B * SKP], packed(WK0, D), packed(CTX, B * SKP)).then_inc(t1_filled, 1)
            pe.wait_ge(heads_done, 2)
            pe.wait_ge(t1_freed, 1)
            three(T1[0:H, 0:B * SKP], (bq_hi[:, :], bq_lo[:, :]), (kt_hi[:, :], kt_lo[:, :])).then_inc(t1_filled, 1)

            def fold_keys(b, n):
                h0, nh = GROUPS[n]
                job = a_job("keys", b, n)
                if job >= 2:
                    pe.wait_ge(a_freed, job - 1)
                keys = kt_hi[:, b * SKP:(b + 1) * SKP], kt_lo[:, b * SKP:(b + 1) * SKP]
                for h in range(nh):
                    ins = three(ringA[job % 2][:, h * SKP:(h + 1) * SKP], (qm_hi[:, h0 + h, :], qm_lo[:, h0 + h, :]), keys)
                ins.then_inc(a_filled, 1)

            def turn(kind, b, src):
                n = t0(kind, b)
                if n:
                    pe.wait_ge(t0_freed, n)
                for t in range(TB):
                    ins = pe.transpose(T0[:, t * P:(t + 1) * P], src[:, t, :], ident)
                ins.then_inc(t0_filled, 1)

            def turn_x(b):
                pe.wait_ge(ln_done, b + 1)
                turn("x", b, XN[:, 0, :, :])

            def max_scores(b, n):
                t, (h0, nh) = unit(n)
                job = a_job("max", b, n)
                at = slice(h0 * SK, (h0 + nh) * SK)
                if n == 0:
                    pe.wait_ge(a_hi, 3 * b + 3)
                    pe.wait_ge(t0_hi, t0("x", b) + 1)
                pe.wait_ge(a_freed, job - 1)
                o = ringA[job % 2][:, 0:nh * SK]
                pe.matmul(o, T_hi[:, b % 2, t * P:(t + 1) * P], kq_hi[:, (b % 2) * HK + at.start:(b % 2) * HK + at.stop],
                          start=True, stop=False)
                pe.matmul(o, Z[0:96, b, t * P:(t + 1) * P], sel[0:96, b, at], start=False, stop=True).then_inc(a_filled, 1)

            def turn_shift(b):
                t1_free("shift", b)
                pe.wait_ge(shift_done, b + 1)
                for t in range(TB):
                    ins = pe.transpose(T1[0:2 * H, t * P // 2:(t + 1) * P // 2].bitcast(BF16), shift[:, t, :], ident_bf[:, :])
                ins.then_inc(t1_filled, 1)

            def pair_scores(b, c):
                n, m = NC * b + c, rows_of(c)
                if c == 0:
                    pe.wait_ge(a_freed, a_job("keys", b, 2) + 1)
                    pe.wait_ge(t0_freed, t0("x", b) + 1)
                    pe.wait_ge(t1_freed, t1("shift", b) + 1)
                if n >= 2:
                    pe.wait_ge(exp_done, n - 1)
                at = (b % 2) * HK + CH * c
                o = ringB[n % 2][0:m, :]
                three(o, (kq_hi[:, at:at + m], kq_lo[:, at:at + m]), (T_hi[:, b % 2, :], T_lo[:, b % 2, :]), stop=False)
                pe.matmul(o, sel[:, b, CH * c:CH * c + m], Z[:, b, :], start=False, stop=True,
                          skip_group_check=True).then_inc(b_filled, 1)

            def weigh(b, c):
                n, m = NC * b + c, rows_of(c)
                pe.wait_ge(exp_done, n + 1)
                if c == 0:
                    pe.wait_ge(v_done, B)
                    if b >= 1:
                        pe.wait_ge(o_done, b)
                for t in range(TB):
                    a = (t % 2) * H * OC + first_head(c) * OC
                    ins = pe.matmul(accs[t // 2][:, a:a + 3 * OC], probs[0:m, n % 3, t * P:(t + 1) * P], vblk[0:m, b, c, :],
                                    start=(c == 0 and t % 2 == 0), stop=(c == NC - 1), skip_group_check=True)
                ins.then_inc(pv_done, 1)

            def project(b):
                t1_free("wo", b)
                pe.wait_ge(t0_freed, t0("o", b) + 1)
                for t in range(TB):
                    at = slice(t * P, (t + 1) * P)
                    ins = three(T1[:, at], (T_hi[:, 2, at], T_lo[:, 2, at]), packed(WO0, D))
                ins.then_inc(t1_filled, 1)

            def turn_o(b):
                pe.wait_ge(o_done, b + 1)
                turn("o", b, O)

            def turn_y(b):
                pe.wait_ge(ln_done, B + b + 1)
                turn("y", b, XN[:, 1, :, :])

            def route(b):
                t1_free("logits", b)
                pe.wait_ge(t0_freed, t0("y", b) + 1)
                for t in range(TB):
                    at = slice(t * P, (t + 1) * P)
                    ins = three(T1[:, t * E:(t + 1) * E], (T_hi[:, 2, at], T_lo[:, 2, at]), packed(RT0, E))
                ins.then_inc(t1_filled, 1)

            pe.wait_ge(heads_done, 1)
            for n in range(3):
                fold_keys(0, n)
            turn_x(0)
            for b in range(B):
                pe.wait_ge(ctx3_hi_done, 1)
                pe.wait_ge(ctx3_done, 1)
                if b >= 2:
                    pe.wait_ge(v_done, b - 1)
                for c in range(NC):
                    m, a = CH, CH * c % SK
                    wv = WV0 + first_head(c) * DK
                    ins = three(accs[b % 2][0:m, 3 * DK * c:3 * DK * (c + 1)], (ctx3_hi[:, b, a:a + m], ctx3_lo[:, b, a:a + m]),
                                packed(wv, 3 * DK))
                ins.then_inc(v_filled, 1)
            pe.wait_ge(keep_done, 2)
            t1_free("flags", 0)
            for t in range(TB):
                ins = pe.matmul(T1[:, t * B:(t + 1) * B], keept[:, t * P:(t + 1) * P], padk[:, :], start=True, stop=True)
            ins.then_inc(t1_filled, 1)
            pe.wait_ge(z_done, 1)
            pe.wait_ge(bias_rows_in, 16 * 3 * B)
            for n in range(12):
                max_scores(0, n)
            pe.wait_ge(tab_in, 16)
            turn_shift(0)
            for b in range(B):
                for c in range(NC):
                    pair_scores(b, c)
                    if c == 0 and b + 1 < B:
                        turn_x(b + 1)
                        for n in range(3):
                            fold_keys(b + 1, n)
                    if b + 1 < B:
                        for n in UNITS_AT[c]:
                            max_scores(b + 1, n)
                    if b >= 1 and c == 2:
                        turn_o(b - 1)
                    if c >= 2:
                        weigh(b, c - 2)
                    if b >= 1 and c == 4:
                        project(b - 1)
                    if b >= 1 and c == 8:
                        turn_y(b - 1)
                    if b >= 1 and c == 9:
                        route(b - 1)
                weigh(b, NC - 2)
                weigh(b, NC - 1)
                if b + 1 < B:
                    turn_shift(b + 1)
            turn_o(B - 1)
            project(B - 1)
            turn_y(B - 1)
            route(B - 1)

            pe.wait_ge(t1_freed, len(T1_USES))
            pe.wait_ge(picked, B)
            ones = tab[:, ON:ON + P]
            pe.matmul(T1[:, 0:NT * E], tab[:, UT:UT + P], cnt[:, :, :].rearrange("p t e -> p (t e)"),
                      start=True, stop=False, skip_group_check=True)
            for t in range(NT - 1):
                pe.matmul(T1[:, (t + 1) * E:NT * E].rearrange("p (t e) -> p t e", e=E), ones,
                          spread(cnt[:, t, :], 1, NT - 1 - t), start=False, stop=(t == NT - 2), skip_group_check=True)
            for t in range(NT):
                ins = pe.matmul(T1[:, NT * E:NT * E + E], ones, cnt[:, t, :], start=False, stop=(t == NT - 1),
                                skip_group_check=True)
            ins.then_inc(rank_filled, 1)

            pe.wait_ge(t0_freed, len(T0_USES))
            pe.wait_ge(split_done, 2)
            three(T0[:, 0:B * SKP], packed(WK1, D), packed(CTX, B * SKP)).then_inc(k1_filled, 1)
            for q in range(TOPK * NT):
                pe.wait_ge(onehot_done, q + 2)
                ins = pe.matmul(T1[:, 0:3 * ST].rearrange("p (v i) -> p v i", i=ST), onehot[:, q, :], where[:, :, q, :],
                                start=(q == 0), stop=(q == TOPK * NT - 1))
            ins.then_inc(inverse_filled, 1)

            pe.wait_ge(k1_done, 1)
            three(T0[:, 0:B * SKP], packed(WQ1, D), kept(K1, B * SKP)).then_inc(k1_filled, 1)
            pe.wait_ge(k1_done, 2)
            for b in range(B):
                ctx_b = packed(CTX + b * SKP, SK)
                ins = three(T0[0:SK, b * D:(b + 1) * D], ctx_b, packed(WV1, D))
            ins.then_inc(k1_filled, 1)
            pe.wait_ge(k1_done, 5)
            three(T0[:, 0:B * SKP], (bq1_hi, bq1_lo), kept(K1, B * SKP)).then_inc(k1_filled, 1)

            def turn_tokens(i, k):
                s, n = 4 * i + k, k % SLOTS
                pe.wait_ge(gathered[n], 16 * (i + k // SLOTS + 1))
                if k >= 1:
                    pe.wait_ge(xt_ready, s)
                pe.transpose(T0[:, 0:P], G[:, n, :], ident).then_inc(xt_filled, 1)

            def gate_up(i, k):
                s, u = 4 * i + k, k % 2
                e = pe.value_load(etab[0:1, bass.ds(s, 1)], min_val=0, max_val=E - 1)
                pe.wait_ge(xt_ready, s + 1)
                if k >= 2:
                    pe.wait_ge(h_done, s - 1)
                left = XT_hi[:, u * P:(u + 1) * P], XT_lo[:, u * P:(u + 1) * P]
                for o, w, done in ((ringA[u], 0, gate_filled), (ringB[u], 1, up_filled)):
                    right = [p[w][:, bass.ds(e * FF, FF)] for p in (w_hi, w_lo)]
                    three(o[:, :], left, right).then_inc(done, 1)

            def down(i, k):
                s, u = 4 * i + k, k % 2
                e = pe.value_load(etab[0:1, bass.ds(s, 1)], min_val=0, max_val=E - 1)
                pe.wait_ge(ht_ready, s + 1)
                if k >= 1:
                    pe.wait_ge(y_copied, s)
                for c in range(FC):
                    at = slice(c * P, (c + 1) * P)
                    right = [p[2][:, bass.ds(e * FF + c * P, P)] for p in (w_hi, w_lo)]
                    ins = three(T1[:, 0:D], (T_hi[:, 1 + u, at], T_lo[:, 1 + u, at]), right, start=(c == 0), stop=(c == FC - 1))
                ins.then_inc(y_filled, 1)

            def turn_hidden(i, k):
                s, u = 4 * i + k, k % 2
                pe.wait_ge(h_done, s + 1)
                if k >= 2:
                    pe.wait_ge(ht_ready, s - 1)
                for c in range(FC):
                    ins = pe.transpose(accs[u][:, c * P:(c + 1) * P], HH[:, u, c * P:(c + 1) * P], ident)
                ins.then_inc(ht_filled, 1)

            def step(i, k):
                if k < ST:
                    gate_up(i, k)
                if k >= 2:
                    down(i, k - 2)
                if k + 1 < ST:
                    turn_tokens(i, k + 1)
                if 1 <= k <= ST:
                    turn_hidden(i, k - 1)

            pe.wait_ge(k1_hi, 4)
            pe.wait_ge(k1_done, 6)
            pe.wait_ge(w_lo_done, NW)
            pe.wait_ge(index_done, 1)
            pe.wait_ge(experts_done, 1)
            turn_tokens(0, 0)
            for k in range(HEAD):
                step(0, k)
            with pe.Fori(0, LOOPS) as i:
                for u in range(SLOTS):
                    step(i, HEAD + u)
            for k in range(HEAD + SLOTS * LOOPS, ST + 2):
                step(0, k)

            def part(n):
                kind, b = T_JOBS[n]
                if n >= 2:
                    pe.wait_ge(f_freed, n - 1)
                if kind == "x":
                    pe.wait_ge(ln_done, 2 * B + b + 1)
                elif kind == "p":
                    pe.wait_ge(p1_done, b + 1)
                elif kind == "y":
                    pe.wait_ge(ln_done, 3 * B + b + 1)
                else:
                    pe.wait_ge(outer_done, b + 1)
                for t in range(TB):
                    src = {"x": XN[:, b % 2, t, :], "p": P1[:, b * TB + t, 0:SK], "y": XN[:, b % 2, t, :],
                           "z": pairs[:, b % 2, t, :]}[kind]
                    ins = pe.transpose((T0, T1)[n % 2][0:src.shape[1], t * P:(t + 1) * P], src, ident)
                ins.then_inc(f_filled, 1)

            def parts_of(kind, b, t, rows_=P):
                n = T_JOBS.index((kind, b))
                at = slice(t * P, (t + 1) * P)
                return T_hi[0:rows_, n % 3, at], T_lo[0:rows_, n % 3, at]

            def ready(kind, b):
                pe.wait_ge(f_freed, T_JOBS.index((kind, b)) + 1)

            def scores1(b):
                ready("x", b)
                if b >= 2:
                    pe.wait_ge(negmax1_done, b - 1)
                for t in range(TB):
                    ins = three(ringA[b % 2][:, t * SKP:(t + 1) * SKP], parts_of("x", b, t), kept(A1 + b * SKP, SKP))
                ins.then_inc(sc_filled, 1)

            def values1(b):
                ready("p", b)
                if b >= 2:
                    pe.wait_ge(ln_stats, 3 * B + b - 1)
                for t in range(TB):
                    ins = three(ringB[b % 2][:, t * D:(t + 1) * D], parts_of("p", b, t, SK), kept(V1 + b * D, D, SK))
                ins.then_inc(pv1_filled, 1)

            def fused(b):
                ready("y", b)
                if b >= 2:
                    pe.wait_ge(result_done, b - 1)
                elif b == 1:
                    pe.wait_ge(negmax1_done, B)
                for t in range(TB):
                    bank_ = (accs, ringA)[b % 2][t // 2]
                    ins = three(bank_[:, (t % 2) * FBW:(t % 2 + 1) * FBW], parts_of("y", b, t), packed(FB1, FBW),
                                start=(t % 2 == 0), stop=False)
                ins.then_inc(fb_filled, 1)

            def lora(b):
                ready("z", b)
                for t in range(TB):
                    bank_ = (accs, ringA)[b % 2][t // 2]
                    ins = three(bank_[:, (t % 2) * FBW:(t % 2) * FBW + D], parts_of("z", b, t, E * R), kept(LBM, D, E * R),
                                start=False)
                ins.then_inc(lora_filled, 1)

            todo = {"s": scores1, "v": values1, "b": fused, "l": lora}
            for what in PE_END:
                if isinstance(what, int):
                    part(what)
                else:
                    todo[what[0]](int(what[1]))


def kernel(**inputs):
    import ml_dtypes
    import numpy as np
    import concourse.bacc as bacc
    from concourse.bass_utils import run_bass_kernel_spmd

    v = {k: np.asarray(a) for k, a in inputs.items()}
    f32, bf16 = np.float32, ml_dtypes.bfloat16
    i = np.arange(P)

    def pad(a):
        return np.concatenate([a, np.zeros((P - a.shape[0], a.shape[1]), a.dtype)], 0)

    ctx = np.zeros((D, B, SKP), f32)
    ctx[:, :, 0:SK] = v["ctx_1024"].transpose(2, 0, 1)
    split = np.concatenate([
        v["L0_xattn_Wk"].T, v["L0_xattn_Wv"].T, ctx.reshape(D, B * SKP), v["L0_xattn_Wo"].T, v["L0_ffn_router_w"].T,
        v["L1_xattn_Wq"].T, v["L1_xattn_Wk"], v["L1_xattn_Wv"],
        v["L1_ffn_base_w"].T, v["L1_ffn_router_w"].T, v["L1_ffn_lora_A"]], 1)

    pair = np.arange(HK)
    block = np.zeros((P, NC, 3), f32)
    for c in range(NC):
        r = np.arange(rows_of(c))
        for n in range(3):
            block[r, c, n] = (CH * c + r) // SK == first_head(c) + n
    own_head = (i[:, None] // DK == np.arange(H)[None, :]).astype(f32)
    before = np.broadcast_to((np.arange(E)[None, :] < np.arange(E)[:, None]).astype(f32).reshape(1, E * E), (P, E * E))
    tile_index = np.broadcast_to(np.arange(TOPK * NT, dtype=f32), (P, TOPK * NT))
    falling = np.broadcast_to(E - np.arange(E, dtype=f32), (P, E))
    steps = np.broadcast_to(P * np.arange(16, dtype=f32), (P, 16))
    plain = np.concatenate([
        np.eye(P, dtype=f32), v["L0_xattn_Wq"], own_head,
        v["L0_xattn_bq"][:, None], v["L0_xattn_bk"][:, None], v["L1_xattn_bk"][:, None], v["L1_xattn_bq"][:, None],
        pad(v["L1_ffn_lora_B"].reshape(E * R, D)), block.reshape(P, 3 * NC), before, tile_index,
        i[:, None].astype(f32), (ROWS + i[:, None]).astype(f32), falling, steps,
        (ROWS + P * np.arange(ST)[None, :] + i[:, None]).astype(f32)], 1)
    bv_blocks = np.concatenate([v["L0_xattn_bv"][first_head(c) * DK:(first_head(c) + 3) * DK] for c in range(NC)])
    rows = np.concatenate([v["L0_xattn_bo"], bv_blocks, v["L1_xattn_bv"], v["L1_ffn_base_b"], v["L1_ffn_router_b"]])[None, :]
    tables = np.concatenate([
        i[:, None] < i[None, :], np.ones((P, P)), np.broadcast_to(i[None, :], (P, P)),
        np.broadcast_to(np.arange(ST)[None, :], (P, ST)), np.eye(P)], 1).astype(bf16)
    select = np.zeros((P, HK), bf16)
    select[pair % SK, pair] = 1
    select[96 + pair // SK, pair] = 1
    select[96 + H + pair // SK, pair] = 1

    arrays = {
        "x": v["x"].reshape(TOK, D), "split": split, "plain": plain, "rows": rows, "tables": tables, "select": select,
        "mask_t": v["mask_SxS2_ik0"].T, "pad_t": v["mask_BxS2_if1"].T,
        "w_gate": v["L0_ffn_w_gate"], "w_up": v["L0_ffn_w_up"], "w_down": v["L0_ffn_w_down"],
    }
    arrays = {f"in_{k}": np.ascontiguousarray(a) for k, a in arrays.items()}
    nc = bacc.Bacc("TRN2", target_bir_lowering=False, num_devices=1)
    args = [nc.dram_tensor(k, a.shape, mybir.dt.from_np(a.dtype), kind="ExternalInput").ap() for k, a in arrays.items()]
    out = nc.dram_tensor("out", (TOK, D), F32, kind="ExternalOutput").ap()
    xattn_moe_xattn_lora_kernel(nc, *args, out)
    result = run_bass_kernel_spmd(nc, [arrays], core_ids=[0])
    return result.results[0]["out"].reshape(B, S, D)
```

```python
from contextlib import ExitStack

import concourse.bass as bass
from concourse import mybir

F32 = mybir.dt.float32
F32R = mybir.dt.float32r
BF16 = mybir.dt.bfloat16
I32 = mybir.dt.int32
ALU = mybir.AluOpType
ACT = mybir.ActivationFunctionType
AX_X = mybir.AxisListType.X

P = 128
B, S, D = 4, 512, 128
TB = S // P
NT = B * TB
TOK = B * S
SK, SKP = 77, 78
H = 16
DK = D // H
OC = DK + 1
HK = H * SK
CH = 124
HALF = H // 2
HW = HALF * SK
NH = -(-HW // CH)
GH = 4
UNITS = TB * H // GH
NC = 2 * NH
E, FF = 8, 512
FC = FF // P
TOPK = 2
ST = (TOK * TOPK + E * (P - 1)) // P
ROWS = TOPK * TOK
R = 8
HARD = -1.0e30
EPS = 1e-5
WP = 1024
NW = 3 * E * FF // WP
SLOTS = 4

WKD, WKN, WQD, WV0, NEARLY = 0, 256, 384, 640, 768
CTX, WO0, RT0, WQ1, WK1, WV1, FB1, NSPLIT = 0, 312, 440, 448, 576, 704, 832, 976
BK, BQ, BK1, BQ1C, BV, HM = 128, 131, 133, 134, 135, 136
IDN, LB, BLK, LT8, TIDX, PCOL, WDS, M128, SPARE, NPLAIN = (
    0, 144, 272, 302, 366, 398, 400, 408, 424, 424 + ST)
BO, BV1, BB1, RB1, NROWS = 0, 128, 256, 384, 392
UT, ON, IOP, IOT, IDB, NTAB = 0, 128, 256, 384, 384 + ST, 512 + ST
FBW = D + E + R


def first_head(c):
    return c // NH * HALF + min(c % NH * CH // SK, HALF - 3)


def rows_of(c):
    return min(CH, HW - CH * (c % NH))


def pair_at(c):
    return c // NH * HW + c % NH * CH


T0_USES = [("x", 0), ("x", 1), ("x", 2), ("o", 0), ("x", 3), ("y", 0)] + [(k, b) for b in (1, 2, 3) for k in ("o", "y")]
T1_USES = ([("flags", 0), ("shift", 0), ("shift", 1), ("wo", 0), ("shift", 2), ("logits", 0), ("wo", 1), ("shift", 3)]
           + [("logits", 1), ("wo", 2), ("logits", 2), ("wo", 3), ("logits", 3)])


def t0(kind, b):
    return T0_USES.index((kind, b))


def t1(kind, b):
    return T1_USES.index((kind, b))


def a_job(kind, b, n):
    return (2 + UNITS) * b + (n if kind == "queries" else 2 + n)


T_JOBS = [("x", 0), ("x", 1), ("x", 2), ("x", 3), ("p", 0), ("p", 1), ("p", 2), ("p", 3),
          ("y", 0), ("y", 1), ("y", 2), ("z", 0), ("z", 1), ("y", 3), ("z", 2), ("z", 3)]
PE_END = [0, 1, "s0", 2, "s1", 3, "s2", 4, "s3", 5, "v0", 6, "v1", 7, "v2", 8, "v3", 9, "b0", 10, "b1",
          11, "l0", 12, "l1", "b2", 13, "b3", 14, "l2", 15, "l3"]
ACT_END = [0, 1, 2, "e0", 3, "e1", 4, "e2", 5, "e3", 6, 7, 8, 9, 10, "g0", "g1", 11, 12, 13, "g2", "g3", 14, 15]
DVE_END = ["c0", "c1", "n0", "c2", "n1", 0, "c3", "n2", 1, "s0", "n3", 2, "s1", 3, "s2", 4, "s3", 5, "a0", 6,
           "a1", 7, "m0", "a2", "m1", 8, "a3", "m2", 9, "m3", "g0", "o0", 10, "g1", "o1", 11, 12, "f0", 13, "f1",
           "g2", "o2", "g3", "o3", 14, 15, "f2", "f3"]
HEAD = 7
LOOPS = (ST - 1 - HEAD) // SLOTS

UNITS_AT = [range(0, 0)] + [range(UNITS * n // 8, UNITS * (n + 1) // 8) for n in range(8)] + [range(0, 0)]
LOGITS_AT = {(2, 1): 0, (3, 1): 1, (3, 9): 2}


def spread(ap, axis, n):
    v = ap.unsqueeze(axis)
    return v.broadcast_to([*v.shape[:axis], n, *v.shape[axis + 1:]])


def xattn_moe_xattn_lora_kernel(nc, x, early, split, plain, rows, tables, select, mask_t, pad_t, w_gate, w_up, w_down, out):
    with ExitStack() as stack:
        def sb(name, shape, dt=F32):
            return stack.enter_context(nc.sbuf_tensor("sb_" + name, shape, dt))

        def bank(name):
            return stack.enter_context(nc.psum_tensor("ps_" + name, [P, 512], F32))

        def sem(name):
            return stack.enter_context(nc.semaphore(name))

        normed_d = nc.dram_tensor("normed_rows", [TOK, D], F32).ap()
        expert_d = nc.dram_tensor("expert_rows", [ROWS + ST * P, D], F32).ap()

        gate_up_w = sb("gate_up_w", [P, E * 4 * FF], F32R)
        down_w = sb("down_w", [P, E * FC * 2 * P], F32R)
        work = sb("work", [P, SLOTS * WP])
        X = sb("X", [P, NT, D])
        XN = sb("XN", [P, 2, TB, D])
        T_hi = sb("T_hi", [P, 3, S], F32R)
        T_lo = sb("T_lo", [P, 3, S], F32R)
        kq_hi = sb("kq_hi", [P, 2 * HK], F32R)
        kq_lo = sb("kq_lo", [P, 2 * HW + 160], F32R)
        QA = sb("QA", [P, 2, 2, S], F32R)
        sel = sb("sel", [P, HK], BF16)
        Z = sb("Z", [P, B, S], BF16)
        probs = sb("probs", [P, 3, S])
        vblk = sb("vblk", [P, B, NC, 3 * OC])
        sp2 = sb("sp", [P, 2, NSPLIT], F32R)
        pl = sb("pl", [P, NPLAIN])
        rw = sb("rw", [P, NROWS])
        tab = sb("tab", [P, NTAB], BF16)
        kt = sb("bias1", [P, B * SKP])
        stats = sb("stats", [P, TB, 6])
        mv = sb("mv", [P, 4 * B, TB, 2])
        rstd = sb("rstd", [P, 4 * B, TB])
        power = sb("power", [P, TB])
        negmax = sb("negmax", [P, TB, H])
        shift = sb("shift", [P, TB, 2 * H], BF16)
        O = sb("O", [P, TB, D])
        rsum = sb("rsum", [P, TB, H])
        flags = sb("flags", [P, NT])
        flag2 = sb("flag2", [P, NT])
        padf = sb("padf", [SK, 2, B])
        padk = sb("padk", [SK, B], BF16)
        padi = sb("padi", [SK, B], I32)
        L = sb("L", [P, NT, E])
        L2 = sb("L2", [P, NT, E])
        oh = sb("oh", [P, TOPK, NT, E])
        m12 = sb("m12", [P, TOPK, NT])
        mx = sb("mx", [P, TOPK, NT])
        cnt = sb("cnt", [P, NT, E], BF16)
        wts = sb("wts", [P, TOPK, NT])
        et = sb("et", [P, NT])
        etab = sb("etab", [1, ST], I32)
        gidx = sb("gidx", [P, ST], I32)
        didx = sb("didx", [P, ST], I32)
        L3 = sb("L3", [P, NT, E])
        tiles = sb("tiles", [P, 2, E])
        nm1 = sb("nm1", [P, NT])
        sum1 = sb("sum1", [P, NT])
        gl = sb("gl", [P, 2, TB, E])
        gm = sb("gm", [P, TB])
        gates = sb("gates", [P, TB, E], BF16)

        ident = pl[:, IDN:IDN + P]
        raw = work[:, 0:NEARLY]
        sp = work[:, WP:WP + NSPLIT]
        sp_hi, sp_lo = sp2[:, 0, :], sp2[:, 1, :]
        early_hi, early_lo = down_w[:, 0:NEARLY], down_w[:, NEARLY:2 * NEARLY]
        keys2 = down_w[:, 1600:1600 + 2 * B * SKP].rearrange("p (u b k) -> p u b k", u=2, b=B)
        keys_hi = down_w[:, 2240:2240 + B * SKP].rearrange("p (b k) -> p b k", b=B)
        keys_lo = down_w[:, 2560:2560 + B * SKP].rearrange("p (b k) -> p b k", b=B)
        values3 = [t.rearrange("p t d -> p (t d)").rearrange("p (b k) -> p b k", b=2)[:, :, 0:3 * SK]
                   for t in (O[:, :, :], XN[:, 1, :, :])]
        maskt = probs[0:SK, 0, :].bitcast(I32)
        keept = probs[0:SK, 1, 0:S // 2].bitcast(BF16)
        maskz = probs[0:SK, 2, :]
        onehot = work[:, 0:2048].bitcast(BF16).rearrange("p (q i) -> p q i", i=P)
        where = work[:, 2048:2048 + 48 * ST].bitcast(BF16).rearrange("p (v q i) -> p v q i", v=3, i=ST)
        G = work[:, 0:512].rearrange("p (s d) -> p s d", s=SLOTS)
        SG = work[:, 512:1536].rearrange("p (s f) -> p s f", s=2)
        HH = work[:, 1536:2560].rearrange("p (s f) -> p s f", s=2)
        Y = work[:, 2560:3072].rearrange("p (s d) -> p s d", s=SLOTS)
        XT_hi, XT_lo = T_hi[:, 0, :], T_lo[:, 0, :]
        yk = work[:, 0:TOPK * NT * D].rearrange("p (k t d) -> p k t d", k=TOPK, t=NT)
        P1 = probs[:, :, :].rearrange("p a s -> p (a s)")[:, 0:NT * SKP].rearrange("p (t k) -> p t k", k=SKP)
        scratch = probs[:, :, :].rearrange("p a s -> p (a s)")
        pos = scratch[:, 0:256].rearrange("p (k t e) -> p k t e", k=TOPK, e=E)
        cmp16 = scratch[:, 256:384].rearrange("p (e m) -> p e m", e=E)
        cmp8 = scratch[:, 384:448].rearrange("p (e f) -> p e f", e=E)
        cmpt = scratch[:, 448:448 + ST * E].rearrange("p (i e) -> p i e", e=E)
        inv = scratch[:, 1024:1024 + 4 * ST]
        etf = scratch[:, 1180:1180 + ST]
        sloti = scratch[:, 1220:1316].bitcast(I32).rearrange("p (v k t) -> p v k t", v=3, k=TOPK)
        tile_row = scratch[:, 1316:1380].rearrange("p (v k t) -> p v k t", v=2, k=TOPK)
        slot = scratch[:, 1380:1412].rearrange("p (k t) -> p k t", k=TOPK)
        pairs = vblk[:, 0:2, :, :].rearrange("p b c j -> p (b c j)")[:, 0:2 * TB * E * R].rearrange(
            "p (u t j) -> p u t j", u=2, t=TB)
        K1, A1, V1, LBM, BQ1 = 0, 312, 624, 1136, 1264
        KA = kq_hi[:, :].rearrange("p (b u h k) -> p b u h k", b=2, u=2, k=SK)
        KB = kq_lo[:, 0:2 * HW].rearrange("p (b h k) -> p b h k", b=2, k=SK)
        own = pl[:, HM:HM + HALF]
        ident_bf = tab[:, IDB:IDB + P]
        bq1_hi, bq1_lo = kq_hi[:, BQ1:BQ1 + P], kq_lo[:, BQ1:BQ1 + P]

        def piece_of(i, part):
            which, e = i // 4, 2 * (i % 4)
            if which < 2:
                return gate_up_w[:, :].rearrange("p (e w v f) -> p e w v f", e=E, w=2, v=2)[:, e:e + 2, which, part, :]
            w = down_w[:, :].rearrange("p (g v d) -> p g v d", v=2, d=P)
            return w[:, FC * e:FC * (e + 2), part, :]

        def staged(i):
            slot = (i + 2) % SLOTS
            at = work[:, slot * WP:(slot + 1) * WP]
            return at.rearrange("p (g d) -> p g d", d=FF if i < 8 else P)

        ringA = [bank(f"A{i}") for i in range(2)]
        ringB = [bank(f"B{i}") for i in range(2)]
        accs = [bank(f"acc{i}") for i in range(2)]
        T0, T1 = bank("T0"), bank("T1")

        plain_in, keys_in, ctx_in, queries_in, late_in, rows_in, tab_in = (
            sem(n) for n in ("plain_in", "keys_in", "ctx_in", "queries_in", "late_in", "rows_in", "tab_in"))
        mask_in, sel_in = sem("mask_in"), sem("sel_in")
        x_in = [sem(f"x_in{b}") for b in range(B)]
        w_in = [sem(f"w_in{i}") for i in range(SLOTS)]
        gathered = [sem(f"gathered{i}") for i in range(SLOTS)]
        scattered = [sem(f"scattered{i}") for i in range(SLOTS)]
        expert_in = [sem(f"expert_in{b}") for b in range(B)]
        normed_out, result_out = sem("normed_out"), sem("result_out")
        split_hi, split_done = sem("split_hi"), sem("split_done")
        values_filled, values3_done, experts_done = sem("values_filled"), sem("values3_done"), sem("experts_done")
        keys_filled, keys_hi_done, keys_lo_done, ka_done, kb_done = (
            sem(n) for n in ("keys_filled", "keys_hi_done", "keys_lo_done", "ka_done", "kb_done"))
        t0_filled, t0_hi, t0_freed = sem("t0_filled"), sem("t0_hi"), sem("t0_freed")
        t1_filled, t1_freed = sem("t1_filled"), sem("t1_freed")
        a_filled, a_hi, a_freed = sem("a_filled"), sem("a_hi"), sem("a_freed")
        b_filled, exp_done, pv_done = sem("b_filled"), sem("exp_done"), sem("pv_done")
        v_filled, v_done, o_done = sem("v_filled"), sem("v_done"), sem("o_done")
        keep_done, ones_done, z_done, shift_done = (sem(n) for n in ("keep_done", "ones_done", "z_done", "shift_done"))
        ln_stats, ln_rstd, ln_done = sem("ln_stats"), sem("ln_rstd"), sem("ln_done")
        w_hi_done, w_lo_done = sem("w_hi_done"), sem("w_lo_done")
        dve_step, act_step, pool_step = sem("dve_step"), sem("act_step"), sem("pool_step")
        picked, rank_filled, onehot_done, inverse_filled, index_done = (
            sem(n) for n in ("picked", "rank_filled", "onehot_done", "inverse_filled", "index_done"))
        wexp_done, weights_done = sem("wexp_done"), sem("weights_done")
        gate_filled, up_filled, silu_done, h_done = (sem(n) for n in ("gate_filled", "up_filled", "silu_done", "h_done"))
        ht_filled, ht_hi, ht_ready = sem("ht_filled"), sem("ht_hi"), sem("ht_ready")
        xt_filled, xt_hi, xt_ready = sem("xt_filled"), sem("xt_hi"), sem("xt_ready")
        y_filled, y_copied = sem("y_filled"), sem("y_copied")
        k1_filled, k1_hi, k1_done = sem("k1_filled"), sem("k1_hi"), sem("k1_done")
        f_filled, f_hi, f_freed = sem("f_filled"), sem("f_hi"), sem("f_freed")
        sc_filled, sc_copied, negmax1_done, p1_done = (sem(n) for n in ("sc_filled", "sc_copied", "negmax1_done", "p1_done"))
        pv1_filled, pv1_freed, fb_filled, fb_freed = (sem(n) for n in ("pv1_filled", "pv1_freed", "fb_filled", "fb_freed"))
        gate_in, gate_exp, outer_done, lora_filled, result_done = (
            sem(n) for n in ("gate_in", "gate_exp", "outer_done", "lora_filled", "result_done"))
        pool_x = sem("pool_x")

        block = stack.enter_context(nc.Block())

        @block.sync
        def _(sp_eng):
            xt = x.rearrange("(b t p) d -> b p t d", p=P, t=TB)
            sp_eng.dma_start(raw[:, 0:WQD], early[:, 0:WQD]).then_inc(keys_in, 16)
            sp_eng.dma_start(X[:, 0:TB, :], xt[0]).then_inc(x_in[0], 16)
            sp_eng.dma_start(sp[:, CTX:WO0], split[:, CTX:WO0]).then_inc(ctx_in, 16)
            sp_eng.dma_start(pl[:, :], plain).then_inc(plain_in, 16)
            sp_eng.dma_start(raw[:, WQD:], early[:, WQD:]).then_inc(queries_in, 16)
            sp_eng.dma_start(maskt, mask_t).then_inc(mask_in, 16)
            sp_eng.dma_start(padi[:, :], pad_t).then_inc(mask_in, 16)
            sp_eng.dma_start(sel[:, :], select).then_inc(sel_in, 16)
            sp_eng.dma_start(rw[:, :], rows.broadcast_to([P, NROWS])).then_inc(rows_in, 16)
            sp_eng.dma_start(tab[:, :], tables).then_inc(tab_in, 16)
            for b in range(1, B):
                sp_eng.dma_start(X[:, b * TB:(b + 1) * TB, :], xt[b]).then_inc(x_in[b], 16)
            sp_eng.dma_start(sp[:, WO0:], split[:, WO0:]).then_inc(late_in, 16)

            def piece(i):
                slot, which, e = (i + 2) % SLOTS, i // 4, 2 * (i % 4)
                if i in (2, 3):
                    sp_eng.wait_ge(split_done, 4)
                if i >= SLOTS:
                    sp_eng.wait_ge(w_lo_done, i - SLOTS + 1)
                for n in range(2):
                    at = work[:, slot * WP + n * FF:slot * WP + (n + 1) * FF]
                    if which < 2:
                        src = (w_gate, w_up)[which][e + n]
                    else:
                        src = w_down[e + n].rearrange("(c p) d -> p c d", p=P)
                        at = at.rearrange("p (c d) -> p c d", c=FC)
                    sp_eng.dma_start(at, src).then_inc(w_in[slot], 16)

            nd = normed_d.rearrange("(b t p) d -> b p t d", p=P, t=TB)
            for i in range(SLOTS):
                piece(i)
            for b in range(B):
                for i in range(SLOTS + 3 * b, min(SLOTS + 3 * b + 3, NW)):
                    piece(i)
                if b >= 1:
                    sp_eng.wait_ge(ln_done, B + b)
                    sp_eng.dma_start(nd[b - 1], XN[:, 1, :, :]).then_inc(normed_out, 16)
            sp_eng.wait_ge(ln_done, 2 * B)
            sp_eng.dma_start(nd[B - 1], XN[:, 1, :, :]).then_inc(normed_out, 16)

            for i in range(SLOTS):
                sp_eng.wait_ge(scattered[i], 16 * len(range(i, ST, SLOTS)))
            ed = expert_d[0:ROWS, :].rearrange("(k b t p) d -> k b p t d", k=TOPK, b=B, p=P)
            for b in range(B):
                for k in range(TOPK):
                    sp_eng.dma_start(yk[:, k, b * TB:(b + 1) * TB, :], ed[k, b]).then_inc(expert_in[b], 16)
            ot = out.rearrange("(b t p) d -> b p t d", p=P, t=TB)
            for b in range(B):
                sp_eng.wait_ge(result_done, b + 1)
                sp_eng.dma_start(ot[b], X[:, b * TB:(b + 1) * TB, :]).then_inc(result_out, 16)
            sp_eng.wait_ge(result_out, 16 * B)
            sp_eng.wait_ge(normed_out, 16 * B)

        @block.gpsimd
        def _(pool):
            steps = [0]

            def then(ins):
                steps[0] += 1
                ins.then_inc(pool_step, 1)
                pool.wait_ge(pool_step, steps[0])

            def rstd_of(n):
                pool.wait_ge(ln_stats, n + 1)
                then(pool.tensor_scalar(rstd[:, n, :], mv[:, n, :, 1], EPS, None, ALU.add))
                pool.tensor_tensor(rstd[:, n, :], rstd[:, n, :], power[:, :], ALU.pow).then_inc(ln_rstd, 1)

            then(pool.memset(power[:, :], -0.5))
            pool.memset(Z[64:96, :, :], 1.0).then_inc(ones_done, 1)
            pool.wait_ge(ones_done, 1)
            rstd_of(0)
            def keys_block(b):
                if b == 0:
                    pool.wait_ge(plain_in, 16)
                    pool.wait_ge(keys_lo_done, 1)
                if b >= 2:
                    pool.wait_ge(b_filled, NC * (b - 1))
                pool.tensor_tensor(KB[:, b % 2, :, :], spread(keys_lo[:, b, 0:SK].bitcast(F32), 1, HALF),
                                   spread(own, 2, SK), ALU.mult).then_inc(kb_done, 1)

            keys_block(0)
            for n in range(1, B):
                rstd_of(n)

            def residual(b):
                here = X[:, b * TB:(b + 1) * TB, :]
                pool.wait_ge(ln_done, b + 1)
                if b == 0:
                    pool.wait_ge(rows_in, 16)
                    pool.wait_ge(t1_freed, t1("flags", 0) + 1)
                then(pool.tensor_tensor(here, here, spread(rw[:, BO:BO + D], 1, TB), ALU.add))
                for t in range(b * TB, (b + 1) * TB):
                    ins = pool.tensor_scalar(X[:, t, :], X[:, t, :], flags[:, t:t + 1], None, ALU.add)
                ins.then_inc(pool_x, 1)

            def low_part(i):
                pool.wait_ge(w_hi_done, i + 1)
                pool.tensor_tensor(piece_of(i, 1), staged(i), piece_of(i, 0).bitcast(F32), ALU.subtract)\
                    .then_inc(w_lo_done, 1)

            for b in range(B):
                residual(b)
                if b + 1 < B:
                    keys_block(b + 1)
                low_part(3 * b)
                if b >= 1:
                    rstd_of(B + b - 1)
                low_part(3 * b + 1)
                low_part(3 * b + 2)
            rstd_of(2 * B - 1)

            pool.wait_ge(index_done, 1)
            pool.wait_ge(normed_out, 16 * B)
            def gather(s):
                n = s % SLOTS
                if s >= SLOTS:
                    pool.wait_ge(xt_filled, s - SLOTS + 1)
                pool.indirect_dma_start(
                    out=G[:, n, :], out_offset=None, in_=normed_d,
                    in_offset=bass.IndirectOffsetOnAxis(ap=gidx[:, s:s + 1], axis=0)).then_inc(gathered[n], 16)

            def scatter(s):
                n = s % SLOTS
                pool.wait_ge(y_copied, s + 1)
                pool.indirect_dma_start(
                    out=expert_d, out_offset=bass.IndirectOffsetOnAxis(ap=didx[:, s:s + 1], axis=0),
                    in_=Y[:, n, :], in_offset=None).then_inc(scattered[n], 16)

            for s in range(ST + SLOTS + 2):
                if s < ST:
                    gather(s)
                if s >= SLOTS + 2:
                    scatter(s - SLOTS - 2)

            for n in range(2 * B, 3 * B):
                rstd_of(n)
            def add_bias(b):
                here = X[:, b * TB:(b + 1) * TB, :]
                pool.wait_ge(ln_done, 3 * B + b + 1)
                pool.tensor_tensor(here, here, spread(rw[:, BB1:BB1 + D], 1, TB), ALU.add).then_inc(pool_x, 1)

            for n in range(3 * B, 4 * B):
                rstd_of(n)
                if n >= 3 * B + 2:
                    add_bias(n - 3 * B - 2)
            add_bias(B - 2)
            add_bias(B - 1)

        @block.scalar
        def _(act):
            def first_parts(n, arrived, out, src):
                act.wait_ge(arrived, 16)
                act.activation(out, src, ACT.Copy).then_inc(split_hi, 1)

            first_parts(1, keys_in, early_hi[:, 0:WQD], raw[:, 0:WQD])
            first_parts(2, ctx_in, sp_hi[:, CTX:WO0], sp[:, CTX:WO0])
            first_parts(3, queries_in, early_hi[:, WQD:], raw[:, WQD:])
            act.wait_ge(plain_in, 16)
            for n in range(3):
                act.wait_ge(keys_filled, n + 1)
                out = (keys2[:, 0, :, :], keys2[:, 1, :, :], keys_hi)[n]
                act.activation(out.rearrange("p b k -> p (b k)"), (ringB[0], ringB[1], T1)[n][:, 0:B * SKP], ACT.Identity,
                               bias=pl[:, BK + n:BK + n + 1]).then_inc(keys_hi_done, 1)

            def turned_hi(kind, b):
                n = t0(kind, b)
                act.wait_ge(t0_filled, n + 1)
                act.activation(T_hi[:, 0 if kind == "x" else 2, :], T0[:, :], ACT.Copy).then_inc(t0_hi, 1)

            def queries_hi(b):
                for n in range(2):
                    job = a_job("queries", b, n)
                    act.wait_ge(a_filled, job + 1)
                    act.activation(QA[:, b % 2, n, :], ringA[job % 2][:, :], ACT.Identity,
                                   bias=pl[:, BQ + n:BQ + n + 1]).then_inc(a_hi, 1)

            def shift_in(b):
                act.wait_ge(t1_filled, t1("shift", b) + 1)
                act.activation(Z[96:96 + 2 * H, b, :], T1[0:2 * H, 0:S // 2].bitcast(BF16), ACT.Copy).then_inc(t1_freed, 1)

            def exps(b, c):
                n = NC * b + c
                act.wait_ge(b_filled, n + 1)
                if n >= 3:
                    act.wait_ge(pv_done, n - 2)
                act.activation(probs[0:rows_of(c), n % 3, :], ringB[n % 2][0:rows_of(c), :], ACT.Exp,
                               scale=DK ** -0.5).then_inc(exp_done, 1)

            def high_part(i):
                slot = (i + 2) % SLOTS
                act.wait_ge(w_in[slot], 32 * (i // SLOTS + 1))
                if i == 8:
                    act.wait_ge(a_filled, a_job("queries", B - 1, 1) + 1)
                    act.wait_ge(ka_done, 2 * B)
                    act.wait_ge(kb_done, B)
                act.activation(piece_of(i, 0), staged(i), ACT.Copy).then_inc(w_hi_done, 1)

            turned_hi("x", 0)
            queries_hi(0)
            act.wait_ge(values_filled, 1)
            for n in range(2):
                here = ringB[1][:, 2 * n * SKP:2 * (n + 1) * SKP].rearrange("p (b k) -> p b k", k=SKP)[:, :, 0:SK]
                act.activation(values3[n].rearrange("p b (r k) -> p b r k", r=3), spread(here, 2, 3), ACT.Identity,
                               bias=pl[:, BV:BV + 1]).then_inc(values3_done, 1)
            turned_hi("x", 1)
            shift_in(0)
            for b in range(B):
                for c in range(NC):
                    exps(b, c)
                    if c == 0 and b + 1 < B:
                        queries_hi(b + 1)
                        if b == 0:
                            first_parts(4, late_in, sp_hi[:, WO0:], sp[:, WO0:])
                    if c == 2 and b >= 1:
                        turned_hi("o", b - 1)
                    if c == 6 and b + 2 < B:
                        turned_hi("x", b + 2)
                    if c == 8 and b >= 1:
                        turned_hi("y", b - 1)
                    if c in (1, 4, 7):
                        high_part(3 * b + c // 3)
                if b + 1 < B:
                    shift_in(b + 1)
            turned_hi("o", B - 1)
            turned_hi("y", B - 1)

            act.wait_ge(picked, 2)
            act.activation(et[:, :], et[:, :], ACT.Exp).then_inc(wexp_done, 1)

            act.wait_ge(k1_filled, 1)
            act.activation(kq_hi[:, K1:K1 + B * SKP], T0[:, 0:B * SKP], ACT.Identity,
                           bias=pl[:, BK1:BK1 + 1]).then_inc(k1_hi, 1)
            act.wait_ge(k1_filled, 2)
            act.activation(kq_hi[:, A1:A1 + B * SKP], T0[:, 0:B * SKP], ACT.Copy).then_inc(k1_hi, 1)
            act.wait_ge(k1_done, 3)
            act.activation(kq_hi[0:SK, V1:V1 + B * D], O[0:SK, :, :].rearrange("p t d -> p (t d)"), ACT.Copy)\
               .then_inc(k1_hi, 1)
            act.wait_ge(k1_filled, 4)
            act.activation(kt[:, :], T0[:, 0:B * SKP], ACT.Copy).then_inc(k1_hi, 1)

            def xt_high(i, k):
                s, u = 4 * i + k, k % 2
                act.wait_ge(xt_filled, s + 1)
                if k >= 2:
                    act.wait_ge(up_filled, s - 1)
                act.activation(XT_hi[:, u * P:(u + 1) * P], T0[:, 0:P], ACT.Copy).then_inc(xt_hi, 1)

            def silu(i, k):
                s, u = 4 * i + k, k % 2
                act.wait_ge(gate_filled, s + 1)
                if k >= 2:
                    act.wait_ge(h_done, s - 1)
                act.activation(SG[:, u, :], ringA[u][:, :], ACT.Silu).then_inc(silu_done, 1)

            def ht_high(i, k):
                s, u = 4 * i + k, k % 2
                act.wait_ge(ht_filled, s + 1)
                if k >= 2:
                    act.wait_ge(y_filled, s - 1)
                act.activation(T_hi[:, 1 + u, :], accs[u][:, :], ACT.Copy).then_inc(ht_hi, 1)

            def step(i, k):
                if 1 <= k <= ST:
                    ht_high(i, k - 1)
                if k < ST:
                    silu(i, k)
                if k + 1 < ST:
                    xt_high(i, k + 1)

            xt_high(0, 0)
            for k in range(HEAD):
                step(0, k)
            with act.Fori(0, LOOPS) as i:
                for u in range(SLOTS):
                    step(i, HEAD + u)
            for k in range(HEAD + SLOTS * LOOPS, ST + 2):
                step(0, k)

            def part(n):
                kind, b = T_JOBS[n]
                rows_ = {"x": P, "p": SK, "y": P, "z": E * R}[kind]
                act.wait_ge(f_filled, n + 1)
                act.activation(T_hi[0:rows_, n % 3, :], (T0, T1)[n % 2][0:rows_, :], ACT.Copy).then_inc(f_hi, 1)

            def exp1(b):
                act.wait_ge(negmax1_done, b + 1)
                for t in range(b * TB, (b + 1) * TB):
                    ins = act.activation(P1[:, t, 0:SK], P1[:, t, 0:SK], ACT.Exp, bias=nm1[:, t:t + 1],
                                         scale=D ** -0.5, accum_out=sum1[:, t:t + 1])
                ins.then_inc(p1_done, 1)

            def gate_exps(b):
                act.wait_ge(gate_in, b + 1)
                act.activation(gl[:, b % 2, :, :], gl[:, b % 2, :, :], ACT.Exp).then_inc(gate_exp, 1)

            for what in ACT_END:
                if isinstance(what, int):
                    part(what)
                elif what[0] == "e":
                    exp1(int(what[1]))
                else:
                    gate_exps(int(what[1]))

        @block.vector
        def _(dve):
            steps = [0]

            def then(ins):
                steps[0] += 1
                ins.then_inc(dve_step, 1)
                dve.wait_ge(dve_step, steps[0])

            def norm_stats(n):
                b = n % B
                if n:
                    dve.wait_ge(ln_stats, n)
                for t in range(TB):
                    ins = dve.bn_stats(stats[:, t, :], X[:, b * TB + t, :])
                then(ins)
                for t in range(TB):
                    ins = dve.bn_aggr(mv[:, n, t, :], stats[:, t, :])
                ins.then_inc(ln_stats, 1)

            def norm(n, slot):
                b = n % B
                dve.wait_ge(ln_rstd, n + 1)
                for t in range(TB):
                    ins = dve.tensor_scalar(XN[:, slot, t, :], X[:, b * TB + t, :], mv[:, n, t, 0:1],
                                            rstd[:, n, t:t + 1], ALU.subtract, ALU.mult)
                ins.then_inc(ln_done, 1)

            dve.wait_ge(x_in[0], 16)
            norm_stats(0)
            def second_parts(n, out, src, high):
                dve.wait_ge(split_hi, n)
                dve.tensor_tensor(out, src, high.bitcast(F32), ALU.subtract).then_inc(split_done, 1)

            def keys_half(b, n):
                if b >= 2:
                    dve.wait_ge(b_filled, NC * (b - 2) + NH * (n + 1))
                if b == 0:
                    dve.wait_ge(keys_hi_done, n + 1)
                dve.tensor_tensor(KA[:, b % 2, n, :, :], spread(keys2[:, n, b, 0:SK].bitcast(F32), 1, HALF),
                                  spread(own, 2, SK), ALU.mult).then_inc(ka_done, 1)

            second_parts(1, early_lo[:, 0:WQD], raw[:, 0:WQD], early_hi[:, 0:WQD])
            second_parts(2, sp_lo[:, CTX:WO0], sp[:, CTX:WO0], sp_hi[:, CTX:WO0])
            norm(0, 0)
            second_parts(3, early_lo[:, WQD:], raw[:, WQD:], early_hi[:, WQD:])
            dve.wait_ge(keys_hi_done, 3)
            dve.scalar_tensor_tensor(out=keys_lo.rearrange("p b k -> p (b k)"), in0=T1[:, 0:B * SKP],
                                     scalar=pl[:, BK + 2:BK + 3], in1=keys_hi.rearrange("p b k -> p (b k)").bitcast(F32),
                                     op0=ALU.add, op1=ALU.subtract).then_inc(keys_lo_done, 1)
            def turned_lo(kind, b):
                n = t0(kind, b)
                u = 0 if kind == "x" else 2
                dve.wait_ge(t0_hi, n + 1)
                dve.tensor_tensor(T_lo[:, u, :], T0[:, :], T_hi[:, u, :].bitcast(F32), ALU.subtract).then_inc(t0_freed, 1)

            keys_half(0, 0)
            keys_half(0, 1)
            turned_lo("x", 0)
            dve.wait_ge(mask_in, 32)
            dve.tensor_scalar(keept, maskt, 0, None, ALU.not_equal).then_inc(keep_done, 1)
            dve.tensor_scalar(padk[:, :], padi[:, :], 0, None, ALU.not_equal).then_inc(keep_done, 1)
            dve.tensor_scalar(maskz, maskt, 0, HARD, ALU.is_equal, ALU.mult)
            then(dve.tensor_scalar(padf[:, 0, :], padi[:, :], 0, HARD, ALU.is_equal, ALU.mult))
            dve.wait_ge(ones_done, 1)
            for b in range(B):
                ins = dve.tensor_scalar(Z[0:SK, b, :], maskz, padf[:, 0, b:b + 1], None, ALU.add)
            ins.then_inc(z_done, 1)

            def queries_lo(b):
                for n in range(2):
                    job = a_job("queries", b, n)
                    rows_ = slice(P // 2 * (1 - n), P // 2 * (2 - n))
                    dve.wait_ge(a_hi, 2 * b + n + 1)
                    dve.scalar_tensor_tensor(out=QA[rows_, b % 2, n, :], in0=ringA[job % 2][rows_, :],
                                             scalar=pl[rows_, BQ + n:BQ + n + 1], in1=QA[rows_, b % 2, n, :].bitcast(F32),
                                             op0=ALU.add, op1=ALU.subtract).then_inc(a_freed, 1)

            def row_max(b, n):
                t, h0 = n // (H // GH), n % (H // GH) * GH
                job = a_job("max", b, n)
                dve.wait_ge(a_filled, job + 1)
                dve.tensor_reduce(negmax[:, t, h0:h0 + GH], ringA[job % 2][:, 0:GH * SK].rearrange("p (h k) -> p h k", k=SK),
                                  AX_X, ALU.max, negate=True).then_inc(a_freed, 1)

            def shift_out(b):
                dve.wait_ge(a_freed, a_job("max", b, UNITS - 1) + 1)
                if b >= 1:
                    dve.wait_ge(t1_filled, t1("shift", b - 1) + 1)
                then(dve.tensor_copy(shift[:, :, 0:H], negmax[:, :, :]))
                dve.tensor_tensor(shift[:, :, H:2 * H], negmax[:, :, :], shift[:, :, 0:H], ALU.subtract).then_inc(shift_done, 1)

            def values(b):
                dve.wait_ge(v_filled, b + 1)
                block_mask = pl[0:CH, BLK:BLK + 3 * NC].rearrange("p (u c h) -> p u c h", u=2, h=3)
                for c in range(NH):
                    src = accs[b % 2][0:CH, c * D:(c + 1) * D] if c < NH - 1 else ringB[0][0:CH, b * D:(b + 1) * D]
                    h = first_head(c)
                    for u in range(2):
                        dve.tensor_tensor(vblk[0:CH, b, u * NH + c, :].rearrange("p (h j) -> p h j", j=OC)[:, :, 0:DK],
                                          src.rearrange("p (h j) -> p h j", j=DK)[:, u * HALF + h:u * HALF + h + 3, :],
                                          spread(block_mask[:, u, c, :], 2, DK), ALU.mult)
                dve.tensor_copy(vblk[0:CH, b, :, :].rearrange("p c (h j) -> p (c h) j", j=OC)[:, :, DK],
                                pl[0:CH, BLK:BLK + 3 * NC]).then_inc(v_done, 1)

            queries_lo(0)
            dve.wait_ge(t1_filled, t1("flags", 0) + 1)
            then(dve.tensor_scalar(flags[:, :].rearrange("p (b t) -> p t b", t=TB),
                                   T1[:, 0:NT].rearrange("p (t b) -> p t b", b=B), 0.0, 3e38, ALU.is_equal, ALU.mult))
            then(dve.tensor_scalar(flag2[:, :], flags[:, :], 1e10, None, ALU.mult))
            dve.tensor_tensor(flags[:, :], flag2[:, :], flag2[:, :], ALU.subtract).then_inc(t1_freed, 1)
            for n in range(UNITS):
                row_max(0, n)
                if n % (UNITS // B) == UNITS // B - 1:
                    values(n // (UNITS // B))
                if n == 1:
                    dve.wait_ge(x_in[1], 16)
                    norm_stats(1)
                if n == 5:
                    dve.wait_ge(t0_filled, t0("x", 0) + 1)
                    norm(1, 0)
                if n == 9:
                    turned_lo("x", 1)
                if n == 13:
                    keys_half(1, 0)
            shift_out(0)
            keys_half(1, 1)

            def context(b):
                dve.wait_ge(pv_done, NC * (b + 1))
                halves = [accs[u][:, 0:2 * H * OC].rearrange("p (t h j) -> p t h j", t=2, j=OC) for u in range(2)]
                dve.reciprocal(rsum[:, 0:2, :], halves[0][:, :, :, DK])
                then(dve.reciprocal(rsum[:, 2:4, :], halves[1][:, :, :, DK]))
                if b >= 1:
                    dve.wait_ge(t0_filled, t0("o", b - 1) + 1)
                for t in range(TB):
                    ins = dve.tensor_tensor(O[:, t, :].rearrange("p (h j) -> p h j", j=DK), halves[t // 2][:, t % 2, :, 0:DK],
                                            spread(rsum[:, t, :], 2, DK), ALU.mult)
                ins.then_inc(o_done, 1)

            def add_attention(b):
                here = X[:, b * TB:(b + 1) * TB, :]
                dve.wait_ge(t1_filled, t1("wo", b) + 1)
                dve.wait_ge(pool_x, b + 1)
                dve.tensor_tensor(here, here, T1[:, :].rearrange("p (t d) -> p t d", t=TB), ALU.add).then_inc(t1_freed, 1)
                dve.wait_ge(t1_freed, t1("wo", b) + 1)
                norm_stats(B + b)

            def norm_for_experts(b):
                if b >= 1:
                    dve.wait_ge(normed_out, 16 * b)
                norm(B + b, 1)

            def take_logits(b):
                dve.wait_ge(t1_filled, t1("logits", b) + 1)
                dve.tensor_reduce(L[:, b * TB:(b + 1) * TB, :], T1[:, 0:TB * 2 * E].rearrange("p (t v e) -> p t e v", v=2, e=E),
                                  AX_X, ALU.add).then_inc(t1_freed, 1)

            def pick():
                falling = spread(pl[:, WDS:WDS + E], 1, NT)
                dve.wait_ge(t1_freed, len(T1_USES))
                for k in range(TOPK):
                    src = (L, L2)[k][:, :, :]
                    then(dve.tensor_reduce(m12[:, k, :], src, AX_X, ALU.max))
                    then(dve.tensor_tensor(L3[:, :, :], src, spread(m12[:, k, :], 2, E), ALU.is_equal))
                    then(dve.tensor_tensor(L3[:, :, :], L3[:, :, :], falling, ALU.mult))
                    then(dve.tensor_reduce(mx[:, k, :], L3[:, :, :], AX_X, ALU.max))
                    then(dve.tensor_tensor(oh[:, k, :, :], falling, spread(mx[:, k, :], 2, E), ALU.is_equal))
                    if k == 0:
                        then(dve.scalar_tensor_tensor(out=L2[:, :, :], in0=oh[:, 0, :, :], scalar=HARD, in1=L[:, :, :],
                                                      op0=ALU.mult, op1=ALU.add))
                dve.tensor_tensor(cnt[:, :, :], oh[:, 0, :, :], oh[:, 1, :, :], ALU.add).then_inc(picked, 1)
                dve.tensor_tensor(et[:, :], m12[:, 1, :], m12[:, 0, :], ALU.subtract).then_inc(picked, 1)

            for b in range(B):
                for c in range(NC):
                    if c == 0:
                        if b >= 1:
                            context(b - 1)
                        if b + 1 < B:
                            if b >= 1:
                                keys_half(b + 1, 1)
                            queries_lo(b + 1)
                    if b + 1 < B:
                        for n in UNITS_AT[c]:
                            row_max(b + 1, n)
                    if b == 0 and c == 2:
                        second_parts(4, sp_lo[:, WO0:], sp[:, WO0:], sp_hi[:, WO0:])
                    if b == 0 and c in (1, 5):
                        n = 2 + c // 5
                        dve.wait_ge(x_in[n], 16)
                        norm_stats(n)
                    if (b, c - 1) in LOGITS_AT:
                        take_logits(LOGITS_AT[b, c - 1])
                    if b >= 1 and c == 3:
                        turned_lo("o", b - 1)
                    if c == 4 and b + 2 < B:
                        norm(b + 2, 0)
                    if b >= 1 and c == 5:
                        add_attention(b - 1)
                    if c == 6 and b + 2 < B:
                        keys_half(b + 2, 0)
                    if c == 7:
                        if b + 2 < B:
                            turned_lo("x", b + 2)
                        if b >= 1:
                            norm_for_experts(b - 1)
                    if c == 9:
                        if b + 1 < B:
                            shift_out(b + 1)
                        if b >= 1:
                            turned_lo("y", b - 1)
            take_logits(B - 2)
            context(B - 1)
            turned_lo("o", B - 1)
            add_attention(B - 1)
            norm_for_experts(B - 1)
            turned_lo("y", B - 1)
            take_logits(B - 1)
            pick()

            dve.wait_ge(tab_in, 16)
            dve.wait_ge(rank_filled, 1)
            rank = T1[:, 0:NT * E].rearrange("p (t e) -> p t e", e=E)
            total = T1[:, NT * E:NT * E + E]
            then(dve.tensor_tensor(cmp16[:, :, :], spread(total, 2, 16), spread(pl[:, M128:M128 + 16], 1, E), ALU.is_gt))
            then(dve.tensor_reduce(tiles[:, 0, :], cmp16[:, :, :], AX_X, ALU.add))
            then(dve.tensor_tensor(cmp8[:, :, :], spread(tiles[:, 0, :], 1, E),
                                   pl[:, LT8:LT8 + E * E].rearrange("p (e f) -> p e f", f=E), ALU.mult))
            then(dve.tensor_reduce(tiles[:, 1, :], cmp8[:, :, :], AX_X, ALU.add))
            then(dve.scalar_tensor_tensor(out=pos[:, 0, :, :], in0=spread(tiles[:, 1, :], 1, NT), scalar=float(P),
                                          in1=rank, op0=ALU.mult, op1=ALU.add))
            then(dve.tensor_tensor(pos[:, 1, :, :], pos[:, 0, :, :], oh[:, 1, :, :], ALU.mult))
            then(dve.tensor_tensor(pos[:, 0, :, :], pos[:, 0, :, :], oh[:, 0, :, :], ALU.mult))
            then(dve.tensor_reduce(slot[:, :, :], pos[:, :, :, :], AX_X, ALU.add))
            then(dve.tensor_scalar(mx[:, :, :], mx[:, :, :], 0.0, float(P * P), ALU.is_equal, ALU.mult))
            then(dve.tensor_tensor(sloti[:, 0, :, :], slot[:, :, :], mx[:, :, :], ALU.add))
            dve.tensor_scalar(sloti[:, 1, :, :], sloti[:, 0, :, :], 7, None, ALU.logical_shift_right)
            then(dve.tensor_scalar(sloti[:, 2, :, :], sloti[:, 0, :, :], P - 1, None, ALU.bitwise_and))
            then(dve.tensor_copy(tile_row[:, :, :, :], sloti[:, 1:3, :, :]))
            row_of = tile_row[:, 1, :, :].rearrange("p k t -> p (k t)")
            tile_of = tile_row[:, 0, :, :].rearrange("p k t -> p (k t)")
            then(dve.tensor_tensor(where[:, 2, :, :], spread(tab[:, IOT:IOT + ST], 1, TOPK * NT),
                                   spread(tile_of, 2, ST), ALU.is_equal))
            dve.tensor_tensor(where[:, 0, :, :], where[:, 2, :, :], spread(pl[:, TIDX:TIDX + TOPK * NT], 2, ST), ALU.mult)
            dve.tensor_scalar(where[:, 1, :, :], where[:, 2, :, :], pl[:, PCOL:PCOL + 1], None, ALU.mult)\
               .then_inc(onehot_done, 1)
            for q in range(TOPK * NT):
                dve.tensor_scalar(onehot[:, q, :], tab[:, IOP:IOP + P], row_of[:, q:q + 1], None, ALU.is_equal)\
                   .then_inc(onehot_done, 1)
            then(dve.tensor_tensor(tiles[:, 0, :], tiles[:, 0, :], tiles[:, 1, :], ALU.add))
            then(dve.tensor_tensor(cmpt[0:1, :, :], spread(tiles[0:1, 0, :], 1, ST), spread(tab[0:1, IOT:IOT + ST], 2, E),
                                   ALU.is_le))
            then(dve.tensor_reduce(etf[0:1, :], cmpt[0:1, :, :], AX_X, ALU.add))
            dve.tensor_scalar(etab[0:1, :], etf[0:1, :], float(E - 1), None, ALU.min).then_inc(experts_done, 1)
            dve.wait_ge(inverse_filled, 1)
            then(dve.tensor_copy(inv[:, 0:3 * ST], T1[:, 0:3 * ST]))
            spare = pl[:, SPARE:SPARE + ST]
            dve.tensor_tensor(inv[:, 3 * ST:4 * ST], inv[:, 2 * ST:3 * ST], spare, ALU.mult)
            then(dve.scalar_tensor_tensor(out=inv[:, 0:ST], in0=inv[:, 0:ST], scalar=float(P), in1=inv[:, ST:2 * ST],
                                          op0=ALU.mult, op1=ALU.add))
            then(dve.tensor_copy(gidx[:, :], inv[:, 0:ST]))
            then(dve.tensor_tensor(inv[:, ST:2 * ST], spare, inv[:, 3 * ST:4 * ST], ALU.subtract))
            dve.tensor_tensor(didx[:, :], inv[:, 0:ST], inv[:, ST:2 * ST], ALU.add)
            dve.tensor_scalar(gidx[:, :], gidx[:, :], TOK - 1, None, ALU.bitwise_and).then_inc(index_done, 1)

            dve.wait_ge(wexp_done, 1)
            then(dve.tensor_scalar(wts[:, 0, :], et[:, :], 1.0, None, ALU.add))
            then(dve.reciprocal(wts[:, 0, :], wts[:, 0, :]))
            then(dve.tensor_tensor(wts[:, 1, :], et[:, :], wts[:, 0, :], ALU.mult))

            dve.wait_ge(k1_hi, 1)
            dve.scalar_tensor_tensor(out=kq_lo[:, K1:K1 + B * SKP], in0=T0[:, 0:B * SKP], scalar=pl[:, BK1:BK1 + 1],
                                     in1=kq_hi[:, K1:K1 + B * SKP].bitcast(F32), op0=ALU.add, op1=ALU.subtract)\
               .then_inc(k1_done, 1)
            dve.wait_ge(k1_hi, 2)
            dve.tensor_tensor(kq_lo[:, A1:A1 + B * SKP], T0[:, 0:B * SKP], kq_hi[:, A1:A1 + B * SKP].bitcast(F32),
                              ALU.subtract).then_inc(k1_done, 1)
            dve.wait_ge(k1_filled, 3)
            v1 = O[0:SK, :, :]
            dve.tensor_tensor(v1, T0[0:SK, :].rearrange("p (b d) -> p b d", d=D), spread(rw[0:SK, BV1:BV1 + D], 1, B),
                              ALU.add).then_inc(k1_done, 1)
            dve.wait_ge(k1_hi, 3)
            dve.tensor_tensor(kq_lo[0:SK, V1:V1 + B * D], v1.rearrange("p t d -> p (t d)"),
                              kq_hi[0:SK, V1:V1 + B * D].bitcast(F32), ALU.subtract).then_inc(k1_done, 1)
            then(dve.tensor_scalar(bq1_hi, ident, 0.0, pl[:, BQ1C:BQ1C + 1], ALU.mult, ALU.add))
            dve.tensor_scalar(bq1_lo, bq1_hi.bitcast(F32), -1.0, pl[:, BQ1C:BQ1C + 1], ALU.mult, ALU.add).then_inc(k1_done, 1)
            then(dve.tensor_scalar(kq_hi[0:E * R, LBM:LBM + D], pl[0:E * R, LB:LB + D], 2.0, None, ALU.mult))
            dve.scalar_tensor_tensor(out=kq_lo[0:E * R, LBM:LBM + D], in0=pl[0:E * R, LB:LB + D], scalar=2.0,
                                     in1=kq_hi[0:E * R, LBM:LBM + D].bitcast(F32), op0=ALU.mult, op1=ALU.subtract)\
               .then_inc(k1_done, 1)

            def xt_low(i, k):
                s, u = 4 * i + k, k % 2
                dve.wait_ge(xt_hi, s + 1)
                dve.tensor_tensor(XT_lo[:, u * P:(u + 1) * P], T0[:, 0:P], XT_hi[:, u * P:(u + 1) * P].bitcast(F32),
                                  ALU.subtract).then_inc(xt_ready, 1)

            def hidden(i, k):
                s, u = 4 * i + k, k % 2
                dve.wait_ge(silu_done, s + 1)
                dve.wait_ge(up_filled, s + 1)
                if k >= 2:
                    dve.wait_ge(ht_filled, s - 1)
                dve.tensor_tensor(HH[:, u, :], SG[:, u, :], ringB[u][:, :], ALU.mult).then_inc(h_done, 1)

            def ht_low(i, k):
                s, u = 4 * i + k, k % 2
                dve.wait_ge(ht_hi, s + 1)
                dve.tensor_tensor(T_lo[:, 1 + u, :], accs[u][:, :], T_hi[:, 1 + u, :].bitcast(F32), ALU.subtract)\
                   .then_inc(ht_ready, 1)

            def results(i, k):
                s, n = 4 * i + k, k % SLOTS
                dve.wait_ge(y_filled, s + 1)
                if k >= SLOTS or not isinstance(i, int):
                    dve.wait_ge(scattered[n], 16 * (i + k // SLOTS))
                dve.tensor_reduce(Y[:, n, :], T1[:, 0:2 * D].rearrange("p (v d) -> p d v", v=2), AX_X, ALU.add)\
                   .then_inc(y_copied, 1)

            def step(i, k):
                if k >= 3:
                    results(i, k - 3)
                if 1 <= k <= ST:
                    ht_low(i, k - 1)
                if k < ST:
                    hidden(i, k)
                if k + 1 < ST:
                    xt_low(i, k + 1)

            xt_low(0, 0)
            for k in range(HEAD):
                step(0, k)
            with dve.Fori(0, LOOPS) as i:
                for u in range(SLOTS):
                    step(i, HEAD + u)
            for k in range(HEAD + SLOTS * LOOPS, ST + 3):
                step(0, k)

            def combine(b):
                dve.wait_ge(expert_in[b], 32)
                for k in range(TOPK):
                    for t in range(b * TB, (b + 1) * TB):
                        ins = dve.scalar_tensor_tensor(out=X[:, t, :], in0=yk[:, k, t, :], scalar=wts[:, k, t:t + 1],
                                                       in1=X[:, t, :], op0=ALU.mult, op1=ALU.add)
                    then(ins)
                norm_stats(2 * B + b)

            def norm3(b):
                if b >= 2:
                    dve.wait_ge(f_filled, T_JOBS.index(("x", b - 2)) + 1)
                norm(2 * B + b, b % 2)

            def low(n):
                kind, b = T_JOBS[n]
                rows_ = {"x": P, "p": SK, "y": P, "z": E * R}[kind]
                dve.wait_ge(f_hi, n + 1)
                dve.tensor_tensor(T_lo[0:rows_, n % 3, :], (T0, T1)[n % 2][0:rows_, :],
                                  T_hi[0:rows_, n % 3, :].bitcast(F32), ALU.subtract).then_inc(f_freed, 1)

            def scores1(b):
                here = slice(b * TB, (b + 1) * TB)
                dve.wait_ge(sc_filled, b + 1)
                then(dve.tensor_tensor(P1[:, here, 0:SK], ringA[b % 2][:, 0:TB * SKP].rearrange("p (t k) -> p t k", k=SKP)[:, :, 0:SK],
                                       spread(kt[:, b * SKP:b * SKP + SK], 1, TB), ALU.add))
                then(dve.tensor_reduce(nm1[:, here], P1[:, here, 0:SK], AX_X, ALU.max, negate=True))
                dve.tensor_scalar(nm1[:, here], nm1[:, here], D ** -0.5, None, ALU.mult).then_inc(negmax1_done, 1)

            def attend1(b):
                here = slice(b * TB, (b + 1) * TB)
                dve.wait_ge(pv1_filled, b + 1)
                then(dve.reciprocal(sum1[:, here], sum1[:, here]))
                for t in range(TB):
                    ins = dve.scalar_tensor_tensor(out=X[:, b * TB + t, :], in0=ringB[b % 2][:, t * D:(t + 1) * D],
                                                   scalar=sum1[:, b * TB + t:b * TB + t + 1], in1=X[:, b * TB + t, :],
                                                   op0=ALU.mult, op1=ALU.add)
                then(ins)
                norm_stats(3 * B + b)

            def norm4(b):
                if b >= 2:
                    dve.wait_ge(f_filled, T_JOBS.index(("y", b - 2)) + 1)
                norm(3 * B + b, b % 2)

            def fused(b, u):
                return (accs, ringA)[b % 2][u][:, 0:2 * FBW].rearrange("p (t j) -> p t j", t=2)

            def softmax(b):
                u = b % 2
                dve.wait_ge(fb_filled, b + 1)
                for n in range(2):
                    ins = dve.tensor_tensor(gl[:, u, 2 * n:2 * n + 2, :], fused(b, n)[:, :, D:D + E],
                                            spread(rw[:, RB1:RB1 + E], 1, 2), ALU.add)
                then(ins)
                then(dve.tensor_reduce(gm[:, :], gl[:, u, :, :], AX_X, ALU.max, negate=True))
                dve.tensor_tensor(gl[:, u, :, :], gl[:, u, :, :], spread(gm[:, :], 2, E), ALU.add).then_inc(gate_in, 1)

            def outer(b):
                u = b % 2
                dve.wait_ge(gate_exp, b + 1)
                then(dve.tensor_reduce(gm[:, :], gl[:, u, :, :], AX_X, ALU.add))
                then(dve.reciprocal(gm[:, :], gm[:, :]))
                then(dve.tensor_tensor(gates[:, :, :], gl[:, u, :, :], spread(gm[:, :], 2, E), ALU.mult))
                for t in range(TB):
                    mid = fused(b, t // 2)[:, t % 2, D + E:D + E + R]
                    ins = dve.tensor_tensor(pairs[:, u, t, :].rearrange("p (e r) -> p e r", r=R), spread(mid, 1, E),
                                            spread(gates[:, t, :], 2, R), ALU.mult)
                ins.then_inc(outer_done, 1)

            def finish(b):
                dve.wait_ge(lora_filled, b + 1)
                dve.wait_ge(pool_x, B + b + 1)
                for n in range(2):
                    here = X[:, b * TB + 2 * n:b * TB + 2 * n + 2, :]
                    ins = dve.tensor_tensor(here, here, fused(b, n)[:, :, 0:D], ALU.add)
                ins.then_inc(result_done, 1)

            todo = {"c": combine, "n": norm3, "s": scores1, "a": attend1, "m": norm4, "g": softmax, "o": outer, "f": finish}
            for what in DVE_END:
                if isinstance(what, int):
                    low(what)
                else:
                    todo[what[0]](int(what[1]))

        @block.tensor
        def _(pe):
            def three(where_, left, right, start=True, stop=True):
                (lh, ll), (rh, rl) = left, right
                pe.matmul(where_, lh, rh, start=start, stop=False, skip_group_check=True)
                pe.matmul(where_, lh, rl, start=False, stop=False, skip_group_check=True)
                return pe.matmul(where_, ll, rh, start=False, stop=stop, skip_group_check=True)

            def packed(a, n):
                return sp_hi[:, a:a + n], sp_lo[:, a:a + n]

            def kept(a, n, rows_=P):
                return kq_hi[0:rows_, a:a + n], kq_lo[0:rows_, a:a + n]

            def t1_free(kind, b):
                if t1(kind, b):
                    pe.wait_ge(t1_freed, t1(kind, b))

            for n in range(3):
                if n == 0:
                    pe.wait_ge(split_done, 2)
                at = slice(WKD + n * P, WKD + (n + 1) * P)
                three((ringB[0], ringB[1], T1)[n][:, 0:B * SKP], (early_hi[:, at], early_lo[:, at]), packed(CTX, B * SKP))\
                    .then_inc(keys_filled, 1)

            def queries(b):
                pe.wait_ge(split_done, 3)
                pe.wait_ge(t0_freed, t0("x", b) + 1)
                for n in range(2):
                    job = a_job("queries", b, n)
                    if job >= 2:
                        pe.wait_ge(a_freed, job - 1)
                    at = slice(WQD + n * P, WQD + (n + 1) * P)
                    three(ringA[job % 2][:, :], (early_hi[:, at], early_lo[:, at]), (T_hi[:, 0, :], T_lo[:, 0, :]))\
                        .then_inc(a_filled, 1)

            def turn(kind, b, src):
                n = t0(kind, b)
                if n:
                    pe.wait_ge(t0_freed, n)
                for t in range(TB):
                    ins = pe.transpose(T0[:, t * P:(t + 1) * P], src[:, t, :], ident)
                ins.then_inc(t0_filled, 1)

            def turn_x(b):
                pe.wait_ge(ln_done, b + 1)
                turn("x", b, XN[:, 0, :, :])

            def max_scores(b, n):
                t, h0 = n // (H // GH), n % (H // GH) * GH
                job = a_job("max", b, n)
                half = h0 // HALF
                rows_ = slice(P // 2 * half, P // 2 * (half + 1))
                if n == 0:
                    pe.wait_ge(a_hi, 2 * b + 2)
                    pe.wait_ge(ka_done, 2 * b + 2)
                pe.wait_ge(a_freed, job - 1)
                o = ringA[job % 2][:, 0:GH * SK]
                keys = KA[rows_, b % 2, half, h0 % HALF:h0 % HALF + GH, :].rearrange("p h k -> p (h k)")
                pe.matmul(o, QA[rows_, b % 2, half, t * P:(t + 1) * P], keys, start=True, stop=False)
                pe.matmul(o, Z[0:96, b, t * P:(t + 1) * P], sel[0:96, h0 * SK:(h0 + GH) * SK], start=False, stop=True)\
                    .then_inc(a_filled, 1)

            def turn_shift(b):
                t1_free("shift", b)
                pe.wait_ge(shift_done, b + 1)
                for t in range(TB):
                    ins = pe.transpose(T1[0:2 * H, t * P // 2:(t + 1) * P // 2].bitcast(BF16), shift[:, t, :], ident_bf[:, :])
                ins.then_inc(t1_filled, 1)

            def pair_scores(b, c):
                n, m = NC * b + c, rows_of(c)
                if c == 0:
                    pe.wait_ge(v_done, B)
                    pe.wait_ge(a_freed, a_job("queries", b, 1) + 1)
                    pe.wait_ge(kb_done, b + 1)
                    pe.wait_ge(t1_freed, t1("shift", b) + 1)
                if n >= 2:
                    pe.wait_ge(exp_done, n - 1)
                u, at, half = b % 2, c % NH * CH, c // NH
                rows_ = slice(P // 2 * half, P // 2 * (half + 1))
                o = ringB[n % 2][0:m, :]
                first = KA[:, u, half, :, :].rearrange("p h k -> p (h k)")[:, at:at + m]
                second = KB[rows_, u, :, :].rearrange("p h k -> p (h k)")[:, at:at + m]
                pe.matmul(o, first, QA[:, u, half, :], start=True, stop=False, skip_group_check=True)
                pe.matmul(o, second, QA[rows_, u, half, :], start=False, stop=False, skip_group_check=True)
                pe.matmul(o, sel[:, pair_at(c):pair_at(c) + m], Z[:, b, :], start=False, stop=True,
                          skip_group_check=True).then_inc(b_filled, 1)

            def weigh(b, c):
                n, m = NC * b + c, rows_of(c)
                pe.wait_ge(exp_done, n + 1)
                if c == 0:
                    if b >= 1:
                        pe.wait_ge(o_done, b)
                for t in range(TB):
                    a = (t % 2) * H * OC + first_head(c) * OC
                    ins = pe.matmul(accs[t // 2][:, a:a + 3 * OC], probs[0:m, n % 3, t * P:(t + 1) * P], vblk[0:m, b, c, :],
                                    start=(c == 0 and t % 2 == 0), stop=(c == NC - 1), skip_group_check=True)
                ins.then_inc(pv_done, 1)

            def project(b):
                t1_free("wo", b)
                pe.wait_ge(t0_freed, t0("o", b) + 1)
                for t in range(TB):
                    at = slice(t * P, (t + 1) * P)
                    ins = three(T1[:, at], (T_hi[:, 2, at], T_lo[:, 2, at]), packed(WO0, D))
                ins.then_inc(t1_filled, 1)

            def turn_o(b):
                pe.wait_ge(o_done, b + 1)
                turn("o", b, O)

            def turn_y(b):
                pe.wait_ge(ln_done, B + b + 1)
                turn("y", b, XN[:, 1, :, :])

            def route(b):
                t1_free("logits", b)
                pe.wait_ge(t0_freed, t0("y", b) + 1)
                for t in range(TB):
                    at = slice(t * P, (t + 1) * P)
                    pe.matmul(T1[:, 2 * t * E:2 * (t + 1) * E].rearrange("p (v e) -> p v e", v=2), T_hi[:, 2, at],
                              sp2[:, :, RT0:RT0 + E], start=(t == 0), stop=False, skip_group_check=True)
                    ins = pe.matmul(T1[:, 2 * t * E:(2 * t + 1) * E], T_lo[:, 2, at], sp_hi[:, RT0:RT0 + E],
                                    start=False, stop=(t == TB - 1), skip_group_check=True)
                ins.then_inc(t1_filled, 1)

            pe.wait_ge(plain_in, 16)
            turn_x(0)
            queries(0)
            pe.wait_ge(keep_done, 2)
            pe.wait_ge(keys_lo_done, 1)
            for t in range(TB):
                ins = pe.matmul(T1[:, t * B:(t + 1) * B], keept[:, t * P:(t + 1) * P], padk[:, :], start=True, stop=True)
            ins.then_inc(t1_filled, 1)
            pe.wait_ge(z_done, 1)
            pe.wait_ge(sel_in, 16)

            three(ringB[1][:, 0:B * SKP], (early_hi[:, WV0:WV0 + D], early_lo[:, WV0:WV0 + D]), packed(CTX, B * SKP))\
                .then_inc(values_filled, 1)

            def turn_values(b):
                pe.wait_ge(values3_done, b // 2 + 1)
                if b >= 2:
                    pe.wait_ge(v_done, b - 1)
                for c in range(NH):
                    a = CH * c % SK
                    o = accs[b % 2][0:CH, c * D:(c + 1) * D] if c < NH - 1 else ringB[0][0:CH, b * D:(b + 1) * D]
                    ins = pe.transpose(o, values3[b // 2][:, b % 2, a:a + CH], ident)
                ins.then_inc(v_filled, 1)

            for n in range(UNITS):
                max_scores(0, n)
                if n % (UNITS // B) == UNITS // B - 2:
                    turn_values(n // (UNITS // B))
                if n == 8:
                    turn_x(1)
            pe.wait_ge(tab_in, 16)
            turn_shift(0)
            for b in range(B):
                for c in range(NC):
                    pair_scores(b, c)
                    if c == 0 and b + 1 < B:
                        queries(b + 1)
                    if (b, c) in LOGITS_AT:
                        route(LOGITS_AT[b, c])
                    if b + 1 < B:
                        for n in UNITS_AT[c]:
                            max_scores(b + 1, n)
                    if b >= 1 and c == 2:
                        turn_o(b - 1)
                    if b >= 1 and c == 4:
                        project(b - 1)
                    if c == 6 and b + 2 < B:
                        turn_x(b + 2)
                    if b >= 1 and c == 8:
                        turn_y(b - 1)
                    if c >= 2:
                        weigh(b, c - 2)
                if b + 1 < B:
                    turn_shift(b + 1)
                weigh(b, NC - 2)
                weigh(b, NC - 1)
            turn_o(B - 1)
            project(B - 1)
            turn_y(B - 1)
            route(B - 1)

            pe.wait_ge(t1_freed, len(T1_USES))
            pe.wait_ge(picked, 1)
            ones = tab[:, ON:ON + P]
            pe.matmul(T1[:, 0:NT * E], tab[:, UT:UT + P], cnt[:, :, :].rearrange("p t e -> p (t e)"),
                      start=True, stop=False, skip_group_check=True)
            for t in range(NT - 1):
                pe.matmul(T1[:, (t + 1) * E:NT * E].rearrange("p (t e) -> p t e", e=E), ones,
                          spread(cnt[:, t, :], 1, NT - 1 - t), start=False, stop=(t == NT - 2), skip_group_check=True)
            for t in range(NT):
                ins = pe.matmul(T1[:, NT * E:NT * E + E], ones, cnt[:, t, :], start=False, stop=(t == NT - 1),
                                skip_group_check=True)
            ins.then_inc(rank_filled, 1)

            pe.wait_ge(t0_freed, len(T0_USES))
            pe.wait_ge(split_done, 2)
            three(T0[:, 0:B * SKP], packed(WK1, D), packed(CTX, B * SKP)).then_inc(k1_filled, 1)
            for q in range(TOPK * NT):
                pe.wait_ge(onehot_done, q + 2)
                ins = pe.matmul(T1[:, 0:3 * ST].rearrange("p (v i) -> p v i", i=ST), onehot[:, q, :], where[:, :, q, :],
                                start=(q == 0), stop=(q == TOPK * NT - 1))
            ins.then_inc(inverse_filled, 1)

            pe.wait_ge(k1_done, 1)
            three(T0[:, 0:B * SKP], packed(WQ1, D), kept(K1, B * SKP)).then_inc(k1_filled, 1)
            pe.wait_ge(k1_done, 2)
            for b in range(B):
                ctx_b = packed(CTX + b * SKP, SK)
                ins = three(T0[0:SK, b * D:(b + 1) * D], ctx_b, packed(WV1, D))
            ins.then_inc(k1_filled, 1)
            pe.wait_ge(k1_done, 5)
            three(T0[:, 0:B * SKP], (bq1_hi, bq1_lo), kept(K1, B * SKP)).then_inc(k1_filled, 1)

            def experts_of(i, k, n):
                _, e = nc.values_load_multi_w_load_instructions(
                    etab[0:1, bass.ds(4 * i + k, n)], engines=[mybir.EngineType.PE], min_val=0, max_val=E - 1,
                    skip_runtime_bounds_check_because="the table's numbers are cut at E - 1 and count from 0")
                return {k + m: e[m] for m in range(n)}

            def turn_tokens(i, k):
                n = k % SLOTS
                pe.wait_ge(gathered[n], 16 * (i + k // SLOTS + 1))
                pe.transpose(T0[:, 0:P], G[:, n, :], ident).then_inc(xt_filled, 1)

            def gate_up(i, k, e):
                s, u = 4 * i + k, k % 2
                pe.wait_ge(xt_ready, s + 1)
                high, low = XT_hi[:, u * P:(u + 1) * P], XT_lo[:, u * P:(u + 1) * P]
                for o, n, done in ((ringA[u], 0, gate_filled), (ringB[u], 2, up_filled)):
                    right = [gate_up_w[:, bass.ds(e * (4 * FF) + (n + part) * FF, FF)] for part in range(2)]
                    three(o[:, :], (high, low), right).then_inc(done, 1)

            def down(i, k, e):
                s, u = 4 * i + k, k % 2
                pe.wait_ge(ht_ready, s + 1)
                if k >= 1:
                    pe.wait_ge(y_copied, s)
                for c in range(FC):
                    at = slice(c * P, (c + 1) * P)
                    start = e * (FC * 2 * P) + c * 2 * P
                    pe.matmul(T1[:, 0:2 * D], T_hi[:, 1 + u, at], down_w[:, bass.ds(start, 2 * P)],
                              start=(c == 0), stop=False, skip_group_check=True)
                    ins = pe.matmul(T1[:, 0:D], T_lo[:, 1 + u, at], down_w[:, bass.ds(start, P)],
                                    start=False, stop=(c == FC - 1), skip_group_check=True)
                ins.then_inc(y_filled, 1)

            def turn_hidden(i, k):
                s, u = 4 * i + k, k % 2
                pe.wait_ge(h_done, s + 1)
                for c in range(FC):
                    ins = pe.transpose(accs[u][:, c * P:(c + 1) * P], HH[:, u, c * P:(c + 1) * P], ident)
                ins.then_inc(ht_filled, 1)

            def step(i, k, e):
                if 1 <= k <= ST:
                    turn_hidden(i, k - 1)
                if k < ST:
                    gate_up(i, k, e[k])
                if k + 1 < ST:
                    turn_tokens(i, k + 1)
                if k >= 2:
                    down(i, k - 2, e[k - 2])

            pe.wait_ge(k1_hi, 4)
            pe.wait_ge(k1_done, 6)
            pe.wait_ge(w_lo_done, NW)
            pe.wait_ge(index_done, 1)
            pe.wait_ge(experts_done, 1)
            turn_tokens(0, 0)
            e = experts_of(0, 0, HEAD)
            for k in range(HEAD):
                step(0, k, e)
            with pe.Fori(0, LOOPS) as i:
                e = experts_of(i, HEAD - 2, SLOTS + 2)
                for u in range(SLOTS):
                    step(i, HEAD + u, e)
            rest = HEAD + SLOTS * LOOPS
            e = experts_of(0, rest - 2, ST - rest + 2)
            for k in range(rest, ST + 2):
                step(0, k, e)

            def part(n):
                kind, b = T_JOBS[n]
                if n >= 2:
                    pe.wait_ge(f_freed, n - 1)
                if kind == "x":
                    pe.wait_ge(ln_done, 2 * B + b + 1)
                elif kind == "p":
                    pe.wait_ge(p1_done, b + 1)
                elif kind == "y":
                    pe.wait_ge(ln_done, 3 * B + b + 1)
                else:
                    pe.wait_ge(outer_done, b + 1)
                for t in range(TB):
                    src = {"x": XN[:, b % 2, t, :], "p": P1[:, b * TB + t, 0:SK], "y": XN[:, b % 2, t, :],
                           "z": pairs[:, b % 2, t, :]}[kind]
                    ins = pe.transpose((T0, T1)[n % 2][0:src.shape[1], t * P:(t + 1) * P], src, ident)
                ins.then_inc(f_filled, 1)

            def parts_of(kind, b, t, rows_=P):
                n = T_JOBS.index((kind, b))
                at = slice(t * P, (t + 1) * P)
                return T_hi[0:rows_, n % 3, at], T_lo[0:rows_, n % 3, at]

            def ready(kind, b):
                pe.wait_ge(f_freed, T_JOBS.index((kind, b)) + 1)

            def scores1(b):
                ready("x", b)
                if b >= 2:
                    pe.wait_ge(negmax1_done, b - 1)
                for t in range(TB):
                    ins = three(ringA[b % 2][:, t * SKP:(t + 1) * SKP], parts_of("x", b, t), kept(A1 + b * SKP, SKP))
                ins.then_inc(sc_filled, 1)

            def values1(b):
                ready("p", b)
                if b >= 2:
                    pe.wait_ge(ln_stats, 3 * B + b - 1)
                for t in range(TB):
                    ins = three(ringB[b % 2][:, t * D:(t + 1) * D], parts_of("p", b, t, SK), kept(V1 + b * D, D, SK))
                ins.then_inc(pv1_filled, 1)

            def fused(b):
                ready("y", b)
                if b >= 2:
                    pe.wait_ge(result_done, b - 1)
                elif b == 1:
                    pe.wait_ge(negmax1_done, B)
                for t in range(TB):
                    bank_ = (accs, ringA)[b % 2][t // 2]
                    ins = three(bank_[:, (t % 2) * FBW:(t % 2 + 1) * FBW], parts_of("y", b, t), packed(FB1, FBW),
                                start=(t % 2 == 0), stop=False)
                ins.then_inc(fb_filled, 1)

            def lora(b):
                ready("z", b)
                for t in range(TB):
                    bank_ = (accs, ringA)[b % 2][t // 2]
                    ins = three(bank_[:, (t % 2) * FBW:(t % 2) * FBW + D], parts_of("z", b, t, E * R), kept(LBM, D, E * R),
                                start=False)
                ins.then_inc(lora_filled, 1)

            todo = {"s": scores1, "v": values1, "b": fused, "l": lora}
            for what in PE_END:
                if isinstance(what, int):
                    part(what)
                else:
                    todo[what[0]](int(what[1]))


def kernel(**inputs):
    import ml_dtypes
    import numpy as np
    import concourse.bacc as bacc
    from concourse.bass_utils import run_bass_kernel_spmd

    v = {k: np.asarray(a) for k, a in inputs.items()}
    f32, bf16 = np.float32, ml_dtypes.bfloat16
    i = np.arange(P)

    def pad(a):
        return np.concatenate([a, np.zeros((P - a.shape[0], a.shape[1]), a.dtype)], 0)

    ctx = np.zeros((D, B, SKP), f32)
    ctx[:, :, 0:SK] = v["ctx_1024"].transpose(2, 0, 1)
    wk, wq = v["L0_xattn_Wk"].T, v["L0_xattn_Wq"].T
    halves = [slice(0, D // 2)] * 2 + [slice(D // 2, D)] * 2
    early = np.concatenate([wk[:, h] for h in halves] + [wk] + [wq[:, h] for h in halves] + [v["L0_xattn_Wv"].T], 1)
    split = np.concatenate([
        ctx.reshape(D, B * SKP), v["L0_xattn_Wo"].T, v["L0_ffn_router_w"].T,
        v["L1_xattn_Wq"].T, v["L1_xattn_Wk"], v["L1_xattn_Wv"],
        v["L1_ffn_base_w"].T, v["L1_ffn_router_w"].T, v["L1_ffn_lora_A"]], 1)

    pair = np.arange(HK)
    block = np.zeros((P, NC, 3), f32)
    for c in range(NC):
        r = np.arange(rows_of(c))
        for n in range(3):
            block[r, c, n] = (pair_at(c) + r) // SK == first_head(c) + n
    own_head = (i[:, None] % (P // 2) // DK == np.arange(HALF)[None, :]).astype(f32)
    bk, bq = v["L0_xattn_bk"], v["L0_xattn_bq"]
    twice = [np.concatenate([a[h], a[h]])[:, None] for a in (bk, bq) for h in (halves[0], halves[2])]
    before = np.broadcast_to((np.arange(E)[None, :] < np.arange(E)[:, None]).astype(f32).reshape(1, E * E), (P, E * E))
    tile_index = np.broadcast_to(np.arange(TOPK * NT, dtype=f32), (P, TOPK * NT))
    falling = np.broadcast_to(E - np.arange(E, dtype=f32), (P, E))
    steps = np.broadcast_to(P * np.arange(16, dtype=f32), (P, 16))
    plain = np.concatenate([
        np.eye(P, dtype=f32), twice[0], twice[1], bk[:, None], twice[2], twice[3],
        v["L1_xattn_bk"][:, None], v["L1_xattn_bq"][:, None], v["L0_xattn_bv"][:, None], own_head,
        pad(v["L1_ffn_lora_B"].reshape(E * R, D)), block.reshape(P, 3 * NC), before, tile_index,
        i[:, None].astype(f32), (ROWS + i[:, None]).astype(f32), falling, steps,
        (ROWS + P * np.arange(ST)[None, :] + i[:, None]).astype(f32)], 1)
    rows = np.concatenate([v["L0_xattn_bo"], v["L1_xattn_bv"], v["L1_ffn_base_b"], v["L1_ffn_router_b"]])[None, :]
    tables = np.concatenate([
        i[:, None] < i[None, :], np.ones((P, P)), np.broadcast_to(i[None, :], (P, P)),
        np.broadcast_to(np.arange(ST)[None, :], (P, ST)), np.eye(P)], 1).astype(bf16)
    select = np.zeros((P, HK), bf16)
    select[pair % SK, pair] = 1
    select[96 + pair // SK, pair] = 1
    select[96 + H + pair // SK, pair] = 1

    arrays = {
        "x": v["x"].reshape(TOK, D), "early": early, "split": split, "plain": plain, "rows": rows, "tables": tables, "select": select,
        "mask_t": v["mask_SxS2_ik0"].T, "pad_t": v["mask_BxS2_if1"].T,
        "w_gate": v["L0_ffn_w_gate"], "w_up": v["L0_ffn_w_up"], "w_down": v["L0_ffn_w_down"],
    }
    arrays = {f"in_{k}": np.ascontiguousarray(a) for k, a in arrays.items()}
    nc = bacc.Bacc("TRN2", target_bir_lowering=False, num_devices=1)
    args = [nc.dram_tensor(k, a.shape, mybir.dt.from_np(a.dtype), kind="ExternalInput").ap() for k, a in arrays.items()]
    out = nc.dram_tensor("out", (TOK, D), F32, kind="ExternalOutput").ap()
    xattn_moe_xattn_lora_kernel(nc, *args, out)
    result = run_bass_kernel_spmd(nc, [arrays], core_ids=[0])
    return result.results[0]["out"].reshape(B, S, D)
```

```python
from contextlib import ExitStack

import concourse.bass as bass
from concourse import mybir

F32 = mybir.dt.float32
F32R = mybir.dt.float32r
BF16 = mybir.dt.bfloat16
I32 = mybir.dt.int32
ALU = mybir.AluOpType
ACT = mybir.ActivationFunctionType
AX_X = mybir.AxisListType.X

P = 128
B, S, D = 4, 512, 128
TB = S // P
NT = B * TB
TOK = B * S
SK, SKP = 77, 78
H = 16
DK = D // H
OC = DK + 1
HK = H * SK
CH = 124
HALF = H // 2
HW = HALF * SK
NH = -(-HW // CH)
GH = 4
UNITS = TB * H // GH
NC = 2 * NH
E, FF = 8, 512
FC = FF // P
TOPK = 2
ST = (TOK * TOPK + E * (P - 1)) // P
ROWS = TOPK * TOK
R = 8
HARD = -1.0e30
EPS = 1e-5
WP = 1024
NW = 2 * E * FF // WP
SLOTS = 4

WKD, WKN, WQD, WV0, NEARLY = 0, 256, 384, 640, 768
BK, BQ, BK1, BQ1C, BV, HM = 128, 131, 133, 134, 135, 136
IDN, CTX, LB, BLK, LT8, TIDX, PCOL, WDS, M128, SPARE = 0, 144, 456, 584, 614, 678, 710, 712, 720, 736
WO0 = SPARE + ST
RT0, WQ1, WK1, WV1, FB1, NPLAIN = WO0 + 128, WO0 + 136, WO0 + 264, WO0 + 392, WO0 + 520, WO0 + 664
BO, BV1, BB1, RB1, NROWS = 0, 128, 256, 384, 392
UT, ON, IOP, IOT, IDB, NTAB = 0, 128, 256, 384, 384 + ST, 512 + ST
FBW = D + E + R


def first_head(c):
    return c // NH * HALF + min(c % NH * CH // SK, HALF - 3)


def rows_of(c):
    return min(CH, HW - CH * (c % NH))


def pair_at(c):
    return c // NH * HW + c % NH * CH


T0_USES = [("x", 0), ("x", 1), ("x", 2), ("o", 0), ("x", 3), ("y", 0)] + [(k, b) for b in (1, 2, 3) for k in ("o", "y")]
T1_USES = ([("flags", 0), ("shift", 0), ("shift", 1), ("wo", 0), ("shift", 2), ("logits", 0), ("wo", 1), ("shift", 3)]
           + [("logits", 1), ("wo", 2), ("logits", 2), ("wo", 3), ("logits", 3)])


def t0(kind, b):
    return T0_USES.index((kind, b))


def t1(kind, b):
    return T1_USES.index((kind, b))


def a_job(kind, b, n):
    return (2 + UNITS) * b + (n if kind == "queries" else 2 + n)


T_JOBS = [("x", 0), ("x", 1), ("x", 2), ("x", 3), ("p", 0), ("p", 1), ("p", 2), ("p", 3),
          ("y", 0), ("y", 1), ("y", 2), ("z", 0), ("y", 3), ("z", 1), ("z", 2), ("z", 3)]
PE_END = [0, 1, "s0", 2, "s1", 3, "s2", 4, "s3", 5, "v0", 6, "v1", 7, "v2", 8, "v3", 9, "b0", 10, "b1",
          11, "l0", "b2", 12, 13, "b3", "l1", 14, "l2", 15, "l3"]
ACT_END = [0, 1, 2, "e0", 3, "e1", 4, "e2", 5, "e3", 6, 7, 8, 9, "g0", 10, "g1", 11, 12, "g2", 13, "g3", 14, 15]
DVE_END = ["c0", "c1", "n0", "c2", "n1", "c3", "n2", "s0", "n3", "s1", "s2", "s3", "a0", "a1", "m0", "a2", "m1",
           "a3", "m2", "g0", "m3", "o0", "g1", "o1", "f0", "g2", "o2", "g3", "o3", "f1", "f2", "f3"]
POOL_ROWS = 11
HEAD = 7
LOOPS = (ST - 1 - HEAD) // SLOTS

UNITS_AT = [range(0, 0)] + [range(UNITS * n // 7, UNITS * (n + 1) // 7) for n in range(7)] + [range(0, 0)] * 2
Y_AT = (None, 9, 9, 8)
LOGITS_AT = {(2, 1): 0, (3, 1): 1, (3, 9): 2}


def spread(ap, axis, n):
    v = ap.unsqueeze(axis)
    return v.broadcast_to([*v.shape[:axis], n, *v.shape[axis + 1:]])


def xattn_moe_xattn_lora_kernel(nc, x, early, plain, rows, tables, select, mask_t, pad_t, w_gate, w_up, w_down, out):
    with ExitStack() as stack:
        def sb(name, shape, dt=F32):
            return stack.enter_context(nc.sbuf_tensor("sb_" + name, shape, dt))

        def bank(name):
            return stack.enter_context(nc.psum_tensor("ps_" + name, [P, 512], F32))

        def sem(name):
            return stack.enter_context(nc.semaphore(name))

        normed_d = nc.dram_tensor("normed_rows", [TOK, D], F32).ap()
        expert_d = nc.dram_tensor("expert_rows", [ROWS + ST * P, D], F32).ap()

        gate_up_w = sb("gate_up_w", [P, E * 4 * FF], F32R)
        down_w = sb("down_w", [P, E * FF])
        first_w = sb("first_w", [P, 2 * NEARLY + 4 * B * SKP], F32R)
        second_w = sb("second_w", [P, 2 * B * SKP + B * D + 2 * P])
        work = sb("work", [P, SLOTS * WP])
        X = sb("X", [P, NT, D])
        XN = sb("XN", [P, 2, TB, D])
        T_hi = sb("T_hi", [P, S], F32R)
        T_lo = sb("T_lo", [P, S], F32R)
        TF = sb("TF", [P, 3, S])
        kq_hi = sb("kq_hi", [P, 2 * HK], F32R)
        kq_lo = sb("kq_lo", [P, 2 * HW], F32R)
        QA = sb("QA", [P, 2, 2, S], F32R)
        sel = sb("sel", [P, HK], BF16)
        Z = sb("Z", [P, B, S], BF16)
        probs = sb("probs", [P, 3, S])
        vblk = sb("vblk", [P, B, NC, 3 * OC])
        ctx2 = sb("ctx2", [P, 2, B * SKP], F32R)
        pl = sb("pl", [P, NPLAIN])
        rw = sb("rw", [P, NROWS])
        tab = sb("tab", [P, NTAB], BF16)
        kt = sb("bias1", [P, B * SKP])
        stats = sb("stats", [P, TB, 6])
        mv = sb("mv", [P, 4 * B, TB, 2])
        rstd = sb("rstd", [P, 4 * B, TB])
        power = sb("power", [P, TB])
        negmax = sb("negmax", [P, TB, H])
        shift = sb("shift", [P, TB, 2 * H], BF16)
        O = sb("O", [P, TB, D])
        rsum = sb("rsum", [P, TB, H])
        flags = sb("flags", [P, NT])
        flag2 = sb("flag2", [P, NT])
        padf = sb("padf", [SK, 2, B])
        padk = sb("padk", [SK, B], BF16)
        padi = sb("padi", [SK, B], I32)
        L = sb("L", [P, NT, E])
        L2 = sb("L2", [P, NT, E])
        oh = sb("oh", [P, TOPK, NT, E])
        m12 = sb("m12", [P, TOPK, NT])
        mx = sb("mx", [P, TOPK, NT])
        cnt = sb("cnt", [P, NT, E], BF16)
        wts = sb("wts", [P, TOPK, NT])
        et = sb("et", [P, NT])
        etab = sb("etab", [1, ST], I32)
        gidx = sb("gidx", [P, ST], I32)
        didx = sb("didx", [P, ST], I32)
        L3 = sb("L3", [P, NT, E])
        tiles = sb("tiles", [P, 2, E])
        nm1 = sb("nm1", [P, NT])
        sum1 = sb("sum1", [P, NT])
        gl = sb("gl", [P, 2, TB, E])
        gm = sb("gm", [P, TB])
        gates = sb("gates", [P, TB, E], BF16)
        early_use = sb("early_use", [1, 2])

        ident = pl[:, IDN:IDN + P]
        raw = work[:, 0:NEARLY]
        ctx_hi, ctx_lo = ctx2[:, 0, :], ctx2[:, 1, :]
        early_hi, early_lo = first_w[:, 0:NEARLY], first_w[:, NEARLY:2 * NEARLY]
        keys_all = first_w[:, 2 * NEARLY:].rearrange("p (v b k) -> p v b k", v=4, b=B)
        keys2, keys_hi, keys_lo = keys_all[:, 0:2, :, :], keys_all[:, 2, :, :], keys_all[:, 3, :, :]
        values3 = [t.rearrange("p t d -> p (t d)").rearrange("p (b k) -> p b k", b=2)[:, :, 0:3 * SK]
                   for t in (O[:, :, :], XN[:, 1, :, :])]
        maskt = probs[0:SK, 0, :].bitcast(I32)
        keept = probs[0:SK, 1, 0:S // 2].bitcast(BF16)
        maskz = probs[0:SK, 2, :]
        onehot = work[:, 0:2048].bitcast(BF16).rearrange("p (q i) -> p q i", i=P)
        where = work[:, 2048:2048 + 48 * ST].bitcast(BF16).rearrange("p (v q i) -> p v q i", v=3, i=ST)
        G = work[:, 0:512].rearrange("p (s d) -> p s d", s=SLOTS)
        SG = work[:, 512:1536].rearrange("p (s f) -> p s f", s=2)
        HH = work[:, 1536:2560].rearrange("p (s f) -> p s f", s=2)
        Y = work[:, 2560:3072].rearrange("p (s d) -> p s d", s=SLOTS)
        XT_hi, XT_lo = T_hi[:, :], T_lo[:, :]
        yk = work[:, 0:TOPK * NT * D].rearrange("p (k t d) -> p k t d", k=TOPK, t=NT)
        P1 = probs[:, :, :].rearrange("p a s -> p (a s)")[:, 0:NT * SKP].rearrange("p (t k) -> p t k", k=SKP)
        scratch = probs[:, :, :].rearrange("p a s -> p (a s)")
        pos = scratch[:, 0:256].rearrange("p (k t e) -> p k t e", k=TOPK, e=E)
        cmp16 = scratch[:, 256:384].rearrange("p (e m) -> p e m", e=E)
        cmp8 = scratch[:, 384:448].rearrange("p (e f) -> p e f", e=E)
        cmpt = scratch[:, 448:448 + ST * E].rearrange("p (i e) -> p i e", e=E)
        inv = scratch[:, 1024:1024 + 4 * ST]
        etf = scratch[:, 1180:1180 + ST]
        sloti = scratch[:, 1220:1316].bitcast(I32).rearrange("p (v k t) -> p v k t", v=3, k=TOPK)
        tile_row = scratch[:, 1316:1380].rearrange("p (v k t) -> p v k t", v=2, k=TOPK)
        row_of = tile_row[:, 1, :, :].rearrange("p k t -> p (k t)")
        slot = scratch[:, 1380:1412].rearrange("p (k t) -> p k t", k=TOPK)
        pairs = vblk[:, 0:2, :, :].rearrange("p b c j -> p (b c j)")[:, 0:2 * TB * E * R].rearrange(
            "p (u t j) -> p u t j", u=2, t=TB)
        k1, a1 = second_w[:, 0:B * SKP], second_w[:, B * SKP:2 * B * SKP]
        v1 = second_w[0:SK, 2 * B * SKP:2 * B * SKP + B * D]
        bq1 = second_w[:, 2 * B * SKP + B * D:2 * B * SKP + B * D + P]
        lb = second_w[0:E * R, 2 * B * SKP + B * D + P:]
        KA = kq_hi[:, :].rearrange("p (b u h k) -> p b u h k", b=2, u=2, k=SK)
        KB = kq_lo[:, 0:2 * HW].rearrange("p (b h k) -> p b h k", b=2, k=SK)
        own = pl[:, HM:HM + HALF]
        ident_bf = tab[:, IDB:IDB + P]

        def half_tiles(n):
            return range(2 * n, 2 * n + 2), slice((B - 1) * TB + 2 * n, (B - 1) * TB + 2 * n + 2)

        def piece_of(i, part):
            which, e = i // 4, 2 * (i % 4)
            return gate_up_w[:, :].rearrange("p (e w v f) -> p e w v f", e=E, w=2, v=2)[:, e:e + 2, which, part, :]

        def staged(i):
            slot = (i + 2) % SLOTS
            return work[:, slot * WP:(slot + 1) * WP].rearrange("p (g f) -> p g f", f=FF)

        ringA = [bank(f"A{i}") for i in range(2)]
        ringB = [bank(f"B{i}") for i in range(2)]
        accs = [bank(f"acc{i}") for i in range(2)]
        T0, T1 = bank("T0"), bank("T1")

        plain_in, tables_in, keys_in, queries_in, late_in, rows_in, tab_in, down_in = (
            sem(n) for n in ("plain_in", "tables_in", "keys_in", "queries_in", "late_in", "rows_in", "tab_in", "down_in"))
        mask_in, sel_in = sem("mask_in"), sem("sel_in")
        x_in = [sem(f"x_in{b}") for b in range(B)]
        w_in = [sem(f"w_in{i}") for i in range(SLOTS)]
        gathered = [sem(f"gathered{i}") for i in range(SLOTS)]
        scattered = [sem(f"scattered{i}") for i in range(SLOTS)]
        expert_in = [sem(f"expert_in{b}") for b in range(B)]
        normed_out, result_out = sem("normed_out"), sem("result_out")
        split_hi, split_done = sem("split_hi"), sem("split_done")
        values_filled, values3_done, experts_done = sem("values_filled"), sem("values3_done"), sem("experts_done")
        keys_filled, keys_hi_done, keys_lo_done, ka_done, kb_done = (
            sem(n) for n in ("keys_filled", "keys_hi_done", "keys_lo_done", "ka_done", "kb_done"))
        t0_filled, t0_copied, x_lo_done = sem("t0_filled"), sem("t0_copied"), sem("x_lo_done")
        t1_filled, t1_freed = sem("t1_filled"), sem("t1_freed")
        a_filled, a_hi, a_freed = sem("a_filled"), sem("a_hi"), sem("a_freed")
        b_filled, exp_done, pv_done = sem("b_filled"), sem("exp_done"), sem("pv_done")
        v_filled, v_done, o_done = sem("v_filled"), sem("v_done"), sem("o_done")
        keep_done, pad_done, ones_done, z_done, z_pool, shift_done = (
            sem(n) for n in ("keep_done", "pad_done", "ones_done", "z_done", "z_pool", "shift_done"))
        ln_stats, ln_rstd, ln_done = sem("ln_stats"), sem("ln_rstd"), sem("ln_done")
        w_hi_done, w_lo_done = sem("w_hi_done"), sem("w_lo_done")
        dve_step, act_step, pool_step = sem("dve_step"), sem("act_step"), sem("pool_step")
        picked, rank_filled, rows_found, where_done, onehot_done, onehot_pool, inverse_filled, index_done = (
            sem(n) for n in ("picked", "rank_filled", "rows_found", "where_done", "onehot_done", "onehot_pool",
                             "inverse_filled", "index_done"))
        wexp_done, weights_done, first_in, first_added = (
            sem(n) for n in ("wexp_done", "weights_done", "first_in", "first_added"))
        gate_filled, up_filled, silu_done, h_done = (sem(n) for n in ("gate_filled", "up_filled", "silu_done", "h_done"))
        ht_filled, ht_ready = sem("ht_filled"), sem("ht_ready")
        xt_filled, xt_hi, xt_ready = sem("xt_filled"), sem("xt_hi"), sem("xt_ready")
        y_filled, y_copied = sem("y_filled"), sem("y_copied")
        k1_filled, k1_copied, v1_done, bq1_done, lb_done = (
            sem(n) for n in ("k1_filled", "k1_copied", "v1_done", "bq1_done", "lb_done"))
        f_filled, f_copied = sem("f_filled"), sem("f_copied")
        sc_filled, sc_copied, negmax1_done, p1_done = (sem(n) for n in ("sc_filled", "sc_copied", "negmax1_done", "p1_done"))
        pv1_filled, pv1_freed, fb_filled, fb_freed = (sem(n) for n in ("pv1_filled", "pv1_freed", "fb_filled", "fb_freed"))
        gate_in, gate_exp, outer_done, lora_filled, result_done = (
            sem(n) for n in ("gate_in", "gate_exp", "outer_done", "lora_filled", "result_done"))
        pool_x = sem("pool_x")
        pv_half, o_half, stats_half, rstd_half, norm_half = (
            sem(n) for n in ("pv_half", "o_half", "stats_half", "rstd_half", "norm_half"))
        turned2, copied2, projected2, logits2 = (sem(n) for n in ("turned2", "copied2", "projected2", "logits2"))

        block = stack.enter_context(nc.Block())

        @block.sync
        def _(sp_eng):
            xt = x.rearrange("(b t p) d -> b p t d", p=P, t=TB)
            sp_eng.dma_start(raw[:, 0:WQD], early[:, 0:WQD]).then_inc(keys_in, 16)
            sp_eng.dma_start(X[:, 0:TB, :], xt[0]).then_inc(x_in[0], 16)
            sp_eng.dma_start(pl[:, 0:LB], plain[:, 0:LB]).then_inc(plain_in, 16)
            sp_eng.dma_start(raw[:, WQD:], early[:, WQD:]).then_inc(queries_in, 16)
            sp_eng.dma_start(maskt, mask_t).then_inc(mask_in, 16)
            sp_eng.dma_start(padi[:, :], pad_t).then_inc(mask_in, 16)
            sp_eng.dma_start(sel[:, :], select).then_inc(sel_in, 16)
            sp_eng.dma_start(pl[:, LB:WO0], plain[:, LB:WO0]).then_inc(tables_in, 16)
            sp_eng.dma_start(rw[:, :], rows.broadcast_to([P, NROWS])).then_inc(rows_in, 16)
            sp_eng.dma_start(tab[:, :], tables).then_inc(tab_in, 16)
            for b in range(1, B):
                sp_eng.dma_start(X[:, b * TB:(b + 1) * TB, :], xt[b]).then_inc(x_in[b], 16)
            sp_eng.dma_start(pl[:, WO0:], plain[:, WO0:]).then_inc(late_in, 16)

            def piece(i):
                slot, which, e = (i + 2) % SLOTS, i // 4, 2 * (i % 4)
                if i == 2:
                    sp_eng.wait_ge(split_done, 3)
                if i >= SLOTS:
                    sp_eng.wait_ge(w_lo_done, i - SLOTS + 1)
                for n in range(2):
                    at = work[:, slot * WP + n * FF:slot * WP + (n + 1) * FF]
                    src = (w_gate, w_up)[which][e + n]
                    sp_eng.dma_start(at, src).then_inc(w_in[slot], 16)

            nd = normed_d.rearrange("(b t p) d -> b p t d", p=P, t=TB)
            for i in range(SLOTS):
                piece(i)
            for b in range(B):
                for i in range(SLOTS + 2 * b, min(SLOTS + 2 * b + 2, NW)):
                    piece(i)
                for e in range(2 * b, 2 * b + 2):
                    at = down_w[:, e * FF:(e + 1) * FF].rearrange("p (c d) -> p c d", c=FC)
                    sp_eng.dma_start(at, w_down[e].rearrange("(c p) d -> p c d", p=P)).then_inc(down_in, 16)
                if b >= 1:
                    sp_eng.wait_ge(ln_done, B + b)
                    sp_eng.dma_start(nd[b - 1], XN[:, 1, :, :]).then_inc(normed_out, 16)
            sp_eng.wait_ge(ln_done, 2 * B)
            sp_eng.dma_start(nd[B - 1], XN[:, 1, :, :]).then_inc(normed_out, 16)

            for i in range(SLOTS):
                sp_eng.wait_ge(scattered[i], 16 * len(range(i, ST, SLOTS)))
            ed = expert_d[0:ROWS, :].rearrange("(k b t p) d -> k b p t d", k=TOPK, b=B, p=P)
            def load(b, k, sem_):
                sp_eng.dma_start(yk[:, k, b * TB:(b + 1) * TB, :], ed[k, b]).then_inc(sem_, 16)

            for b in range(B):
                for k in range(TOPK):
                    if (b, k) != (B - 1, 0):
                        load(b, k, expert_in[b])
                if b == 0:
                    load(B - 1, 0, first_in)
            ot = out.rearrange("(b t p) d -> b p t d", p=P, t=TB)
            for b in range(B):
                sp_eng.wait_ge(result_done, b + 1)
                sp_eng.dma_start(ot[b], X[:, b * TB:(b + 1) * TB, :]).then_inc(result_out, 16)
            sp_eng.wait_ge(result_out, 16 * B)
            sp_eng.wait_ge(normed_out, 16 * B)

        @block.gpsimd
        def _(pool):
            steps = [0]

            def then(ins):
                steps[0] += 1
                ins.then_inc(pool_step, 1)
                pool.wait_ge(pool_step, steps[0])

            def rstd_of(n):
                pool.wait_ge(ln_stats, n + 1)
                then(pool.tensor_scalar(rstd[:, n, :], mv[:, n, :, 1], EPS, None, ALU.add))
                pool.tensor_tensor(rstd[:, n, :], rstd[:, n, :], power[:, :], ALU.pow).then_inc(ln_rstd, 1)

            then(pool.memset(power[:, :], -0.5))
            pool.memset(Z[64:96, :, :], 1.0).then_inc(ones_done, 1)
            pool.wait_ge(ones_done, 1)
            rstd_of(0)
            def keys_block(b):
                if b == 0:
                    pool.wait_ge(plain_in, 16)
                    pool.wait_ge(keys_lo_done, 1)
                if b >= 2:
                    pool.wait_ge(b_filled, NC * (b - 1))
                pool.tensor_tensor(KB[:, b % 2, :, :], spread(keys_lo[:, b, 0:SK].bitcast(F32), 1, HALF),
                                   spread(own, 2, SK), ALU.mult).then_inc(kb_done, 1)

            keys_block(0)
            pool.wait_ge(pad_done, 1)
            for b in range(1, B):
                if b == B - 1:
                    rstd_of(1)
                pool.tensor_scalar(Z[0:SK, b, :], maskz, padf[:, 0, b:b + 1], None, ALU.add).then_inc(z_pool, 1)
            for n in range(2):
                pool.tensor_tensor(KA[:, 1, n, :, :], spread(keys2[:, n, 1, 0:SK].bitcast(F32), 1, HALF),
                                   spread(own, 2, SK), ALU.mult).then_inc(ka_done, 1)
            for n in range(2, B):
                rstd_of(n)

            def residual(b):
                here = X[:, b * TB:(b + 1) * TB, :]
                pool.wait_ge(ln_done, b + 1)
                if b == 0:
                    pool.wait_ge(rows_in, 16)
                    pool.wait_ge(t1_freed, t1("flags", 0) + 1)
                then(pool.tensor_tensor(here, here, spread(rw[:, BO:BO + D], 1, TB), ALU.add))
                for t in range(b * TB, (b + 1) * TB):
                    ins = pool.tensor_scalar(X[:, t, :], X[:, t, :], flags[:, t:t + 1], None, ALU.add)
                ins.then_inc(pool_x, 1)

            def low_part(i):
                pool.wait_ge(w_hi_done, i + 1)
                pool.tensor_tensor(piece_of(i, 1), staged(i), piece_of(i, 0).bitcast(F32), ALU.subtract)\
                    .then_inc(w_lo_done, 1)

            for b in range(B):
                residual(b)
                if b + 1 < B:
                    keys_block(b + 1)
                low_part(2 * b)
                if b >= 1:
                    rstd_of(B + b - 1)
                low_part(2 * b + 1)
            for n, done in ((0, rstd_half), (1, ln_rstd)):
                if n == 0:
                    pool.wait_ge(stats_half, 1)
                else:
                    pool.wait_ge(ln_stats, 2 * B)
                at = rstd[:, 2 * B - 1, 2 * n:2 * n + 2]
                then(pool.tensor_scalar(at, mv[:, 2 * B - 1, 2 * n:2 * n + 2, 1], EPS, None, ALU.add))
                pool.tensor_tensor(at, at, power[:, 0:2], ALU.pow).then_inc(done, 1)

            pool.wait_ge(rows_found, 1)
            for q in range(POOL_ROWS):
                pool.tensor_scalar(onehot[:, q, :], tab[:, IOP:IOP + P], row_of[:, q:q + 1], None, ALU.is_equal)\
                    .then_inc(onehot_pool, 1)

            pool.wait_ge(index_done, 1)
            pool.wait_ge(normed_out, 16 * B)
            def gather(s):
                n = s % SLOTS
                if s >= SLOTS:
                    pool.wait_ge(xt_filled, s - SLOTS + 1)
                pool.indirect_dma_start(
                    out=G[:, n, :], out_offset=None, in_=normed_d,
                    in_offset=bass.IndirectOffsetOnAxis(ap=gidx[:, s:s + 1], axis=0)).then_inc(gathered[n], 16)

            def scatter(s):
                n = s % SLOTS
                pool.wait_ge(y_copied, s + 1)
                pool.indirect_dma_start(
                    out=expert_d, out_offset=bass.IndirectOffsetOnAxis(ap=didx[:, s:s + 1], axis=0),
                    in_=Y[:, n, :], in_offset=None).then_inc(scattered[n], 16)

            for s in range(ST + SLOTS + 2):
                if s < ST:
                    gather(s)
                if s >= SLOTS + 2:
                    scatter(s - SLOTS - 2)

            here = slice((B - 1) * TB, NT)
            pool.wait_ge(weights_done, 1)
            pool.wait_ge(first_in, 16)
            for t in range((B - 1) * TB, NT):
                ins = pool.tensor_scalar(yk[:, 0, t, :], yk[:, 0, t, :], wts[:, 0, t:t + 1], None, ALU.mult)
            then(ins)
            pool.tensor_tensor(X[:, here, :], X[:, here, :], yk[:, 0, here, :], ALU.add).then_inc(first_added, 1)
            for n in range(2 * B, 3 * B):
                rstd_of(n)

            def add_bias(b):
                here = X[:, b * TB:(b + 1) * TB, :]
                pool.wait_ge(ln_done, 3 * B + b + 1)
                pool.tensor_tensor(here, here, spread(rw[:, BB1:BB1 + D], 1, TB), ALU.add).then_inc(pool_x, 1)

            for n in range(3 * B, 4 * B):
                rstd_of(n)
                if n >= 3 * B + 2:
                    add_bias(n - 3 * B - 2)
            add_bias(B - 2)
            add_bias(B - 1)

        @block.scalar
        def _(act):
            def first_parts(n, arrived, out, src):
                act.wait_ge(arrived, 16)
                act.activation(out, src, ACT.Copy).then_inc(split_hi, 1)

            first_parts(1, keys_in, early_hi[:, 0:WQD], raw[:, 0:WQD])
            first_parts(2, plain_in, ctx_hi, pl[:, CTX:CTX + B * SKP])
            first_parts(3, queries_in, early_hi[:, WQD:], raw[:, WQD:])
            for n in range(3):
                act.wait_ge(keys_filled, n + 1)
                out = (keys2[:, 0, :, :], keys2[:, 1, :, :], keys_hi)[n]
                act.activation(out.rearrange("p b k -> p (b k)"), (ringB[0], ringB[1], T1)[n][:, 0:B * SKP], ACT.Identity,
                               bias=pl[:, BK + n:BK + n + 1]).then_inc(keys_hi_done, 1)

            def turned(kind, b):
                n = t0(kind, b)
                act.wait_ge(t0_filled, n + 1)
                act.activation(T_hi[:, :] if kind == "x" else TF[:, 2, :], T0[:, :], ACT.Copy).then_inc(t0_copied, 1)

            def queries_hi(b):
                for n in range(2):
                    job = a_job("queries", b, n)
                    act.wait_ge(a_filled, job + 1)
                    act.activation(QA[:, b % 2, n, :], ringA[job % 2][:, :], ACT.Identity,
                                   bias=pl[:, BQ + n:BQ + n + 1]).then_inc(a_hi, 1)

            def shift_in(b):
                act.wait_ge(t1_filled, t1("shift", b) + 1)
                act.activation(Z[96:96 + 2 * H, b, :], T1[0:2 * H, 0:S // 2].bitcast(BF16), ACT.Copy).then_inc(t1_freed, 1)

            def exps(b, c):
                n = NC * b + c
                act.wait_ge(b_filled, n + 1)
                if n == 2:
                    act.wait_ge(z_pool, B - 1)
                if n >= 3:
                    act.wait_ge(pv_done, n - 2)
                act.activation(probs[0:rows_of(c), n % 3, :], ringB[n % 2][0:rows_of(c), :], ACT.Exp,
                               scale=DK ** -0.5).then_inc(exp_done, 1)

            def high_part(i):
                slot = (i + 2) % SLOTS
                act.wait_ge(w_in[slot], 32 * (i // SLOTS + 1))
                act.activation(piece_of(i, 0), staged(i), ACT.Copy).then_inc(w_hi_done, 1)

            turned("x", 0)
            queries_hi(0)
            act.wait_ge(values_filled, 1)
            for n in range(2):
                here = ringB[1][:, 2 * n * SKP:2 * (n + 1) * SKP].rearrange("p (b k) -> p b k", k=SKP)[:, :, 0:SK]
                act.activation(values3[n].rearrange("p b (r k) -> p b r k", r=3), spread(here, 2, 3), ACT.Identity,
                               bias=pl[:, BV:BV + 1]).then_inc(values3_done, 1)
            turned("x", 1)
            shift_in(0)
            def second_attention(c):
                n = {1: 0, 3: 1, 7: 2}.get(c)
                if n is not None:
                    act.wait_ge(k1_filled, n + 1 + n // 2)
                    act.activation((k1, a1, kt[:, :])[n], ringA[(0, 1, 1)[n]][:, 0:B * SKP], ACT.Identity,
                                   bias=pl[:, BK1:BK1 + 1] if n == 0 else 0.0).then_inc(k1_copied, 1)

            for b in range(B):
                for c in range(NC):
                    exps(b, c)
                    if b == B - 1:
                        second_attention(c)
                    if c == 0 and b + 1 < B:
                        queries_hi(b + 1)
                    if c == 3 and b >= 1:
                        turned("o", b - 1)
                    if c == 6 and b + 2 < B:
                        turned("x", b + 2)
                    if b >= 1 and c == Y_AT[b]:
                        turned("y", b - 1)
                    if c == 8 and b + 1 < B:
                        shift_in(b + 1)
                    if c in (1, 4):
                        high_part(2 * b + c // 4)
            for n, kind in enumerate("oy"):
                act.wait_ge(t0_filled, t0(kind, B - 1) + 1)
                act.activation(TF[:, 2, 0:S // 2], T0[:, 0:S // 2], ACT.Copy).then_inc(t0_copied, 1)
                act.wait_ge(turned2, n + 1)
                act.activation(TF[:, 2, S // 2:], (ringB[0], ringA[0])[n][:, 0:S // 2], ACT.Copy).then_inc(copied2, 1)

            act.wait_ge(picked, 2)
            act.activation(et[:, :], et[:, :], ACT.Exp).then_inc(wexp_done, 1)
            act.activation(early_use[:, 0:1], pl[0:1, IDN:IDN + 1], ACT.Silu)

            def xt_high(i, k):
                s, u = 4 * i + k, k % 2
                act.wait_ge(xt_filled, s + 1)
                if k >= 2:
                    act.wait_ge(up_filled, s - 1)
                act.activation(XT_hi[:, u * P:(u + 1) * P], T0[:, 0:P], ACT.Copy).then_inc(xt_hi, 1)

            def silu(i, k):
                s, u = 4 * i + k, k % 2
                act.wait_ge(gate_filled, s + 1)
                if k >= 2:
                    act.wait_ge(h_done, s - 1)
                act.activation(SG[:, u, :], ringA[u][:, :], ACT.Silu).then_inc(silu_done, 1)

            def ht_copy(i, k):
                s, u = 4 * i + k, k % 2
                act.wait_ge(ht_filled, s + 1)
                if k >= 2:
                    act.wait_ge(y_filled, s - 1)
                act.activation(TF[:, 1 + u, :], accs[u][:, :], ACT.Copy).then_inc(ht_ready, 1)

            def step(i, k):
                if 1 <= k <= ST:
                    ht_copy(i, k - 1)
                if k < ST:
                    silu(i, k)
                if k + 1 < ST:
                    xt_high(i, k + 1)

            xt_high(0, 0)
            for k in range(HEAD):
                step(0, k)
            with act.Fori(0, LOOPS) as i:
                for u in range(SLOTS):
                    step(i, HEAD + u)
            for k in range(HEAD + SLOTS * LOOPS, ST + 2):
                step(0, k)
            act.activation(early_use[:, 1:2], pl[0:1, IDN:IDN + 1], ACT.Exp)

            def part(n):
                kind, b = T_JOBS[n]
                rows_ = {"x": P, "p": SK, "y": P, "z": E * R}[kind]
                act.wait_ge(f_filled, n + 1)
                act.activation(TF[0:rows_, n % 3, :], (T0, T1)[n % 2][0:rows_, :], ACT.Copy).then_inc(f_copied, 1)

            def exp1(b):
                act.wait_ge(negmax1_done, b + 1)
                for t in range(b * TB, (b + 1) * TB):
                    ins = act.activation(P1[:, t, 0:SK], P1[:, t, 0:SK], ACT.Exp, bias=nm1[:, t:t + 1],
                                         scale=D ** -0.5, accum_out=sum1[:, t:t + 1])
                ins.then_inc(p1_done, 1)

            def gate_exps(b):
                act.wait_ge(gate_in, b + 1)
                act.activation(gl[:, b % 2, :, :], gl[:, b % 2, :, :], ACT.Exp).then_inc(gate_exp, 1)

            for what in ACT_END:
                if isinstance(what, int):
                    part(what)
                elif what[0] == "e":
                    exp1(int(what[1]))
                else:
                    gate_exps(int(what[1]))

        @block.vector
        def _(dve):
            steps = [0]

            def then(ins):
                steps[0] += 1
                ins.then_inc(dve_step, 1)
                dve.wait_ge(dve_step, steps[0])

            def norm_stats(n):
                b = n % B
                if n:
                    dve.wait_ge(ln_stats, n)
                for t in range(TB):
                    ins = dve.bn_stats(stats[:, t, :], X[:, b * TB + t, :])
                then(ins)
                for t in range(TB):
                    ins = dve.bn_aggr(mv[:, n, t, :], stats[:, t, :])
                ins.then_inc(ln_stats, 1)

            def norm(n, slot):
                b = n % B
                dve.wait_ge(ln_rstd, n + 1)
                for t in range(TB):
                    ins = dve.tensor_scalar(XN[:, slot, t, :], X[:, b * TB + t, :], mv[:, n, t, 0:1],
                                            rstd[:, n, t:t + 1], ALU.subtract, ALU.mult)
                ins.then_inc(ln_done, 1)

            dve.wait_ge(x_in[0], 16)
            norm_stats(0)
            def second_parts(n, out, src, high):
                dve.wait_ge(split_hi, n)
                dve.tensor_tensor(out, src, high.bitcast(F32), ALU.subtract).then_inc(split_done, 1)

            def keys_half(b, n):
                if b >= 2:
                    dve.wait_ge(b_filled, NC * (b - 2) + NH * (n + 1))
                if b == 0:
                    dve.wait_ge(keys_hi_done, n + 1)
                dve.tensor_tensor(KA[:, b % 2, n, :, :], spread(keys2[:, n, b, 0:SK].bitcast(F32), 1, HALF),
                                  spread(own, 2, SK), ALU.mult).then_inc(ka_done, 1)

            second_parts(1, early_lo[:, 0:WQD], raw[:, 0:WQD], early_hi[:, 0:WQD])
            second_parts(2, ctx_lo, pl[:, CTX:CTX + B * SKP], ctx_hi)
            norm(0, 0)
            second_parts(3, early_lo[:, WQD:], raw[:, WQD:], early_hi[:, WQD:])
            dve.wait_ge(mask_in, 32)
            dve.tensor_scalar(keept, maskt, 0, None, ALU.not_equal).then_inc(keep_done, 1)
            dve.tensor_scalar(padk[:, :], padi[:, :], 0, None, ALU.not_equal).then_inc(keep_done, 1)
            dve.tensor_scalar(maskz, maskt, 0, HARD, ALU.is_equal, ALU.mult)
            dve.tensor_scalar(padf[:, 0, :], padi[:, :], 0, HARD, ALU.is_equal, ALU.mult).then_inc(pad_done, 1)
            dve.wait_ge(pad_done, 1)
            dve.wait_ge(ones_done, 1)
            dve.wait_ge(keys_hi_done, 3)
            dve.scalar_tensor_tensor(out=keys_lo.rearrange("p b k -> p (b k)"), in0=T1[:, 0:B * SKP],
                                     scalar=pl[:, BK + 2:BK + 3], in1=keys_hi.rearrange("p b k -> p (b k)").bitcast(F32),
                                     op0=ALU.add, op1=ALU.subtract).then_inc(keys_lo_done, 1)
            def x_lo(b):
                dve.wait_ge(t0_copied, t0("x", b) + 1)
                dve.tensor_tensor(T_lo[:, :], T0[:, :], T_hi[:, :].bitcast(F32), ALU.subtract).then_inc(x_lo_done, 1)

            x_lo(0)
            keys_half(0, 0)
            keys_half(0, 1)
            dve.tensor_scalar(Z[0:SK, 0, :], maskz, padf[:, 0, 0:1], None, ALU.add).then_inc(z_done, 1)

            def queries_lo(b):
                for n in range(2):
                    job = a_job("queries", b, n)
                    rows_ = slice(P // 2 * (1 - n), P // 2 * (2 - n))
                    dve.wait_ge(a_hi, 2 * b + n + 1)
                    dve.scalar_tensor_tensor(out=QA[rows_, b % 2, n, :], in0=ringA[job % 2][rows_, :],
                                             scalar=pl[rows_, BQ + n:BQ + n + 1], in1=QA[rows_, b % 2, n, :].bitcast(F32),
                                             op0=ALU.add, op1=ALU.subtract).then_inc(a_freed, 1)

            def row_max(b, n):
                t, h0 = n // (H // GH), n % (H // GH) * GH
                job = a_job("max", b, n)
                dve.wait_ge(a_filled, job + 1)
                dve.tensor_reduce(negmax[:, t, h0:h0 + GH], ringA[job % 2][:, 0:GH * SK].rearrange("p (h k) -> p h k", k=SK),
                                  AX_X, ALU.max, negate=True).then_inc(a_freed, 1)

            def shift_out(b):
                dve.wait_ge(a_freed, a_job("max", b, UNITS - 1) + 1)
                if b >= 1:
                    dve.wait_ge(t1_filled, t1("shift", b - 1) + 1)
                then(dve.tensor_copy(shift[:, :, 0:H], negmax[:, :, :]))
                dve.tensor_tensor(shift[:, :, H:2 * H], negmax[:, :, :], shift[:, :, 0:H], ALU.subtract).then_inc(shift_done, 1)

            def values(b):
                dve.wait_ge(v_filled, b + 1)
                block_mask = pl[0:CH, BLK:BLK + 3 * NC].rearrange("p (u c h) -> p u c h", u=2, h=3)
                for c in range(NH):
                    src = accs[b % 2][0:CH, c * D:(c + 1) * D] if c < NH - 1 else ringB[0][0:CH, b * D:(b + 1) * D]
                    h = first_head(c)
                    dve.tensor_tensor(vblk[0:CH, b, c:NC:NH, :].rearrange("p u (h j) -> p u h j", j=OC)[:, :, :, 0:DK],
                                      src.rearrange("p (u h j) -> p u h j", u=2, j=DK)[:, :, h:h + 3, :],
                                      spread(block_mask[:, :, c, :], 3, DK), ALU.mult)
                dve.tensor_copy(vblk[0:CH, b, :, :].rearrange("p c (h j) -> p (c h) j", j=OC)[:, :, DK],
                                pl[0:CH, BLK:BLK + 3 * NC]).then_inc(v_done, 1)

            queries_lo(0)
            dve.wait_ge(t1_filled, t1("flags", 0) + 1)
            then(dve.tensor_scalar(flags[:, :].rearrange("p (b t) -> p t b", t=TB),
                                   T1[:, 0:NT].rearrange("p (t b) -> p t b", b=B), 0.0, 3e38, ALU.is_equal, ALU.mult))
            then(dve.tensor_scalar(flag2[:, :], flags[:, :], 1e10, None, ALU.mult))
            dve.tensor_tensor(flags[:, :], flag2[:, :], flag2[:, :], ALU.subtract).then_inc(t1_freed, 1)
            dve.wait_ge(tables_in, 16)
            for n in range(UNITS):
                row_max(0, n)
                if n % (UNITS // B) == UNITS // B - 1:
                    values(n // (UNITS // B))
                if n == 1:
                    dve.wait_ge(x_in[1], 16)
                    norm_stats(1)
                if n == 5:
                    dve.wait_ge(t0_filled, t0("x", 0) + 1)
                    norm(1, 0)
                if n == 9:
                    x_lo(1)
            shift_out(0)

            def context(b):
                dve.wait_ge(pv_done, NC * (b + 1))
                halves = [accs[u][:, 0:2 * H * OC].rearrange("p (t h j) -> p t h j", t=2, j=OC) for u in range(2)]
                dve.reciprocal(rsum[:, 0:2, :], halves[0][:, :, :, DK])
                then(dve.reciprocal(rsum[:, 2:4, :], halves[1][:, :, :, DK]))
                if b >= 1:
                    dve.wait_ge(t0_filled, t0("o", b - 1) + 1)
                for t in range(TB):
                    ins = dve.tensor_tensor(O[:, t, :].rearrange("p (h j) -> p h j", j=DK), halves[t // 2][:, t % 2, :, 0:DK],
                                            spread(rsum[:, t, :], 2, DK), ALU.mult)
                ins.then_inc(o_done, 1)

            def add_attention(b):
                here = X[:, b * TB:(b + 1) * TB, :]
                dve.wait_ge(t1_filled, t1("wo", b) + 1)
                dve.wait_ge(pool_x, b + 1)
                dve.tensor_tensor(here, here, T1[:, :].rearrange("p (t d) -> p t d", t=TB), ALU.add).then_inc(t1_freed, 1)
                dve.wait_ge(t1_freed, t1("wo", b) + 1)
                norm_stats(B + b)

            def norm_for_experts(b):
                if b >= 1:
                    dve.wait_ge(normed_out, 16 * b)
                norm(B + b, 1)

            def take_logits(b):
                dve.wait_ge(t1_filled, t1("logits", b) + 1)
                dve.tensor_copy(L[:, b * TB:(b + 1) * TB, :], T1[:, 0:TB * E].rearrange("p (t e) -> p t e", e=E))\
                   .then_inc(t1_freed, 1)

            def pick():
                falling = spread(pl[:, WDS:WDS + E], 1, NT)
                dve.wait_ge(t1_freed, len(T1_USES))
                for k in range(TOPK):
                    src = (L, L2)[k][:, :, :]
                    then(dve.tensor_reduce(m12[:, k, :], src, AX_X, ALU.max))
                    then(dve.tensor_tensor(L3[:, :, :], src, spread(m12[:, k, :], 2, E), ALU.is_equal))
                    then(dve.tensor_tensor(L3[:, :, :], L3[:, :, :], falling, ALU.mult))
                    then(dve.tensor_reduce(mx[:, k, :], L3[:, :, :], AX_X, ALU.max))
                    then(dve.tensor_tensor(oh[:, k, :, :], falling, spread(mx[:, k, :], 2, E), ALU.is_equal))
                    if k == 0:
                        then(dve.scalar_tensor_tensor(out=L2[:, :, :], in0=oh[:, 0, :, :], scalar=HARD, in1=L[:, :, :],
                                                      op0=ALU.mult, op1=ALU.add))
                dve.tensor_tensor(cnt[:, :, :], oh[:, 0, :, :], oh[:, 1, :, :], ALU.add).then_inc(picked, 1)
                dve.tensor_tensor(et[:, :], m12[:, 1, :], m12[:, 0, :], ALU.subtract).then_inc(picked, 1)

            def second_attention(c):
                if c == 0:
                    dve.tensor_scalar(bq1, ident, 0.0, pl[:, BQ1C:BQ1C + 1], ALU.mult, ALU.add).then_inc(bq1_done, 1)
                    dve.tensor_scalar(lb, pl[0:E * R, LB:LB + D], 2.0, None, ALU.mult).then_inc(lb_done, 1)
                if c == 6:
                    dve.wait_ge(k1_filled, 3)
                    dve.tensor_tensor(v1.rearrange("p (b d) -> p b d", d=D), ringA[0][0:SK, :].rearrange("p (b d) -> p b d", d=D),
                                      spread(rw[0:SK, BV1:BV1 + D], 1, B), ALU.add).then_inc(v1_done, 1)

            for b in range(B):
                for c in range(NC):
                    if b == B - 1:
                        second_attention(c)
                    if c == 0:
                        if b + 1 < B:
                            if b >= 1:
                                keys_half(b + 1, 1)
                            queries_lo(b + 1)
                    if b + 1 < B:
                        for n in UNITS_AT[c]:
                            row_max(b + 1, n)
                        if c == 7:
                            shift_out(b + 1)
                    if c == 1 and b >= 1:
                        context(b - 1)
                    if b == 0 and c in (1, 5):
                        n = 2 + c // 5
                        dve.wait_ge(x_in[n], 16)
                        norm_stats(n)
                    if (b, c - 1) in LOGITS_AT:
                        take_logits(LOGITS_AT[b, c - 1])
                    if c == 4 and b + 2 < B:
                        norm(b + 2, 0)
                    if b >= 1 and c == 5:
                        add_attention(b - 1)
                    if c == 6 and b + 2 < B:
                        keys_half(b + 2, 0)
                    if c == 7:
                        if b + 2 < B:
                            x_lo(b + 2)
                        if b >= 1:
                            norm_for_experts(b - 1)
            take_logits(B - 2)
            for n in range(2):
                part = accs[n][:, 0:2 * H * OC].rearrange("p (t h j) -> p t h j", t=2, j=OC)
                if n == 0:
                    dve.wait_ge(pv_half, 1)
                else:
                    dve.wait_ge(pv_done, NC * B)
                then(dve.reciprocal(rsum[:, 2 * n:2 * n + 2, :], part[:, :, :, DK]))
                for t in half_tiles(n)[0]:
                    ins = dve.tensor_tensor(O[:, t, :].rearrange("p (h j) -> p h j", j=DK), part[:, t % 2, :, 0:DK],
                                            spread(rsum[:, t, :], 2, DK), ALU.mult)
                ins.then_inc((o_half, o_done)[n], 1)
            for n in range(2):
                tiles_, here = half_tiles(n)
                if n == 0:
                    dve.wait_ge(t1_filled, t1("wo", B - 1) + 1)
                    dve.wait_ge(pool_x, B)
                    dve.tensor_tensor(X[:, here, :], X[:, here, :], T1[:, 0:2 * D].rearrange("p (t d) -> p t d", d=D),
                                      ALU.add).then_inc(t1_freed, 1)
                    dve.wait_ge(t1_freed, t1("wo", B - 1) + 1)
                else:
                    dve.wait_ge(projected2, 1)
                    then(dve.tensor_tensor(X[:, here, :], X[:, here, :],
                                           ringB[1][:, 0:2 * D].rearrange("p (t d) -> p t d", d=D), ALU.add))
                for t in tiles_:
                    ins = dve.bn_stats(stats[:, t, :], X[:, (B - 1) * TB + t, :])
                then(ins)
                for t in tiles_:
                    ins = dve.bn_aggr(mv[:, 2 * B - 1, t, :], stats[:, t, :])
                ins.then_inc((stats_half, ln_stats)[n], 1)
            dve.wait_ge(normed_out, 16 * (B - 1))
            dve.wait_ge(stats_half, 1)
            dve.wait_ge(ln_stats, 2 * B)
            for n in range(2):
                if n == 0:
                    dve.wait_ge(rstd_half, 1)
                else:
                    dve.wait_ge(ln_rstd, 2 * B)
                for t in half_tiles(n)[0]:
                    ins = dve.tensor_scalar(XN[:, 1, t, :], X[:, (B - 1) * TB + t, :], mv[:, 2 * B - 1, t, 0:1],
                                            rstd[:, 2 * B - 1, t:t + 1], ALU.subtract, ALU.mult)
                ins.then_inc((norm_half, ln_done)[n], 1)
            dve.wait_ge(t1_filled, t1("logits", B - 1) + 1)
            dve.tensor_copy(L[:, half_tiles(0)[1], :], T1[:, 0:2 * E].rearrange("p (t e) -> p t e", e=E)).then_inc(t1_freed, 1)
            dve.wait_ge(logits2, 1)
            then(dve.tensor_copy(L[:, half_tiles(1)[1], :], ringA[1][:, 0:2 * E].rearrange("p (t e) -> p t e", e=E)))
            pick()

            dve.wait_ge(tab_in, 16)
            dve.wait_ge(rank_filled, 1)
            rank = T1[:, 0:NT * E].rearrange("p (t e) -> p t e", e=E)
            total = T1[:, NT * E:NT * E + E]
            then(dve.tensor_tensor(cmp16[:, :, :], spread(total, 2, 16), spread(pl[:, M128:M128 + 16], 1, E), ALU.is_gt))
            then(dve.tensor_reduce(tiles[:, 0, :], cmp16[:, :, :], AX_X, ALU.add))
            then(dve.tensor_tensor(cmp8[:, :, :], spread(tiles[:, 0, :], 1, E),
                                   pl[:, LT8:LT8 + E * E].rearrange("p (e f) -> p e f", f=E), ALU.mult))
            then(dve.tensor_reduce(tiles[:, 1, :], cmp8[:, :, :], AX_X, ALU.add))
            then(dve.scalar_tensor_tensor(out=pos[:, 0, :, :], in0=spread(tiles[:, 1, :], 1, NT), scalar=float(P),
                                          in1=rank, op0=ALU.mult, op1=ALU.add))
            then(dve.tensor_tensor(pos[:, 1, :, :], pos[:, 0, :, :], oh[:, 1, :, :], ALU.mult))
            then(dve.tensor_tensor(pos[:, 0, :, :], pos[:, 0, :, :], oh[:, 0, :, :], ALU.mult))
            then(dve.tensor_reduce(slot[:, :, :], pos[:, :, :, :], AX_X, ALU.add))
            then(dve.tensor_scalar(mx[:, :, :], mx[:, :, :], 0.0, float(P * P), ALU.is_equal, ALU.mult))
            then(dve.tensor_tensor(sloti[:, 0, :, :], slot[:, :, :], mx[:, :, :], ALU.add))
            dve.tensor_scalar(sloti[:, 1, :, :], sloti[:, 0, :, :], 7, None, ALU.logical_shift_right)
            then(dve.tensor_scalar(sloti[:, 2, :, :], sloti[:, 0, :, :], P - 1, None, ALU.bitwise_and))
            dve.tensor_copy(tile_row[:, :, :, :], sloti[:, 1:3, :, :]).then_inc(rows_found, 1)
            dve.wait_ge(rows_found, 1)
            tile_of = tile_row[:, 0, :, :].rearrange("p k t -> p (k t)")
            then(dve.tensor_tensor(where[:, 2, :, :], spread(tab[:, IOT:IOT + ST], 1, TOPK * NT),
                                   spread(tile_of, 2, ST), ALU.is_equal))
            dve.tensor_tensor(where[:, 0, :, :], where[:, 2, :, :], spread(pl[:, TIDX:TIDX + TOPK * NT], 2, ST), ALU.mult)
            dve.tensor_scalar(where[:, 1, :, :], where[:, 2, :, :], pl[:, PCOL:PCOL + 1], None, ALU.mult)\
               .then_inc(where_done, 1)
            for q in range(POOL_ROWS, TOPK * NT):
                dve.tensor_scalar(onehot[:, q, :], tab[:, IOP:IOP + P], row_of[:, q:q + 1], None, ALU.is_equal)\
                   .then_inc(onehot_done, 1)
            dve.wait_ge(inverse_filled, 1)
            then(dve.tensor_copy(inv[:, 0:3 * ST], T1[:, 0:3 * ST]))
            spare = pl[:, SPARE:SPARE + ST]
            dve.tensor_tensor(inv[:, 3 * ST:4 * ST], inv[:, 2 * ST:3 * ST], spare, ALU.mult)
            then(dve.scalar_tensor_tensor(out=inv[:, 0:ST], in0=inv[:, 0:ST], scalar=float(P), in1=inv[:, ST:2 * ST],
                                          op0=ALU.mult, op1=ALU.add))
            then(dve.tensor_copy(gidx[:, :], inv[:, 0:ST]))
            then(dve.tensor_tensor(inv[:, ST:2 * ST], spare, inv[:, 3 * ST:4 * ST], ALU.subtract))
            dve.tensor_tensor(didx[:, :], inv[:, 0:ST], inv[:, ST:2 * ST], ALU.add)
            dve.tensor_scalar(gidx[:, :], gidx[:, :], TOK - 1, None, ALU.bitwise_and).then_inc(index_done, 1)

            then(dve.tensor_tensor(tiles[:, 0, :], tiles[:, 0, :], tiles[:, 1, :], ALU.add))
            then(dve.tensor_tensor(cmpt[0:1, :, :], spread(tiles[0:1, 0, :], 1, ST), spread(tab[0:1, IOT:IOT + ST], 2, E),
                                   ALU.is_le))
            then(dve.tensor_reduce(etf[0:1, :], cmpt[0:1, :, :], AX_X, ALU.add))
            dve.tensor_scalar(etab[0:1, :], etf[0:1, :], float(E - 1), None, ALU.min).then_inc(experts_done, 1)

            dve.wait_ge(wexp_done, 1)
            then(dve.tensor_scalar(wts[:, 0, :], et[:, :], 1.0, None, ALU.add))
            then(dve.reciprocal(wts[:, 0, :], wts[:, 0, :]))
            dve.tensor_tensor(wts[:, 1, :], et[:, :], wts[:, 0, :], ALU.mult).then_inc(weights_done, 1)

            def xt_low(i, k):
                s, u = 4 * i + k, k % 2
                dve.wait_ge(xt_hi, s + 1)
                dve.tensor_tensor(XT_lo[:, u * P:(u + 1) * P], T0[:, 0:P], XT_hi[:, u * P:(u + 1) * P].bitcast(F32),
                                  ALU.subtract).then_inc(xt_ready, 1)

            def hidden(i, k):
                s, u = 4 * i + k, k % 2
                dve.wait_ge(silu_done, s + 1)
                dve.wait_ge(up_filled, s + 1)
                if k >= 2:
                    dve.wait_ge(ht_filled, s - 1)
                dve.tensor_tensor(HH[:, u, :], SG[:, u, :], ringB[u][:, :], ALU.mult).then_inc(h_done, 1)

            def results(i, k):
                s, n = 4 * i + k, k % SLOTS
                dve.wait_ge(y_filled, s + 1)
                if k >= SLOTS or not isinstance(i, int):
                    dve.wait_ge(scattered[n], 16 * (i + k // SLOTS))
                dve.tensor_copy(Y[:, n, :], T1[:, 0:D]).then_inc(y_copied, 1)

            def step(i, k):
                if k >= 3:
                    results(i, k - 3)
                if k < ST:
                    hidden(i, k)
                if k + 1 < ST:
                    xt_low(i, k + 1)

            xt_low(0, 0)
            for k in range(HEAD):
                step(0, k)
            with dve.Fori(0, LOOPS) as i:
                for u in range(SLOTS):
                    step(i, HEAD + u)
            for k in range(HEAD + SLOTS * LOOPS, ST + 3):
                step(0, k)

            def combine(b):
                last = b == B - 1
                dve.wait_ge(expert_in[b], 16 if last else 32)
                if last:
                    dve.wait_ge(first_added, 1)
                for k in range(1 if last else 0, TOPK):
                    for t in range(b * TB, (b + 1) * TB):
                        ins = dve.scalar_tensor_tensor(out=X[:, t, :], in0=yk[:, k, t, :], scalar=wts[:, k, t:t + 1],
                                                       in1=X[:, t, :], op0=ALU.mult, op1=ALU.add)
                    then(ins)
                norm_stats(2 * B + b)

            def norm3(b):
                if b >= 2:
                    dve.wait_ge(f_filled, T_JOBS.index(("x", b - 2)) + 1)
                norm(2 * B + b, b % 2)

            def norm4(b):
                dve.wait_ge(f_filled, T_JOBS.index(("y", b - 2) if b >= 2 else ("x", b + 2)) + 1)
                norm(3 * B + b, b % 2)

            def scores1(b):
                here = slice(b * TB, (b + 1) * TB)
                dve.wait_ge(sc_filled, b + 1)
                then(dve.tensor_tensor(P1[:, here, 0:SK], ringA[b % 2][:, 0:TB * SKP].rearrange("p (t k) -> p t k", k=SKP)[:, :, 0:SK],
                                       spread(kt[:, b * SKP:b * SKP + SK], 1, TB), ALU.add))
                then(dve.tensor_reduce(nm1[:, here], P1[:, here, 0:SK], AX_X, ALU.max, negate=True))
                dve.tensor_scalar(nm1[:, here], nm1[:, here], D ** -0.5, None, ALU.mult).then_inc(negmax1_done, 1)

            def attend1(b):
                here = slice(b * TB, (b + 1) * TB)
                dve.wait_ge(pv1_filled, b + 1)
                then(dve.reciprocal(sum1[:, here], sum1[:, here]))
                for t in range(TB):
                    ins = dve.scalar_tensor_tensor(out=X[:, b * TB + t, :], in0=ringB[b % 2][:, t * D:(t + 1) * D],
                                                   scalar=sum1[:, b * TB + t:b * TB + t + 1], in1=X[:, b * TB + t, :],
                                                   op0=ALU.mult, op1=ALU.add)
                then(ins)
                norm_stats(3 * B + b)

            def fused(b, u):
                return (accs, ringA, ringB, accs)[b][u][:, 0:2 * FBW].rearrange("p (t j) -> p t j", t=2)

            def softmax(b):
                u = b % 2
                dve.wait_ge(fb_filled, b + 1)
                for n in range(2):
                    ins = dve.tensor_tensor(gl[:, u, 2 * n:2 * n + 2, :], fused(b, n)[:, :, D:D + E],
                                            spread(rw[:, RB1:RB1 + E], 1, 2), ALU.add)
                then(ins)
                then(dve.tensor_reduce(gm[:, :], gl[:, u, :, :], AX_X, ALU.max, negate=True))
                dve.tensor_tensor(gl[:, u, :, :], gl[:, u, :, :], spread(gm[:, :], 2, E), ALU.add).then_inc(gate_in, 1)

            def outer(b):
                u = b % 2
                dve.wait_ge(gate_exp, b + 1)
                then(dve.tensor_reduce(gm[:, :], gl[:, u, :, :], AX_X, ALU.add))
                then(dve.reciprocal(gm[:, :], gm[:, :]))
                then(dve.tensor_tensor(gates[:, :, :], gl[:, u, :, :], spread(gm[:, :], 2, E), ALU.mult))
                for t in range(TB):
                    mid = fused(b, t // 2)[:, t % 2, D + E:D + E + R]
                    ins = dve.tensor_tensor(pairs[:, u, t, :].rearrange("p (e r) -> p e r", r=R), spread(mid, 1, E),
                                            spread(gates[:, t, :], 2, R), ALU.mult)
                ins.then_inc(outer_done, 1)

            def finish(b):
                dve.wait_ge(lora_filled, b + 1)
                dve.wait_ge(pool_x, B + b + 1)
                for n in range(2):
                    here = X[:, b * TB + 2 * n:b * TB + 2 * n + 2, :]
                    ins = dve.tensor_tensor(here, here, fused(b, n)[:, :, 0:D], ALU.add)
                ins.then_inc(result_done, 1)

            todo = {"c": combine, "n": norm3, "s": scores1, "a": attend1, "m": norm4, "g": softmax, "o": outer,
                    "f": finish}
            for what in DVE_END:
                todo[what[0]](int(what[1]))

        @block.tensor
        def _(pe):
            def three(where_, left, right, start=True, stop=True):
                (lh, ll), (rh, rl) = left, right
                pe.matmul(where_, lh, rh, start=start, stop=False, skip_group_check=True)
                pe.matmul(where_, lh, rl, start=False, stop=False, skip_group_check=True)
                return pe.matmul(where_, ll, rh, start=False, stop=stop, skip_group_check=True)

            context_keys = ctx_hi, ctx_lo

            def t1_free(kind, b):
                if t1(kind, b):
                    pe.wait_ge(t1_freed, t1(kind, b))

            for n in range(3):
                if n == 0:
                    pe.wait_ge(split_done, 2)
                at = slice(WKD + n * P, WKD + (n + 1) * P)
                three((ringB[0], ringB[1], T1)[n][:, 0:B * SKP], (early_hi[:, at], early_lo[:, at]), context_keys)\
                    .then_inc(keys_filled, 1)

            def queries(b):
                pe.wait_ge(split_done, 3)
                pe.wait_ge(x_lo_done, b + 1)
                for n in range(2):
                    job = a_job("queries", b, n)
                    if job >= 2:
                        pe.wait_ge(a_freed, job - 1)
                    at = slice(WQD + n * P, WQD + (n + 1) * P)
                    three(ringA[job % 2][:, :], (early_hi[:, at], early_lo[:, at]), (T_hi[:, :], T_lo[:, :]))\
                        .then_inc(a_filled, 1)

            def turn(kind, b, src):
                n = t0(kind, b)
                if n:
                    pe.wait_ge(t0_copied, n)
                    before, b_before = T0_USES[n - 1]
                    if before == "x":
                        pe.wait_ge(x_lo_done, b_before + 1)
                for t in range(TB):
                    ins = pe.transpose(T0[:, t * P:(t + 1) * P], src[:, t, :], ident)
                ins.then_inc(t0_filled, 1)

            def turn_x(b):
                pe.wait_ge(ln_done, b + 1)
                turn("x", b, XN[:, 0, :, :])

            def max_scores(b, n):
                t, h0 = n // (H // GH), n % (H // GH) * GH
                job = a_job("max", b, n)
                half = h0 // HALF
                rows_ = slice(P // 2 * half, P // 2 * (half + 1))
                if n == 0:
                    pe.wait_ge(a_hi, 2 * b + 2)
                    pe.wait_ge(ka_done, 2 * b + 2)
                    if b >= 1:
                        pe.wait_ge(z_pool, b)
                pe.wait_ge(a_freed, job - 1)
                o = ringA[job % 2][:, 0:GH * SK]
                keys = KA[rows_, b % 2, half, h0 % HALF:h0 % HALF + GH, :].rearrange("p h k -> p (h k)")
                pe.matmul(o, QA[rows_, b % 2, half, t * P:(t + 1) * P], keys, start=True, stop=False)
                pe.matmul(o, Z[0:96, b, t * P:(t + 1) * P], sel[0:96, h0 * SK:(h0 + GH) * SK], start=False, stop=True)\
                    .then_inc(a_filled, 1)

            def turn_shift(b):
                t1_free("shift", b)
                pe.wait_ge(shift_done, b + 1)
                for t in range(TB):
                    ins = pe.transpose(T1[0:2 * H, t * P // 2:(t + 1) * P // 2].bitcast(BF16), shift[:, t, :], ident_bf[:, :])
                ins.then_inc(t1_filled, 1)

            def pair_scores(b, c):
                n, m = NC * b + c, rows_of(c)
                if c == 0:
                    pe.wait_ge(v_done, B)
                    pe.wait_ge(a_freed, a_job("queries", b, 1) + 1)
                    pe.wait_ge(kb_done, b + 1)
                    pe.wait_ge(t1_freed, t1("shift", b) + 1)
                if n >= 2:
                    pe.wait_ge(exp_done, n - 1)
                u, at, half = b % 2, c % NH * CH, c // NH
                rows_ = slice(P // 2 * half, P // 2 * (half + 1))
                o = ringB[n % 2][0:m, :]
                first = KA[:, u, half, :, :].rearrange("p h k -> p (h k)")[:, at:at + m]
                second = KB[rows_, u, :, :].rearrange("p h k -> p (h k)")[:, at:at + m]
                pe.matmul(o, first, QA[:, u, half, :], start=True, stop=False, skip_group_check=True)
                pe.matmul(o, second, QA[rows_, u, half, :], start=False, stop=False, skip_group_check=True)
                pe.matmul(o, sel[:, pair_at(c):pair_at(c) + m], Z[:, b, :], start=False, stop=True,
                          skip_group_check=True).then_inc(b_filled, 1)

            def weigh(b, c):
                n, m = NC * b + c, rows_of(c)
                pe.wait_ge(exp_done, n + 1)
                if c == 0:
                    if b >= 1:
                        pe.wait_ge(o_done, b)
                for t in range(TB):
                    a = (t % 2) * H * OC + first_head(c) * OC
                    ins = pe.matmul(accs[t // 2][:, a:a + 3 * OC], probs[0:m, n % 3, t * P:(t + 1) * P], vblk[0:m, b, c, :],
                                    start=(c == 0 and t % 2 == 0), stop=(c == NC - 1), skip_group_check=True)
                    if (b, c, t) == (B - 1, NC - 1, 1):
                        ins.then_inc(pv_half, 1)
                ins.then_inc(pv_done, 1)

            def project(b):
                t1_free("wo", b)
                pe.wait_ge(t0_copied, t0("o", b) + 1)
                pe.wait_ge(late_in, 16)
                for t in range(TB):
                    at = slice(t * P, (t + 1) * P)
                    ins = pe.matmul(T1[:, at], TF[:, 2, at], pl[:, WO0:WO0 + D], start=True, stop=True)
                ins.then_inc(t1_filled, 1)

            def turn_o(b):
                pe.wait_ge(o_done, b + 1)
                turn("o", b, O)

            def turn_y(b):
                pe.wait_ge(ln_done, B + b + 1)
                turn("y", b, XN[:, 1, :, :])

            def route(b):
                t1_free("logits", b)
                pe.wait_ge(t0_copied, t0("y", b) + 1)
                for t in range(TB):
                    ins = pe.matmul(T1[:, t * E:(t + 1) * E], TF[:, 2, t * P:(t + 1) * P], pl[:, RT0:RT0 + E],
                                    start=True, stop=True)
                ins.then_inc(t1_filled, 1)

            pe.wait_ge(plain_in, 16)
            def second_attention(c):
                if c == 1:
                    pe.wait_ge(late_in, 16)
                    pe.wait_ge(a_freed, a_job("max", B - 1, UNITS - 1) + 1)
                    pe.matmul(ringA[0][:, 0:B * SKP], pl[:, WK1:WK1 + D], pl[:, CTX:CTX + B * SKP],
                              start=True, stop=True).then_inc(k1_filled, 1)
                if c == 3:
                    pe.wait_ge(k1_copied, 1)
                    pe.matmul(ringA[1][:, 0:B * SKP], pl[:, WQ1:WQ1 + D], k1, start=True, stop=True).then_inc(k1_filled, 1)
                if c == 5:
                    for b in range(B):
                        ins = pe.matmul(ringA[0][0:SK, b * D:(b + 1) * D], pl[:, CTX + b * SKP:CTX + b * SKP + SK],
                                        pl[:, WV1:WV1 + D], start=True, stop=True)
                    ins.then_inc(k1_filled, 1)
                if c == 7:
                    pe.wait_ge(k1_copied, 2)
                    pe.wait_ge(bq1_done, 1)
                    pe.matmul(ringA[1][:, 0:B * SKP], bq1, k1, start=True, stop=True).then_inc(k1_filled, 1)

            turn_x(0)
            queries(0)
            pe.wait_ge(keep_done, 2)
            pe.wait_ge(keys_lo_done, 1)
            for t in range(TB):
                ins = pe.matmul(T1[:, t * B:(t + 1) * B], keept[:, t * P:(t + 1) * P], padk[:, :], start=True, stop=True)
            ins.then_inc(t1_filled, 1)
            pe.wait_ge(z_done, 1)
            pe.wait_ge(sel_in, 16)

            three(ringB[1][:, 0:B * SKP], (early_hi[:, WV0:WV0 + D], early_lo[:, WV0:WV0 + D]), context_keys)\
                .then_inc(values_filled, 1)

            def turn_values(b):
                pe.wait_ge(values3_done, b // 2 + 1)
                if b >= 2:
                    pe.wait_ge(v_done, b - 1)
                for c in range(NH):
                    a = CH * c % SK
                    o = accs[b % 2][0:CH, c * D:(c + 1) * D] if c < NH - 1 else ringB[0][0:CH, b * D:(b + 1) * D]
                    ins = pe.transpose(o, values3[b // 2][:, b % 2, a:a + CH], ident)
                ins.then_inc(v_filled, 1)

            for n in range(UNITS):
                max_scores(0, n)
                if n % (UNITS // B) == UNITS // B - 2:
                    turn_values(n // (UNITS // B))
                if n == 8:
                    turn_x(1)
            pe.wait_ge(tab_in, 16)
            turn_shift(0)
            for b in range(B):
                for c in range(NC):
                    pair_scores(b, c)
                    if c == 0 and b + 1 < B:
                        queries(b + 1)
                    if b == B - 1:
                        second_attention(c)
                    if (b, c) in LOGITS_AT:
                        route(LOGITS_AT[b, c])
                    if b + 1 < B:
                        for n in UNITS_AT[c]:
                            max_scores(b + 1, n)
                    if b >= 1 and c == 3:
                        turn_o(b - 1)
                    if b >= 1 and c == 4:
                        project(b - 1)
                    if c == 6 and b + 2 < B:
                        turn_x(b + 2)
                    if b >= 1 and c == Y_AT[b]:
                        turn_y(b - 1)
                    if c == 8 and b + 1 < B:
                        turn_shift(b + 1)
                    if c >= 2:
                        weigh(b, c - 2)
                    elif 1 <= b < B - 1:
                        weigh(b - 1, NC + c - 2)
                    elif b == B - 1 and c == 0:
                        weigh(b - 1, NC - 2)
                        weigh(b - 1, NC - 1)
            weigh(B - 1, NC - 2)
            weigh(B - 1, NC - 1)
            last = NC * B
            for kind, src, bank_ in (("o", O, ringB[0]), ("y", XN[:, 1, :, :], ringA[0])):
                pe.wait_ge(t0_copied, t0(kind, B - 1))
                if kind == "o":
                    pe.wait_ge(o_half, 1)
                else:
                    pe.wait_ge(norm_half, 1)
                for t in range(2):
                    ins = pe.transpose(T0[:, t * P:(t + 1) * P], src[:, t, :], ident)
                ins.then_inc(t0_filled, 1)
                if kind == "o":
                    pe.wait_ge(exp_done, last)
                    pe.wait_ge(o_done, B)
                else:
                    pe.wait_ge(v1_done, 1)
                    pe.wait_ge(k1_copied, 3)
                    pe.wait_ge(ln_done, 2 * B)
                for t in range(2):
                    ins = pe.transpose(bank_[:, t * P:(t + 1) * P], src[:, 2 + t, :], ident)
                ins.then_inc(turned2, 1)
                n, wide, right = (D, D, pl[:, WO0:WO0 + D]) if kind == "o" else (E, E, pl[:, RT0:RT0 + E])
                use = "wo" if kind == "o" else "logits"
                t1_free(use, B - 1)
                pe.wait_ge(t0_copied, t0(kind, B - 1) + 1)
                for t in range(2):
                    ins = pe.matmul(T1[:, t * wide:(t + 1) * wide], TF[:, 2, t * P:(t + 1) * P], right, start=True, stop=True)
                ins.then_inc(t1_filled, 1)
                pe.wait_ge(copied2, 1 if kind == "o" else 2)
                out_ = ringB[1] if kind == "o" else ringA[1]
                for t in range(2):
                    ins = pe.matmul(out_[:, t * wide:(t + 1) * wide], TF[:, 2, (2 + t) * P:(3 + t) * P], right,
                                    start=True, stop=True)
                ins.then_inc(projected2 if kind == "o" else logits2, 1)

            pe.wait_ge(t1_freed, len(T1_USES))
            pe.wait_ge(picked, 1)
            ones = tab[:, ON:ON + P]
            pe.matmul(T1[:, 0:NT * E], tab[:, UT:UT + P], cnt[:, :, :].rearrange("p t e -> p (t e)"),
                      start=True, stop=False, skip_group_check=True)
            for t in range(NT - 1):
                pe.matmul(T1[:, (t + 1) * E:NT * E].rearrange("p (t e) -> p t e", e=E), ones,
                          spread(cnt[:, t, :], 1, NT - 1 - t), start=False, stop=(t == NT - 2), skip_group_check=True)
            for t in range(NT):
                ins = pe.matmul(T1[:, NT * E:NT * E + E], ones, cnt[:, t, :], start=False, stop=(t == NT - 1),
                                skip_group_check=True)
            ins.then_inc(rank_filled, 1)

            for q in range(TOPK * NT):
                if q == 0:
                    pe.wait_ge(where_done, 1)
                if q < POOL_ROWS:
                    pe.wait_ge(onehot_pool, q + 1)
                else:
                    pe.wait_ge(onehot_done, q - POOL_ROWS + 1)
                ins = pe.matmul(T1[:, 0:3 * ST].rearrange("p (v i) -> p v i", i=ST), onehot[:, q, :], where[:, :, q, :],
                                start=(q == 0), stop=(q == TOPK * NT - 1))
            ins.then_inc(inverse_filled, 1)

            def experts_of(i, k, n):
                _, e = nc.values_load_multi_w_load_instructions(
                    etab[0:1, bass.ds(4 * i + k, n)], engines=[mybir.EngineType.PE], min_val=0, max_val=E - 1,
                    skip_runtime_bounds_check_because="the table's numbers are cut at E - 1 and count from 0")
                return {k + m: e[m] for m in range(n)}

            def turn_tokens(i, k):
                n = k % SLOTS
                pe.wait_ge(gathered[n], 16 * (i + k // SLOTS + 1))
                pe.transpose(T0[:, 0:P], G[:, n, :], ident).then_inc(xt_filled, 1)

            def gate_up(i, k, e):
                s, u = 4 * i + k, k % 2
                pe.wait_ge(xt_ready, s + 1)
                high, low = XT_hi[:, u * P:(u + 1) * P], XT_lo[:, u * P:(u + 1) * P]
                for o, n, done in ((ringA[u], 0, gate_filled), (ringB[u], 2, up_filled)):
                    right = [gate_up_w[:, bass.ds(e * (4 * FF) + (n + part) * FF, FF)] for part in range(2)]
                    three(o[:, :], (high, low), right).then_inc(done, 1)

            def down(i, k, e):
                s, u = 4 * i + k, k % 2
                pe.wait_ge(ht_ready, s + 1)
                if k >= 1:
                    pe.wait_ge(y_copied, s)
                for c in range(FC):
                    ins = pe.matmul(T1[:, 0:D], TF[:, 1 + u, c * P:(c + 1) * P], down_w[:, bass.ds(e * FF + c * P, P)],
                                    start=(c == 0), stop=(c == FC - 1))
                ins.then_inc(y_filled, 1)

            def turn_hidden(i, k):
                s, u = 4 * i + k, k % 2
                pe.wait_ge(h_done, s + 1)
                for c in range(FC):
                    ins = pe.transpose(accs[u][:, c * P:(c + 1) * P], HH[:, u, c * P:(c + 1) * P], ident)
                ins.then_inc(ht_filled, 1)

            def step(i, k, e):
                if 1 <= k <= ST:
                    turn_hidden(i, k - 1)
                if k < ST:
                    gate_up(i, k, e[k])
                if k + 1 < ST:
                    turn_tokens(i, k + 1)
                if k >= 2:
                    down(i, k - 2, e[k - 2])

            pe.wait_ge(k1_copied, 3)
            pe.wait_ge(v1_done, 1)
            pe.wait_ge(lb_done, 1)
            pe.wait_ge(down_in, 16 * E)
            pe.wait_ge(w_lo_done, NW)
            pe.wait_ge(index_done, 1)
            pe.wait_ge(experts_done, 1)
            turn_tokens(0, 0)
            e = experts_of(0, 0, HEAD)
            for k in range(HEAD):
                step(0, k, e)
            with pe.Fori(0, LOOPS) as i:
                e = experts_of(i, HEAD - 2, SLOTS + 2)
                for u in range(SLOTS):
                    step(i, HEAD + u, e)
            rest = HEAD + SLOTS * LOOPS
            e = experts_of(0, rest - 2, ST - rest + 2)
            for k in range(rest, ST + 2):
                step(0, k, e)

            def part(n):
                kind, b = T_JOBS[n]
                if n >= 2:
                    pe.wait_ge(f_copied, n - 1)
                if kind == "x":
                    pe.wait_ge(ln_done, 2 * B + b + 1)
                elif kind == "p":
                    pe.wait_ge(p1_done, b + 1)
                elif kind == "y":
                    pe.wait_ge(ln_done, 3 * B + b + 1)
                else:
                    pe.wait_ge(outer_done, b + 1)
                for t in range(TB):
                    src = {"x": XN[:, b % 2, t, :], "p": P1[:, b * TB + t, 0:SK], "y": XN[:, b % 2, t, :],
                           "z": pairs[:, b % 2, t, :]}[kind]
                    ins = pe.transpose((T0, T1)[n % 2][0:src.shape[1], t * P:(t + 1) * P], src, ident)
                ins.then_inc(f_filled, 1)

            def turned(kind, b, t, rows_=P):
                n = T_JOBS.index((kind, b))
                return TF[0:rows_, n % 3, t * P:(t + 1) * P]

            def ready(kind, b):
                pe.wait_ge(f_copied, T_JOBS.index((kind, b)) + 1)

            def scores1(b):
                ready("x", b)
                if b >= 2:
                    pe.wait_ge(negmax1_done, b - 1)
                for t in range(TB):
                    ins = pe.matmul(ringA[b % 2][:, t * SKP:(t + 1) * SKP], turned("x", b, t), a1[:, b * SKP:(b + 1) * SKP],
                                    start=True, stop=True)
                ins.then_inc(sc_filled, 1)

            def values1(b):
                ready("p", b)
                if b >= 2:
                    pe.wait_ge(ln_stats, 3 * B + b - 1)
                for t in range(TB):
                    ins = pe.matmul(ringB[b % 2][:, t * D:(t + 1) * D], turned("p", b, t, SK), v1[:, b * D:(b + 1) * D],
                                    start=True, stop=True)
                ins.then_inc(pv1_filled, 1)

            def fused(b):
                ready("y", b)
                if b == 1:
                    pe.wait_ge(negmax1_done, B)
                elif b == 2:
                    pe.wait_ge(ln_stats, 4 * B)
                elif b == 3:
                    pe.wait_ge(result_done, 1)
                for t in range(TB):
                    bank_ = (accs, ringA, ringB, accs)[b][t // 2]
                    ins = pe.matmul(bank_[:, (t % 2) * FBW:(t % 2 + 1) * FBW], turned("y", b, t), pl[:, FB1:FB1 + FBW],
                                    start=(t % 2 == 0), stop=False, skip_group_check=True)
                ins.then_inc(fb_filled, 1)

            def lora(b):
                ready("z", b)
                for t in range(TB):
                    bank_ = (accs, ringA, ringB, accs)[b][t // 2]
                    ins = pe.matmul(bank_[:, (t % 2) * FBW:(t % 2) * FBW + D], turned("z", b, t, E * R), lb,
                                    start=False, stop=True, skip_group_check=True)
                ins.then_inc(lora_filled, 1)

            todo = {"s": scores1, "v": values1, "b": fused, "l": lora}
            for what in PE_END:
                if isinstance(what, int):
                    part(what)
                else:
                    todo[what[0]](int(what[1]))


def kernel(**inputs):
    import ml_dtypes
    import numpy as np
    import concourse.bacc as bacc
    from concourse.bass_utils import run_bass_kernel_spmd

    v = {k: np.asarray(a) for k, a in inputs.items()}
    f32, bf16 = np.float32, ml_dtypes.bfloat16
    i = np.arange(P)

    def pad(a):
        return np.concatenate([a, np.zeros((P - a.shape[0], a.shape[1]), a.dtype)], 0)

    ctx = np.zeros((D, B, SKP), f32)
    ctx[:, :, 0:SK] = v["ctx_1024"].transpose(2, 0, 1)
    wk, wq = v["L0_xattn_Wk"].T, v["L0_xattn_Wq"].T
    halves = [slice(0, D // 2)] * 2 + [slice(D // 2, D)] * 2
    early = np.concatenate([wk[:, h] for h in halves] + [wk] + [wq[:, h] for h in halves] + [v["L0_xattn_Wv"].T], 1)
    pair = np.arange(HK)
    block = np.zeros((P, NC, 3), f32)
    for c in range(NC):
        r = np.arange(rows_of(c))
        for n in range(3):
            block[r, c, n] = (pair_at(c) + r) // SK == first_head(c) + n
    own_head = (i[:, None] % (P // 2) // DK == np.arange(HALF)[None, :]).astype(f32)
    bk, bq = v["L0_xattn_bk"], v["L0_xattn_bq"]
    twice = [np.concatenate([a[h], a[h]])[:, None] for a in (bk, bq) for h in (halves[0], halves[2])]
    before = np.broadcast_to((np.arange(E)[None, :] < np.arange(E)[:, None]).astype(f32).reshape(1, E * E), (P, E * E))
    tile_index = np.broadcast_to(np.arange(TOPK * NT, dtype=f32), (P, TOPK * NT))
    falling = np.broadcast_to(E - np.arange(E, dtype=f32), (P, E))
    steps = np.broadcast_to(P * np.arange(16, dtype=f32), (P, 16))
    plain = np.concatenate([
        np.eye(P, dtype=f32), twice[0], twice[1], bk[:, None], twice[2], twice[3],
        v["L1_xattn_bk"][:, None], v["L1_xattn_bq"][:, None], v["L0_xattn_bv"][:, None], own_head, ctx.reshape(D, B * SKP),
        pad(v["L1_ffn_lora_B"].reshape(E * R, D)), block.reshape(P, 3 * NC), before, tile_index,
        i[:, None].astype(f32), (ROWS + i[:, None]).astype(f32), falling, steps,
        (ROWS + P * np.arange(ST)[None, :] + i[:, None]).astype(f32),
        v["L0_xattn_Wo"].T, v["L0_ffn_router_w"].T, v["L1_xattn_Wq"].T, v["L1_xattn_Wk"], v["L1_xattn_Wv"],
        v["L1_ffn_base_w"].T, v["L1_ffn_router_w"].T, v["L1_ffn_lora_A"]], 1)
    rows = np.concatenate([v["L0_xattn_bo"], v["L1_xattn_bv"], v["L1_ffn_base_b"], v["L1_ffn_router_b"]])[None, :]
    tables = np.concatenate([
        i[:, None] < i[None, :], np.ones((P, P)), np.broadcast_to(i[None, :], (P, P)),
        np.broadcast_to(np.arange(ST)[None, :], (P, ST)), np.eye(P)], 1).astype(bf16)
    select = np.zeros((P, HK), bf16)
    select[pair % SK, pair] = 1
    select[96 + pair // SK, pair] = 1
    select[96 + H + pair // SK, pair] = 1

    arrays = {
        "x": v["x"].reshape(TOK, D), "early": early, "plain": plain, "rows": rows, "tables": tables, "select": select,
        "mask_t": v["mask_SxS2_ik0"].T, "pad_t": v["mask_BxS2_if1"].T,
        "w_gate": v["L0_ffn_w_gate"], "w_up": v["L0_ffn_w_up"], "w_down": v["L0_ffn_w_down"],
    }
    arrays = {f"in_{k}": np.ascontiguousarray(a) for k, a in arrays.items()}
    nc = bacc.Bacc("TRN2", target_bir_lowering=False, num_devices=1)
    args = [nc.dram_tensor(k, a.shape, mybir.dt.from_np(a.dtype), kind="ExternalInput").ap() for k, a in arrays.items()]
    out = nc.dram_tensor("out", (TOK, D), F32, kind="ExternalOutput").ap()
    xattn_moe_xattn_lora_kernel(nc, *args, out)
    result = run_bass_kernel_spmd(nc, [arrays], core_ids=[0])
    return result.results[0]["out"].reshape(B, S, D)
```
